# Optimizing a Trainium2 kernel written in Bass

```python
import numpy as np
import jax
import jax.numpy as jnp

def _softmax(x, axis=-1):
    return jax.nn.softmax(x, axis=axis)

def _gelu(x):
    return jax.nn.gelu(x, approximate=True)

def _silu(x):
    return jax.nn.silu(x)

def _sigmoid(x):
    return jax.nn.sigmoid(x)

def _layernorm(x, axis=-1, eps=1e-05):
    m = jnp.mean(x, axis=axis, keepdims=True)
    v = jnp.var(x, axis=axis, keepdims=True)
    return (x - m) / jnp.sqrt(v + eps)

def _scatter_add(tgt, idx, src, axis=0):
    return tgt.at[idx].add(src)

def _segment_sum(src, seg, n):
    return jax.ops.segment_sum(src, seg, n)
kernel_name = 'mk_sandwich_d1_jaxref_r8_bacea6'

def setup_inputs(seed: int=0):
    np.random.seed(seed)
    _w = jnp.asarray

    def _L0_attn_setup():
        import jax, jax.numpy as jnp
        import numpy as np
        B, S, D_MODEL = (2, 256, 128)
        NUM_HEADS, ATTN_DIM = (16, 64)
        key = jax.random.key(seed)
        ks = jax.random.split(key, 9)
        scale = 1.0 / np.sqrt(D_MODEL)
        states = jax.random.normal(ks[0], (B, S, D_MODEL), dtype=jnp.float32)
        Wq = jax.random.normal(ks[1], (D_MODEL, NUM_HEADS * ATTN_DIM), dtype=jnp.float32) * scale
        bq = jnp.zeros((NUM_HEADS * ATTN_DIM,), dtype=jnp.float32)
        Wk = jax.random.normal(ks[2], (D_MODEL, NUM_HEADS * ATTN_DIM), dtype=jnp.float32) * scale
        bk = jnp.zeros((NUM_HEADS * ATTN_DIM,), dtype=jnp.float32)
        Wv = jax.random.normal(ks[3], (D_MODEL, NUM_HEADS * ATTN_DIM), dtype=jnp.float32) * scale
        bv = jnp.zeros((NUM_HEADS * ATTN_DIM,), dtype=jnp.float32)
        Wo = jax.random.normal(ks[4], (NUM_HEADS * ATTN_DIM, D_MODEL), dtype=jnp.float32) * scale
        bo = jnp.zeros((D_MODEL,), dtype=jnp.float32)
        return {'states': states, 'Wq': Wq, 'bq': bq, 'Wk': Wk, 'bk': bk, 'Wv': Wv, 'bv': bv, 'Wo': Wo, 'bo': bo}
    _L0_attn_in = _L0_attn_setup()

    def _L0_ffn_setup():
        import jax, jax.numpy as jnp
        import numpy as np
        import math
        D = 128
        H = 16
        E = 8
        TOPK = 2
        LAT = D // 2
        KPH = LAT // H
        HD = D // H

        def _forward(hs, q_w, q_b, k_w, k_b, v_w, v_b, o_w, o_b, router_w, router_b, w1, b1, w2, b2):
            B, S, _ = hs.shape
            Q = (hs @ q_w + q_b).reshape(B, S, H, HD).transpose(0, 2, 1, 3)
            K = (hs @ k_w + k_b).reshape(B, S, H, KPH).transpose(0, 2, 1, 3)
            V = (hs @ v_w + v_b).reshape(B, S, H, KPH).transpose(0, 2, 1, 3)
            scores = jnp.einsum('bhsk,bhtk->bhst', Q[..., :KPH], K) / math.sqrt(KPH)
            attn = jax.nn.softmax(scores, axis=-1)
            ao = jnp.einsum('bhst,bhtv->bhsv', attn, V)
            ao = ao.transpose(0, 2, 1, 3).reshape(B, S, H * KPH)
            ao = jnp.concatenate([ao, jnp.zeros((B, S, D - LAT), ao.dtype)], axis=-1)
            mla_out = ao @ o_w + o_b
            probs = jax.nn.softmax(mla_out @ router_w + router_b, axis=-1)
            topw, topi = jax.lax.top_k(probs, TOPK)
            topw = topw / (topw.sum(-1, keepdims=True) + 1e-08)
            combine = jnp.sum(jax.nn.one_hot(topi, E, dtype=probs.dtype) * topw[..., None], axis=-2)
            h1 = jnp.einsum('bsd,edf->ebsf', mla_out, w1) + b1[:, None, None, :]
            h1 = jax.nn.gelu(h1, approximate=False)
            h2 = jnp.einsum('ebsf,efd->ebsd', h1, w2) + b2[:, None, None, :]
            moe_out = jnp.einsum('bse,ebsd->bsd', combine, h2)
            return hs + 0.3 * moe_out
        key = jax.random.key(seed)
        ks = jax.random.split(key, 16)
        s = 0.02
        inp = {'hidden_states': jax.random.normal(ks[0], (2, 256, D), jnp.float32), 'q_w': jax.random.normal(ks[1], (D, D), jnp.float32) * s, 'q_b': jnp.zeros((D,), jnp.float32), 'k_w': jax.random.normal(ks[2], (D, LAT), jnp.float32) * s, 'k_b': jnp.zeros((LAT,), jnp.float32), 'v_w': jax.random.normal(ks[3], (D, LAT), jnp.float32) * s, 'v_b': jnp.zeros((LAT,), jnp.float32), 'o_w': jax.random.normal(ks[4], (D, D), jnp.float32) * s, 'o_b': jnp.zeros((D,), jnp.float32), 'router_w': jax.random.normal(ks[5], (D, E), jnp.float32) * s, 'router_b': jnp.zeros((E,), jnp.float32), 'w1': jax.random.normal(ks[6], (E, D, 2 * D), jnp.float32) * s, 'b1': jnp.zeros((E, 2 * D), jnp.float32), 'w2': jax.random.normal(ks[7], (E, 2 * D, D), jnp.float32) * s, 'b2': jnp.zeros((E, D), jnp.float32)}
        return inp
    _L0_ffn_in = _L0_ffn_setup()
    _d = {'L0_attn_states': _L0_attn_in['states'], 'L0_attn_Wq': _L0_attn_in['Wq'], 'L0_attn_bq': _L0_attn_in['bq'], 'L0_attn_Wk': _L0_attn_in['Wk'], 'L0_attn_bk': _L0_attn_in['bk'], 'L0_attn_Wv': _L0_attn_in['Wv'], 'L0_attn_bv': _L0_attn_in['bv'], 'L0_attn_Wo': _L0_attn_in['Wo'], 'L0_attn_bo': _L0_attn_in['bo'], 'L0_ffn_q_w': _L0_ffn_in['q_w'], 'L0_ffn_q_b': _L0_ffn_in['q_b'], 'L0_ffn_k_w': _L0_ffn_in['k_w'], 'L0_ffn_k_b': _L0_ffn_in['k_b'], 'L0_ffn_v_w': _L0_ffn_in['v_w'], 'L0_ffn_v_b': _L0_ffn_in['v_b'], 'L0_ffn_o_w': _L0_ffn_in['o_w'], 'L0_ffn_o_b': _L0_ffn_in['o_b'], 'L0_ffn_router_w': _L0_ffn_in['router_w'], 'L0_ffn_router_b': _L0_ffn_in['router_b'], 'L0_ffn_w1': _L0_ffn_in['w1'], 'L0_ffn_b1': _L0_ffn_in['b1'], 'L0_ffn_w2': _L0_ffn_in['w2'], 'L0_ffn_b2': _L0_ffn_in['b2']}
    _x0 = _d['L0_attn_states']
    _d['L0_attn_states'] = jax.random.normal(jax.random.fold_in(jax.random.key(seed), 1), (4, 1024, 128), dtype=_x0.dtype)
    del _x0
    return _d

def reference(L0_attn_states, L0_attn_Wq, L0_attn_bq, L0_attn_Wk, L0_attn_bk, L0_attn_Wv, L0_attn_bv, L0_attn_Wo, L0_attn_bo, L0_ffn_q_w, L0_ffn_q_b, L0_ffn_k_w, L0_ffn_k_b, L0_ffn_v_w, L0_ffn_v_b, L0_ffn_o_w, L0_ffn_o_b, L0_ffn_router_w, L0_ffn_router_b, L0_ffn_w1, L0_ffn_b1, L0_ffn_w2, L0_ffn_b2):

    def _L0_attn_ref(states, Wq, bq, Wk, bk, Wv, bv, Wo, bo):
        import jax, jax.numpy as jnp
        import numpy as np
        B, S, D_MODEL = (2, 256, 128)
        NUM_HEADS, ATTN_DIM = (16, 64)
        b, s, _ = states.shape
        h, d = (NUM_HEADS, ATTN_DIM)

        def proj(W, bias):
            y = jnp.tanh(states @ W + bias)
            return y.reshape(b, s, h, d).transpose(0, 2, 1, 3)
        q, k, v = (proj(Wq, bq), proj(Wk, bk), proj(Wv, bv))
        alpha = jnp.einsum('bhqd,bhkd->bhqk', q, k) / jnp.sqrt(jnp.float32(d))
        causal = jnp.tril(jnp.ones((s, s), dtype=bool))
        alpha = jnp.where(causal, alpha, jnp.finfo(jnp.float32).min)
        alpha = jax.nn.softmax(alpha, axis=-1)
        ctx = jnp.einsum('bhqk,bhkd->bhqd', alpha, v)
        ctx = ctx.transpose(0, 2, 1, 3).reshape(b, s, h * d)
        return jnp.tanh(ctx @ Wo + bo)

    def _L0_ffn_ref(hidden_states, q_w, q_b, k_w, k_b, v_w, v_b, o_w, o_b, router_w, router_b, w1, b1, w2, b2):
        import jax, jax.numpy as jnp
        import numpy as np
        import math
        D = 128
        H = 16
        E = 8
        TOPK = 2
        LAT = D // 2
        KPH = LAT // H
        HD = D // H

        def _forward(hs, q_w, q_b, k_w, k_b, v_w, v_b, o_w, o_b, router_w, router_b, w1, b1, w2, b2):
            B, S, _ = hs.shape
            Q = (hs @ q_w + q_b).reshape(B, S, H, HD).transpose(0, 2, 1, 3)
            K = (hs @ k_w + k_b).reshape(B, S, H, KPH).transpose(0, 2, 1, 3)
            V = (hs @ v_w + v_b).reshape(B, S, H, KPH).transpose(0, 2, 1, 3)
            scores = jnp.einsum('bhsk,bhtk->bhst', Q[..., :KPH], K) / math.sqrt(KPH)
            attn = jax.nn.softmax(scores, axis=-1)
            ao = jnp.einsum('bhst,bhtv->bhsv', attn, V)
            ao = ao.transpose(0, 2, 1, 3).reshape(B, S, H * KPH)
            ao = jnp.concatenate([ao, jnp.zeros((B, S, D - LAT), ao.dtype)], axis=-1)
            mla_out = ao @ o_w + o_b
            probs = jax.nn.softmax(mla_out @ router_w + router_b, axis=-1)
            topw, topi = jax.lax.top_k(probs, TOPK)
            topw = topw / (topw.sum(-1, keepdims=True) + 1e-08)
            combine = jnp.sum(jax.nn.one_hot(topi, E, dtype=probs.dtype) * topw[..., None], axis=-2)
            h1 = jnp.einsum('bsd,edf->ebsf', mla_out, w1) + b1[:, None, None, :]
            h1 = jax.nn.gelu(h1, approximate=False)
            h2 = jnp.einsum('ebsf,efd->ebsd', h1, w2) + b2[:, None, None, :]
            moe_out = jnp.einsum('bse,ebsd->bsd', combine, h2)
            return hs + 0.3 * moe_out
        return _forward(hidden_states, q_w, q_b, k_w, k_b, v_w, v_b, o_w, o_b, router_w, router_b, w1, b1, w2, b2)
    x = L0_attn_states
    x = x + _layernorm(_L0_attn_ref(_layernorm(x, axis=-1), L0_attn_Wq, L0_attn_bq, L0_attn_Wk, L0_attn_bk, L0_attn_Wv, L0_attn_bv, L0_attn_Wo, L0_attn_bo), axis=-1)
    x = x + _layernorm(_L0_ffn_ref(_layernorm(x, axis=-1), L0_ffn_q_w, L0_ffn_q_b, L0_ffn_k_w, L0_ffn_k_b, L0_ffn_v_w, L0_ffn_v_b, L0_ffn_o_w, L0_ffn_o_b, L0_ffn_router_w, L0_ffn_router_b, L0_ffn_w1, L0_ffn_b1, L0_ffn_w2, L0_ffn_b2), axis=-1)
    return x

_drawn_inputs = setup_inputs


def setup_inputs(seed=0):
    import zlib

    import numpy as np

    out = dict(_drawn_inputs(seed))
    spreads = {'L0_attn_bq': (0.0, 0.364),
     'L0_attn_bk': (0.0, 0.8),
     'L0_attn_bv': (0.0, 0.1),
     'L0_attn_bo': (0.0, 0.1),
     'L0_ffn_q_b': (0.0, 0.8),
     'L0_ffn_k_b': (0.0, 0.8),
     'L0_ffn_v_b': (0.0, 0.8),
     'L0_ffn_o_b': (0.0, 0.8),
     'L0_ffn_router_b': (0.0, 0.8),
     'L0_ffn_b1': (0.0, 0.8),
     'L0_ffn_b2': (0.0, 0.8)}
    factors = {'L0_ffn_q_w': 8.0,
     'L0_ffn_k_w': 8.0,
     'L0_ffn_v_w': 8.0,
     'L0_ffn_o_w': 8.0,
     'L0_ffn_router_w': 8.0,
     'L0_ffn_w1': 8.0,
     'L0_ffn_w2': 8.0}
    for name, (base, spread) in spreads.items():
        noise = np.random.default_rng([zlib.crc32(name.encode()), seed]).standard_normal(out[name].shape)
        drawn = base * np.exp(spread * noise) if base else spread * noise
        out[name] = jnp.asarray(drawn.astype(out[name].dtype))
    for name, factor in factors.items():
        out[name] = (out[name] * factor).astype(out[name].dtype)
    return out
```

```python
from contextlib import ExitStack

import concourse.bass as bass
from concourse import mybir

F32 = mybir.dt.float32
F16 = mybir.dt.float16
BF16 = mybir.dt.bfloat16
U32 = mybir.dt.uint32
ALU = mybir.AluOpType
ACT = mybir.ActivationFunctionType
AX = mybir.AxisListType

P = 128
B, S, D = 4, 1024, 128
T = S // P
NT = B * T
HALF = 512
H1, DH = 16, 64
PAIRS = H1 // 2
N1 = B * PAIRS
WSCALE = 64.0
H2, KD = 16, 4
LAT = H2 * KD
GH = 4
GROUPS = H2 // GH
N2 = B * GROUPS
PARTS = 3
PROD = PARTS * PARTS * KD
MAXROW = 64
E, F = 8, 256
FC = F // P
EPS = 1e-5
LOWEST = -3.4e38

CAUSAL = [
    [(0, 0, 512, 0), (1, 128, 384, 512), (3, 384, 128, 896)],
    [(0, 512, 512, 0), (1, 512, 512, 512)],
    [(2, 512, 512, 0), (3, 512, 512, 512)],
    [(4, 512, 512, 0), (5, 640, 384, 512), (7, 896, 128, 896)],
    [(2, 256, 256, 0), (6, 768, 256, 256)],
]
WIDTH = [1024, 1024, 1024, 1024, 512]
QSLOT, KSLOT, VSLOT, NSLOT = 0, 2, 4, 7


class Steps:

    def __init__(self, eng, sem, per=0, turn=0):
        self.eng, self.sem, self.n, self.turn = eng, sem, 0, turn
        self.base = turn * per

    def done(self, ins):
        self.n += 1
        ins.then_inc(self.sem, 1)
        return self.n

    def now(self, n=None):
        self.eng.wait_ge(self.sem, self.count(n))

    def count(self, n=None):
        return self.base + (self.n if n is None else n)


def upto(eng, sem, count):
    if not isinstance(count, int) or count > 0:
        eng.wait_ge(sem, count)


def build(nc, states, Wq, bq, Wk, bk, Wv, bv, Wo, bo, q_w, q_b, k_w, k_b, v_w, v_b, o_w, o_b,
          router_w, router_b, w1, b1, w2, b2, out):
    x_dram = states.rearrange("b (t p) d -> p (b t) d", p=P)
    out_dram = out.rearrange("b (t p) d -> p (b t) d", p=P)
    q_dram = nc.dram_tensor("latent_q", (B, PARTS, LAT, S), BF16, kind="Internal").ap()
    k_dram = nc.dram_tensor("latent_k", (B, PARTS, PARTS, LAT, S), BF16, kind="Internal").ap()
    kpm_dram = nc.dram_tensor("latent_kpm", (B, PARTS, PARTS, LAT, S), BF16, kind="Internal").ap()

    with ExitStack() as ctx:
        def sb(name, shape, dt=F32):
            return ctx.enter_context(nc.sbuf_tensor(name, shape, dt))

        def sem(name):
            return ctx.enter_context(nc.semaphore(name))

        apart = sem("apart")

        def wait_apart(eng, semaphore, count):
            if not isinstance(count, int) or count > 0:
                eng.wait_ge(semaphore, count)
                eng.sem_inc(apart, 1)

        psum = ctx.enter_context(nc.psum_tensor("psum", [P, 8 * HALF], F32))

        def bank(n, count=1):
            return psum[:, n * HALF:(n + count) * HALF]

        X = sb("X", [P, NT, D])
        acc = sb("acc", [P, NT, D])
        hs = sb("hs", [P, NT, D])
        ident = sb("ident", [P, P])
        identb = sb("identb", [P, P], BF16)
        stats = sb("stats", [P, NT, 6])
        mv = sb("mv", [P, NT, 2])
        rstd = sb("rstd", [P, NT])
        mhalf = sb("mhalf", [P, NT])
        bo_b = sb("bo_b", [P, D])
        vb_b = sb("vb_b", [P, LAT])
        ob_b = sb("ob_b", [P, D])
        rb_b = sb("rb_b", [P, E])
        w_lat = sb("w_lat", [P, 2 * LAT])
        w_lat_in = sb("w_lat_in", [P, 2 * LAT])
        b_lat = sb("b_lat", [P, 1])
        w_lv = sb("w_lv", [P, LAT])
        w_router = sb("w_router", [P, E])
        b2_sb = sb("b2_sb", [P, D])
        b1_in = sb("b1_in", [P, P])
        b1T = sb("b1T", [P, E * FC])
        iota_e = sb("iota_e", [P, E])
        arena = sb("arena", [P, 37300])

        class Arena:
            def __init__(self, at=0):
                self.at = at

            def take(self, words, dt=F32):
                v = arena[:, self.at:self.at + words]
                self.at += words
                assert self.at <= 37300, self.at
                return v if dt == F32 else v.bitcast(dt)

        a1 = Arena()
        xT_all = a1.take(B * S, F16).rearrange("p (b h s) -> p b h s", b=B, h=2)
        W_all = a1.take(PAIRS * NSLOT * P // 2, F16).rearrange("p (n j c) -> p n j c", n=PAIRS, j=NSLOT)
        qk_bias = a1.take(2 * PAIRS).rearrange("p (t n) -> p t n", t=2)
        pick_bias = a1.take(P // 2, F16)
        ones = a1.take(DH)
        a0 = Arena(a1.at)
        w_in = a0.take(3 * H1 * DH).rearrange("p (t n) -> p t n", t=3)
        w_hi = a0.take(H1 * DH // 2, F16)
        bias_in = a0.take(2 * P).rearrange("p (t n) -> p t n", t=2)
        vbias = a0.take(H1 * DH)
        vb_hi = a0.take(H1 * DH // 2, F16)

        x_in = [sem(f"x_in{b}") for b in range(B)]
        small_in, w_got, b_got = sem("small_in"), sem("w_got"), sem("b_got")
        consts0, consts = sem("consts0"), sem("consts")
        SMALL = 4 + 6 + 2 * KD
        d0, p0, a0s = sem("d0"), sem("p0"), sem("a0s")
        rstd0, xn0, xt_ps, xt_hi, xt_lo = sem("rstd0"), sem("xn0"), sem("xt_ps"), sem("xt_hi"), sem("xt_lo")
        biasT_ps, whi_done, wlo_done, mv0 = sem("biasT_ps"), sem("whi_done"), sem("wlo_done"), sem("mv0")

        def norm_stats(dve, steps, src, b):
            for t in range(T):
                steps.done(nc.vector.bn_stats(stats[:, b * T + t, :], src(t)))
            steps.now()
            for t in range(b * T, (b + 1) * T):
                last = nc.vector.bn_aggr(mv[:, t, :], stats[:, t, :])
            return last

        with nc.Block() as block:
            @block.sync
            def _(sp):
                for b in range(B):
                    sp.dma_start(X[:, b * T:(b + 1) * T, :], x_dram[:, b * T:(b + 1) * T, :]).then_inc(x_in[b], 16)
                HD = D // H2
                for dst, src in ((w_lat_in[:, 0:LAT], q_w.rearrange("d (h r) -> d h r", r=HD)[:, :, 0:KD]),
                                 (w_lat_in[:, LAT:], k_w), (w_lv[:, :], v_w), (w_router[:, :], router_w), (b2_sb[0:E, :], b2),
                                 (b1_in[0:E * FC, :], b1.rearrange("e (c f) -> (e c) f", c=FC))):
                    sp.dma_start(dst, src).then_inc(small_in, 16)
                for d in range(KD):
                    for at, src, step in ((0, q_b, HD), (LAT, k_b, KD)):
                        sp.dma_start(b_lat[at + d * H2:at + (d + 1) * H2, :],
                                     src.rearrange("(h r) -> h r", r=step)[:, d:d + 1], allow_slow_non_contiguous=True).then_inc(small_in, 16)

            @block.scalar
            def _(act):
                for t, w in enumerate((Wq, Wk, Wv)):
                    act.dma_start(w_in[:, t, :], w).then_inc(w_got, 16)
                act.wait_ge(consts, 4)
                for t, w in enumerate((bq, bk)):
                    act.dma_start(bias_in[0:PAIRS, t, :], w.rearrange("(n c) -> n c", n=PAIRS)).then_inc(b_got, 16)
                for row in (0, 32):
                    act.dma_start(vbias[row:row + 1, :], bv.rearrange("(a n) -> a n", a=1)).then_inc(b_got, 16)
                for dst, src in ((bo_b, bo), (vb_b, v_b), (ob_b, o_b), (rb_b, router_b)):
                    act.dma_start(dst[:, :], src.partition_broadcast(P)).then_inc(small_in, 16)
                act.wait_ge(w_got, 48)
                for t, slot in enumerate((QSLOT, KSLOT, VSLOT)):
                    nc.scalar.activation(W_all[:, :, slot, :], w_in[:, t, :].rearrange("p (n c) -> p n c", n=PAIRS),
                                         ACT.Copy, scale=WSCALE).then_inc(whi_done, 1)
                act.wait_ge(b_got, 64)
                nc.scalar.activation(vb_hi[0:64, :], vbias[0:64, :], ACT.Copy, scale=WSCALE).then_inc(whi_done, 1)
                for b in range(B):
                    act.wait_ge(xt_ps, b + 1)
                    nc.scalar.copy(xT_all[:, b, 0, :], bank(2 * b, 2)).then_inc(xt_hi, 1)
                act.wait_ge(biasT_ps, 1)
                act.wait_ge(xt_lo, 1)
                nc.scalar.copy(qk_bias, bank(0)[:, 0:2 * PAIRS].rearrange("p (t n) -> p t n", t=2)).then_inc(a0s, 1)
                nc.scalar.copy(b1T[:, :], bank(0)[:, 2 * PAIRS:2 * PAIRS + E * FC]).then_inc(a0s, 1)
                act.wait_ge(small_in, 16 * SMALL)
                for t in range(2):
                    half = slice(t * LAT, (t + 1) * LAT)
                    nc.scalar.copy(w_lat[:, half].rearrange("p (d h) -> p d h", d=KD),
                                   w_lat_in[:, half].rearrange("p (h d) -> p d h", d=KD)).then_inc(a0s, 1)
                nc.scalar.copy(acc[:, :, :], bo_b[:, :].unsqueeze(1).to_broadcast([P, NT, D])).then_inc(a0s, 1)
                act.wait_ge(a0s, 5)

            @block.gpsimd
            def _(pool):
                nc.gpsimd.memset(ident[:, :], 0.0).then_inc(consts0, 1)
                pool.wait_ge(consts0, 1)
                nc.gpsimd.affine_select(out=ident[:, :], in_=ident[:, :], compare_op=ALU.not_equal, fill=1.0,
                                        base=0, pattern=[[-1, P]], channel_multiplier=1).then_inc(consts, 1)
                nc.gpsimd.memset(vbias, 0.0).then_inc(consts, 1)
                nc.gpsimd.memset(bias_in, 0.0).then_inc(consts, 1)
                nc.gpsimd.memset(mhalf[:, :], -0.5).then_inc(consts, 1)
                nc.gpsimd.memset(ones, 1.0).then_inc(consts, 1)
                pool.wait_ge(consts, 1)
                nc.gpsimd.tensor_copy(identb[:, :], ident[:, :]).then_inc(consts, 1)
                pool.wait_ge(consts, 6)
                for b in range(B):
                    now = slice(b * T, (b + 1) * T)
                    pool.wait_ge(mv0, b + 1)
                    nc.gpsimd.tensor_scalar(rstd[:, now], mv[:, now, 1], EPS, None, ALU.add).then_inc(p0, 1)
                    pool.wait_ge(p0, b + 1)
                    nc.gpsimd.tensor_tensor(rstd[:, now], rstd[:, now], mhalf[:, now], ALU.pow).then_inc(rstd0, 1)

            @block.vector
            def _(dve):
                steps = Steps(dve, d0)
                steps.done(nc.vector.memset(pick_bias, 0.0))
                steps.now()
                for row in (0, 32):
                    steps.done(nc.vector.memset(pick_bias[row:row + 1, :], 1.0))
                for e in range(E):
                    nc.vector.memset(iota_e[:, e:e + 1], float(e))
                for b in range(B):
                    dve.wait_ge(x_in[b], 16)
                    norm_stats(dve, steps, lambda t: X[:, b * T + t, :], b).then_inc(mv0, 1)
                dve.wait_ge(w_got, 48)
                dve.wait_ge(whi_done, 4)
                for t, slot in enumerate((QSLOT, KSLOT, VSLOT)):
                    nc.vector.scalar_tensor_tensor(
                        W_all[:, :, slot + 1, :], w_in[:, t, :].rearrange("p (n c) -> p n c", n=PAIRS), WSCALE,
                        W_all[:, :, slot, :], ALU.mult, ALU.subtract)
                steps.done(nc.vector.memset(W_all[:, :, VSLOT + 2, :], 0.0))
                steps.now()
                rows = vb_hi.rearrange("p (n c) -> p n c", n=PAIRS)
                nc.vector.tensor_copy(W_all[0:32, :, VSLOT + 2, :], rows[0:32]).then_inc(wlo_done, 1)
                nc.vector.scalar_tensor_tensor(
                    W_all[32:64, :, VSLOT + 2, :], vbias[32:64, :].rearrange("p (n c) -> p n c", n=PAIRS), WSCALE,
                    rows[32:64], ALU.mult, ALU.subtract).then_inc(wlo_done, 1)
                for b in range(B):
                    dve.wait_ge(rstd0, b + 1)
                    for t in range(b * T, (b + 1) * T):
                        last = nc.vector.tensor_scalar(hs[:, t, :], X[:, t, :], mv[:, t, 0:1], rstd[:, t:t + 1],
                                                       ALU.subtract, ALU.mult)
                    last.then_inc(xn0, 1)
                for b in range(B):
                    dve.wait_ge(xt_hi, b + 1)
                    nc.vector.tensor_tensor(xT_all[:, b, 1, :], bank(2 * b, 2), xT_all[:, b, 0, :],
                                            ALU.subtract).then_inc(xt_lo, 1)

            @block.tensor
            def _(pe):
                pe.wait_ge(consts, 1)
                for b in range(B):
                    pe.wait_ge(xn0, b + 1)
                    for t in range(T):
                        last = nc.tensor.transpose(bank(2 * b, 2)[:, t * P:(t + 1) * P], hs[:, b * T + t, :], ident[:, :])
                    last.then_inc(xt_ps, 1)
                pe.wait_ge(b_got, 64)
                pe.wait_ge(xt_lo, 1)
                for t in range(2):
                    last = nc.tensor.transpose(bank(0)[:, t * PAIRS:(t + 1) * PAIRS], bias_in[0:PAIRS, t, :],
                                               ident[0:PAIRS, 0:PAIRS])
                pe.wait_ge(small_in, 16 * SMALL)
                last = nc.tensor.transpose(bank(0)[:, 2 * PAIRS:2 * PAIRS + E * FC], b1_in[0:E * FC, :],
                                           ident[0:E * FC, 0:E * FC])
                last.then_inc(biasT_ps, 1)

        a1b = Arena(a1.at)
        w_qk = a1b.take(4 * P // 2, F16).rearrange("p (j c) -> p j c", j=4)
        w_v = a1b.take(3 * P // 2, F16).rearrange("p (j c) -> p j c", j=3)
        w_o = a1b.take(D)
        xT = a1b.take(S, F16).rearrange("p (h s) -> p h s", h=2)
        probs = [[a1b.take(w) for w in WIDTH] for _ in range(2)]
        q_hi = [[a1b.take(S // 2, F16) for _ in range(2)] for _ in range(2)]
        q_lo = [[a1b.take(S // 2, F16) for _ in range(2)] for _ in range(2)]
        k_hl = [[a1b.take(S // 2, F16) for _ in range(2)] for _ in range(2)]
        qk_f32 = [a1b.take(S) for _ in range(2)]
        qk_hi = [a1b.take(S // 2, F16) for _ in range(2)]
        qk_lo = [a1b.take(S // 2, F16) for _ in range(2)]
        sum_full = [a1b.take(S) for _ in range(2)]
        sum_hi = [a1b.take(HALF) for _ in range(2)]
        sum_lo = [a1b.take(HALF) for _ in range(2)]
        denT = a1b.take(S)
        rden_col = a1b.take(S // 32)
        spare = hs[:, :, :].rearrange("p t d -> p (t d)")
        vals = [spare[:, m * S:(m + 1) * S].rearrange("p (t c) -> p t c", t=T) for m in range(2)]
        ctxT = spare[:, 2 * S:3 * S]
        rden = spare[:, 3 * S:4 * S]

        SC = [bank(0, 2), bank(2, 2)]
        PJ = bank(4, 2)
        OUT = [bank(6), bank(7)]

        wqk_in, wv_in, wo_in, xt_in = sem("wqk_in"), sem("wv_in"), sem("wo_in"), sem("xt_in")
        qk_done, tanh_done, lo_done = sem("qk_done"), sem("tanh_done"), sem("lo_done")
        head_in = [[sem(f"head_in{m}{s}") for s in range(2)] for m in range(2)]
        vproj_done, vals_ready = sem("vproj_done"), sem("vals_ready")
        scores_done, exp_done, masked, full_summed = (sem("scores_done"), sem("exp_done"), sem("masked"),
                                                      sem("full_summed"))
        pv_done, sums_done, den_done, den_read = sem("pv_done"), sem("sums_done"), sem("den_done"), sem("den_read")
        ctx_ready, wo_done, acc_added, d1 = sem("ctx_ready"), sem("wo_done"), sem("acc_added"), sem("d1")
        lo_summed = sem("lo_summed")
        HEAD_DMAS = 6
        D1 = 15

        def each_pair(engine, pair):
            pair(0, 0, first=True)
            pair(1, 1)
            with engine.Fori(1, N1 // 2 - 1) as k:
                for par in range(2):
                    pair(2 * k + par, par)
            pair(N1 - 2, 0)
            pair(N1 - 1, 1, last=True)

        with nc.Block() as block:
            @block.sync
            def _(sp):
                def load_inputs(n):
                    if not isinstance(n, int) or n > 0:
                        sp.wait_ge(qk_done, 2 * n)
                    at = bass.ds(n % PAIRS, 1)
                    sp.dma_start(xT, xT_all[:, bass.ds(n // PAIRS, 1), :, :].rearrange("p a h s -> p (a h) s")
                                 ).then_inc(xt_in, 16)
                    sp.dma_start(w_v, W_all[:, at, VSLOT:NSLOT, :].rearrange("p a j c -> p (a j) c")).then_inc(wv_in, 16)
                    sp.dma_start(w_qk, W_all[:, at, 0:VSLOT, :].rearrange("p a j c -> p (a j) c")).then_inc(wqk_in, 16)

                def heads(n, par):
                    if not isinstance(n, int) or n > 1:
                        sp.wait_ge(scores_done, 10 * (n - 1))
                    for j, dst in ((0, (q_hi[par], q_lo[par])), (1, (k_hl[par], k_hl[par]))):
                        for part, (src, ready) in enumerate(((qk_hi[j], tanh_done), (qk_lo[j], lo_done))):
                            sp.wait_ge(ready, (4 * n + 2 * j + 1) if part == 0 else (2 * n + j + 1))
                            for s in range(2):
                                rows = (0, 1) if j == 0 else (part,)
                                for r in rows:
                                    sp.dma_start(dst[part][s][r * DH:(r + 1) * DH, :], src[s * DH:(s + 1) * DH, :]
                                                 ).then_inc(head_in[par][s], 16)

                def load_o(n):
                    upto(sp, wo_done, n)
                    sp.dma_start(w_o, Wo[bass.ds((n % PAIRS) * P, P), :]).then_inc(wo_in, 16)

                def pair(i, par, first=False, last=False):
                    if not first:
                        load_o(i - 1)
                    if not last:
                        heads(i + 1, 1 - par)
                        if not isinstance(i, int) or i < N1 - 2:
                            load_inputs(i + 2)

                load_inputs(0)
                heads(0, 0)
                load_inputs(1)
                each_pair(sp, pair)
                load_o(N1 - 1)

            @block.tensor
            def _(pe):
                def project(n, j):
                    if j == 0:
                        pe.wait_ge(wqk_in, 16 * (n + 1))
                        pe.wait_ge(vals_ready, n + 1)
                    else:
                        pe.wait_ge(tanh_done, 4 * n + 2)
                    for half in range(2):
                        passes = ((0, 0), (0, 1), (1, 0))
                        for m, (w, x) in enumerate(passes):
                            last = nc.tensor.matmul(PJ[:, half * HALF:(half + 1) * HALF], w_qk[:, 2 * j + w, :],
                                                    xT[:, x, half * HALF:(half + 1) * HALF], start=(m == 0), stop=(m == 2))
                    last.then_inc(qk_done, 1)

                def values(n):
                    pe.wait_ge(wv_in, 16 * (n + 1))
                    pe.wait_ge(xt_in, 16 * (n + 1))
                    for t in range(T):
                        if t in (0, T // 2):
                            upto(pe, den_read, 2 * n - 3 + 2 * t // T)
                        tok = slice(t * P, (t + 1) * P)
                        o = PJ[:, tok]
                        nc.tensor.matmul(o, xT[:, 0, tok], w_v[:, 0, :], start=True, stop=False)
                        nc.tensor.matmul(o, xT[:, 0, tok], w_v[:, 1, :], start=False, stop=False)
                        nc.tensor.matmul(o, xT[:, 1, tok], w_v[:, 0, :], start=False, stop=False)
                        last = nc.tensor.matmul(o, pick_bias, w_v[:, 2, :], start=False, stop=True)
                    last.then_inc(vproj_done, 1)

                def scores(s, g, par):
                    for kt, q0, n, c in CAUSAL[g]:
                        k = k_hl[par][s][:, kt * P:(kt + 1) * P]
                        nc.tensor.matmul(SC[s][:, c:c + n], k, q_hi[par][s][:, q0:q0 + n], start=True, stop=False,
                                         skip_group_check=True)
                        last = nc.tensor.matmul(SC[s][:, c:c + n], k, q_lo[par][s][:, q0:q0 + n], start=False, stop=True,
                                                skip_group_check=True)
                    last.then_inc(scores_done, 1)

                def context(g, par):
                    for kt, q0, n, c in CAUSAL[g]:
                        half = q0 // HALF
                        first = g == half and kt == 0
                        for s in range(2):
                            last = nc.tensor.matmul(
                                OUT[half][s * DH:(s + 1) * DH, q0 - half * HALF:q0 - half * HALF + n],
                                vals[par][:, kt, s * DH:(s + 1) * DH], probs[s][g][:, c:c + n],
                                start=first, stop=(g == 4), skip_group_check=True)
                    last.then_inc(pv_done, 1)

                def denominators(n):
                    pe.wait_ge(sums_done, n + 1)
                    for half, sums in enumerate((sum_lo, sum_hi)):
                        for s in range(2):
                            last = nc.tensor.matmul(PJ[s * DH:(s + 1) * DH, half * HALF:(half + 1) * HALF],
                                                    ones, sums[s], start=True, stop=True, skip_group_check=True)
                        last.then_inc(den_done, 1)

                def output(n):
                    pe.wait_ge(ctx_ready, n + 1)
                    pe.wait_ge(wo_in, 16 * (n + 1))
                    for t in range(T):
                        last = nc.tensor.matmul(PJ[:, t * P:(t + 1) * P], ctxT[:, t * P:(t + 1) * P], w_o,
                                                start=True, stop=True)
                    last.then_inc(wo_done, 1)

                def begin(n, par):
                    for s in range(2):
                        pe.wait_ge(head_in[par][s], 16 * HEAD_DMAS * (n // 2 + 1))
                        upto(pe, exp_done, 10 * n - 1 + s)
                        scores(s, 0, par)

                def pair(i, par, first=False, last=False):
                    def next_scores(s, g):
                        pe.wait_ge(exp_done, 10 * i + 2 * g - 1 + s)
                        scores(s, g, par)

                    next_scores(0, 1)
                    next_scores(1, 1)
                    if not last:
                        values(i + 1)
                    next_scores(0, 2)
                    next_scores(1, 2)
                    if not last:
                        project(i + 1, 0)
                    pe.wait_ge(masked, 6 * i + 2)
                    upto(pe, ctx_ready, i)
                    context(0, par)
                    next_scores(0, 3)
                    next_scores(1, 3)
                    if not last:
                        project(i + 1, 1)
                    context(1, par)
                    context(2, par)
                    if not first:
                        if last:
                            pe.wait_ge(den_read, 2 * i)
                        else:
                            pe.wait_ge(tanh_done, 4 * (i + 1) + 4)
                        output(i - 1)
                    next_scores(0, 4)
                    next_scores(1, 4)
                    pe.wait_ge(masked, 6 * i + 4)
                    context(3, par)
                    if not last:
                        begin(i + 1, 1 - par)
                    pe.wait_ge(masked, 6 * i + 6)
                    context(4, par)
                    if first:
                        pe.wait_ge(tanh_done, 4 * (i + 1) + 4)
                    else:
                        pe.wait_ge(acc_added, i)
                    denominators(i)

                values(0)
                project(0, 0)
                project(0, 1)
                pe.wait_ge(tanh_done, 4)
                begin(0, 0)
                each_pair(pe, pair)
                pe.wait_ge(den_read, 2 * N1)
                output(N1 - 1)

            @block.scalar
            def _(act):
                def tanh(n, j, par):
                    act.wait_ge(qk_done, 2 * n + j + 1)
                    for s in range(2):
                        wait_apart(act, head_in[1 - par][s], 16 * HEAD_DMAS * ((n + 1) // 2))
                    bias = qk_bias[:, j, bass.ds(n % PAIRS, 1)]
                    nc.scalar.activation(qk_hi[j], PJ, ACT.Tanh, scale=1.0 / WSCALE, bias=bias).then_inc(tanh_done, 1)
                    wait_apart(act, lo_done, 2 * (n - 1) + j + 1)
                    nc.scalar.activation(qk_f32[j], PJ, ACT.Tanh, scale=1.0 / WSCALE, bias=bias).then_inc(tanh_done, 1)

                def value_tanh(n, par):
                    act.wait_ge(vproj_done, n + 1)
                    if not isinstance(n, int) or n > 1:
                        act.wait_ge(pv_done, 5 * (n - 1))
                    nc.scalar.activation(vals[par], PJ.rearrange("p (t c) -> p t c", t=T), ACT.Tanh,
                                         scale=1.0 / WSCALE).then_inc(vals_ready, 1)

                def exp(i, s, g):
                    if s == 0 and (not isinstance(i, int) or i > 0):
                        act.wait_ge(pv_done, 5 * (i - 1) + g + 1)
                        if g == 0:
                            act.wait_ge(lo_summed, 2 * i)
                        elif g < 3:
                            act.wait_ge(full_summed, 2 * i)
                        else:
                            act.wait_ge(sums_done, i)
                    act.wait_ge(scores_done, 10 * i + 2 * g + s + 1)
                    nc.scalar.activation(probs[s][g], SC[s][:, 0:WIDTH[g]], ACT.Exp,
                                         scale=DH ** -0.5).then_inc(exp_done, 1)

                def pair(i, par, first=False, last=False):
                    for g in range(2):
                        for s in range(2):
                            exp(i, s, g)
                    if not last:
                        value_tanh(i + 1, 1 - par)
                    exp(i, 0, 2)
                    exp(i, 1, 2)
                    if not last:
                        tanh(i + 1, 0, 1 - par)
                    exp(i, 0, 3)
                    exp(i, 1, 3)
                    if not last:
                        tanh(i + 1, 1, 1 - par)
                    for s in range(2):
                        exp(i, s, 4)

                value_tanh(0, 0)
                tanh(0, 0, 0)
                tanh(0, 1, 0)
                each_pair(act, pair)

            @block.gpsimd
            def _(pool):
                def keep_causal(v, blocks):
                    return nc.gpsimd.affine_select(out=v, in_=v, compare_op=ALU.is_ge, fill=0.0, base=0,
                                                   pattern=([[0, blocks]] if blocks > 1 else []) + [[1, P]], channel_multiplier=-1)

                def mask(i, s, g):
                    wait_apart(pool, exp_done, 10 * i + 2 * g + s + 1)
                    tiles = probs[s][g].rearrange("p (a c) -> p a c", a=2)[:, :, 0:P]
                    last = keep_causal(tiles, 2)
                    if g < 4:
                        last = keep_causal(probs[s][g][:, 7 * P:], 1)
                    last.then_inc(masked, 1)

                def pair(i, par, first=False, last=False):
                    for s in range(2):
                        mask(i, s, 0)
                    upto(pool, sums_done, i)
                    for s in range(2):
                        pool.wait_ge(exp_done, 10 * i + 5 + s)
                        nc.gpsimd.tensor_tensor(sum_full[s], probs[s][1], probs[s][2], ALU.add).then_inc(full_summed, 1)
                    for g in (3, 4):
                        for s in range(2):
                            mask(i, s, g)

                each_pair(pool, pair)

            @block.vector
            def _(dve):
                def low_part(n, j, par):
                    dve.wait_ge(tanh_done, 4 * n + 2 * j + 2)
                    for s in range(2):
                        upto(dve, head_in[1 - par][s], 16 * HEAD_DMAS * ((n + 1) // 2))
                    nc.vector.tensor_tensor(qk_lo[j], qk_f32[j], qk_hi[j], ALU.subtract).then_inc(lo_done, 1)

                def add_output(n):
                    dve.wait_ge(wo_done, n + 1)
                    upto(dve, acc_added, n)
                    if isinstance(n, int):
                        v = acc[:, (n // PAIRS) * T:(n // PAIRS + 1) * T, :]
                    else:
                        v = acc[:, bass.ds((n // PAIRS) * T, T), :]
                    nc.vector.tensor_tensor(v, PJ.rearrange("p (t c) -> p t c", t=T), v, ALU.add).then_inc(acc_added, 1)

                def normalise(n, steps):
                    for half in range(2):
                        dve.wait_ge(den_done, 2 * n + half + 1)
                        now = slice(half * HALF, (half + 1) * HALF)
                        nc.vector.transpose(denT[:, now], PJ[:, now]).then_inc(den_read, 1)
                    dve.wait_ge(den_read, 2 * n + 2)
                    steps.done(nc.vector.reciprocal(rden_col, denT.rearrange("p (b c) -> p b c", c=32)[:, :, 0]))
                    steps.now()
                    steps.done(nc.vector.transpose(rden.rearrange("p (b c) -> p b c", c=32),
                                                   rden_col.unsqueeze(2).to_broadcast([P, S // 32, 32])))
                    steps.now()
                    dve.wait_ge(pv_done, 5 * (n + 1))
                    upto(dve, wo_done, n)
                    nc.vector.tensor_tensor(ctxT[:, 0:HALF], OUT[0], rden[:, 0:HALF], ALU.mult)
                    nc.vector.tensor_tensor(ctxT[:, HALF:], OUT[1], rden[:, HALF:], ALU.mult).then_inc(ctx_ready, 1)

                def pair(i, par, first=False, last=False):
                    steps = Steps(dve, d1, D1, i)
                    if not first:
                        steps.base = steps.base - 2
                        normalise(i - 1, steps)
                    n0 = steps.n
                    for s in range(2):
                        dve.wait_ge(masked, 6 * i + 1 + s)
                        nc.vector.tensor_copy(sum_lo[s][:, 0:P], probs[s][0][:, 0:P])
                        steps.done(nc.vector.tensor_tensor(sum_lo[s][:, P:], probs[s][0][:, HALF:HALF + 3 * P],
                                                           probs[s][0][:, P:HALF], ALU.add))
                    for s in range(2):
                        steps.now(n0 + 1 + s)
                        v = sum_lo[s][:, 3 * P:]
                        nc.vector.tensor_tensor(v, v, probs[s][0][:, 7 * P:], ALU.add).then_inc(lo_summed, 1)
                    if not last:
                        low_part(i + 1, 0, 1 - par)
                    for s in range(2):
                        dve.wait_ge(full_summed, 2 * i + 1 + s)
                        steps.done(nc.vector.tensor_tensor(sum_hi[s], sum_full[s][:, 0:HALF], sum_full[s][:, HALF:],
                                                           ALU.add))
                    if not last:
                        low_part(i + 1, 1, 1 - par)
                    for m, (q, c, n) in enumerate(((0, 0, 4 * P), (P, 4 * P, 3 * P), (3 * P, 7 * P, P))):
                        for s in range(2):
                            if m == 0:
                                dve.wait_ge(masked, 6 * i + 3 + s)
                            steps.now(n0 + 3 + 2 * m + s)
                            v = sum_hi[s][:, q:q + n]
                            steps.done(nc.vector.tensor_tensor(v, v, probs[s][3][:, c:c + n], ALU.add))
                    if not first:
                        add_output(i - 1)
                    for s in range(2):
                        dve.wait_ge(masked, 6 * i + 5 + s)
                        v = sum_lo[s][:, 2 * P:]
                        dve.wait_ge(lo_summed, 2 * i + 1 + s)
                        steps.done(nc.vector.tensor_tensor(v, v, probs[s][4][:, 0:2 * P], ALU.add))
                    for s in range(2):
                        v = sum_hi[s][:, 2 * P:]
                        steps.now(n0 + 9 + s)
                        ins = nc.vector.tensor_tensor(v, v, probs[s][4][:, 2 * P:], ALU.add)
                        if s == 0:
                            steps.done(ins)
                        else:
                            ins.then_inc(sums_done, 1)
                    assert steps.n == D1 - 2 * first, steps.n

                low_part(0, 0, 0)
                low_part(0, 1, 0)
                each_pair(dve, pair)
                steps = Steps(dve, d1, D1, N1)
                steps.base -= 2
                normalise(N1 - 1, steps)
                add_output(N1 - 1)

        a2 = Arena()
        lat_vals = a2.take(NT * LAT).rearrange("p (t c) -> p t c", t=NT)
        q_rows = [a2.take(GH * S // 2, BF16).rearrange("p (j t) -> p j t", j=GH) for _ in range(2)]
        k_rows = [a2.take(GH * S // 2, BF16).rearrange("p (j t) -> p j t", j=GH) for _ in range(2)]
        kpm_rows = [a2.take(GH * S // 2, BF16).rearrange("p (j t) -> p j t", j=GH) for _ in range(2)]
        v_cols = [a2.take(T * GH * 32).rearrange("p (t j c) -> p t j c", t=T, j=GH) for _ in range(2)]
        ow_rows = [a2.take(D) for _ in range(2)]
        out_norm = a2.take(HALF)
        head_rows = a2.take(GH)
        a2k = a2.at
        hsT = [a2.take(S) for _ in range(2)]
        qk = [a2.take(S) for _ in range(2)]
        qk_rest = a2.take(S)
        qk_part = [[a2.take(S // 2, BF16) for _ in range(PARTS)] for _ in range(2)]
        kpm = a2.take(S)
        kpm_rest = a2.take(S)
        kpm_part = [[a2.take(S // 2, BF16) for _ in range(PARTS)] for _ in range(2)]

        pow2, stats2, rstd2, tanh2, normed2, x_added = (sem("pow2"), sem("stats2"), sem("rstd2"), sem("tanh2"),
                                                        sem("normed2"), sem("x_added"))
        d2 = sem("d2")
        hs_ready, hsT_ps, hsT_ready, qk_ps, lv_ps = (sem("hs_ready"), sem("hsT_ps"), sem("hsT_ready"), sem("qk_ps"),
                                                     sem("lv_ps"))
        qk_ready, rest_ready, lv_ready = sem("qk_ready"), sem("rest_ready"), sem("lv_ready")
        part_ready = [sem(f"part_ready{c}") for c in range(PARTS)]
        kpm_ready, kpm_rest_ready = sem("kpm_ready"), sem("kpm_rest_ready")
        kpm_part_ready = [sem(f"kpm_part_ready{c}") for c in range(PARTS)]
        parts_out = [sem(f"parts_out{m}") for m in range(2)]
        BATCH_DMAS = 3 * PARTS
        init3, init3k, init3v, init3h = sem("init3"), sem("init3k"), sem("init3v"), sem("init3h")
        acc_set = sem("acc_set")

        def wide(row, count=T):
            return row.unsqueeze(1).to_broadcast([P, count, row.shape[-1]])

        def batch(v, b):
            return v[:, b * T:(b + 1) * T, :]

        with nc.Block() as block:
            @block.vector
            def _(dve):
                steps = Steps(dve, d2)

                def moments(src, b, turn):
                    at = 2 * b + turn
                    slot = (at % B) * T
                    for t in range(T):
                        steps.done(nc.vector.bn_stats(stats[:, slot + t, :], src[:, t, :]))
                    steps.now()
                    if at >= B:
                        dve.wait_ge(rstd2, at - B + 1)
                    for t in range(T):
                        last = nc.vector.bn_aggr(mv[:, slot + t, :], stats[:, slot + t, :])
                    last.then_inc(stats2, 1)

                def normed(dst, src, b, turn):
                    slot = ((2 * b + turn) % B) * T
                    dve.wait_ge(rstd2, 2 * b + turn + 1)
                    for t in range(T):
                        last = nc.vector.tensor_scalar(dst[:, t, :], src[:, t, :], mv[:, slot + t, 0:1],
                                                       rstd[:, slot + t:slot + t + 1], ALU.subtract, ALU.mult)
                    return last

                def latent(b):
                    dve.wait_ge(lv_ps, b + 1)
                    nc.vector.tensor_tensor(batch(lat_vals, b), bank(6 + b % 2).rearrange("p (t c) -> p t c", t=T),
                                            wide(vb_b[:, :]), ALU.add).then_inc(lv_ready, 1)
                    dve.wait_ge(part_ready[0], b + 1)
                    if b > 0:
                        dve.wait_ge(part_ready[2], b)
                    nc.vector.tensor_tensor(qk_rest, qk[b % 2], qk_part[b % 2][0], ALU.subtract).then_inc(rest_ready, 1)

                def last_part(b):
                    dve.wait_ge(part_ready[1], b + 1)
                    if b >= 2:
                        dve.wait_ge(parts_out[b % 2], 16 * BATCH_DMAS * (b // 2))
                    nc.vector.tensor_tensor(qk_part[b % 2][2], qk_rest, qk_part[b % 2][1], ALU.subtract
                                            ).then_inc(part_ready[2], 1)

                for b in range(B + 2):
                    if b < B:
                        dve.wait_ge(tanh2, b + 1)
                        moments(batch(acc, b), b, 0)
                    if b == 0:
                        nc.vector.tensor_tensor(head_rows, ident[:, MAXROW:MAXROW + GH], ident[:, MAXROW + GH:MAXROW + 2 * GH],
                                                ALU.add).then_inc(init3h, 1)
                        dve.wait_ge(init3h, 1)
                        nc.vector.tensor_tensor(head_rows, head_rows, ident[:, MAXROW + 2 * GH:MAXROW + 3 * GH],
                                                ALU.add).then_inc(init3h, 1)
                    if 1 <= b <= B:
                        normed(batch(hs, b - 1), batch(X, b - 1), b - 1, 1).then_inc(hs_ready, 1)
                    if b < B:
                        normed(batch(acc, b), batch(acc, b), b, 0).then_inc(normed2, 1)
                    if b >= 2:
                        last_part(b - 2)
                    if b < B:
                        dve.wait_ge(x_added, b + 1)
                        moments(batch(X, b), b, 1)
                    if 1 <= b <= B:
                        latent(b - 1)

            @block.gpsimd
            def _(pool):
                def inverse_deviation(b, turn):
                    at = 2 * b + turn
                    now = slice((at % B) * T, (at % B + 1) * T)
                    pool.wait_ge(stats2, at + 1)
                    if at >= B:
                        pool.wait_ge(normed2 if turn == 0 else hs_ready, (at - B) // 2 + 1)
                    nc.gpsimd.tensor_scalar(rstd[:, now], mv[:, now, 1], EPS, None, ALU.add).then_inc(pow2, 1)
                    pool.wait_ge(pow2, at + 1)
                    nc.gpsimd.tensor_tensor(rstd[:, now], rstd[:, now], mhalf[:, now], ALU.pow).then_inc(rstd2, 1)

                def keys(b):
                    pool.wait_ge(qk_ready, b + 1)
                    if b > 0:
                        pool.wait_ge(kpm_rest_ready, b)
                    k = qk[b % 2]
                    nc.gpsimd.tensor_tensor(kpm[:, 0:HALF], k[:, 0:HALF], k[:, HALF:], ALU.add)
                    nc.gpsimd.tensor_tensor(kpm[:, HALF:], k[:, 0:HALF], k[:, HALF:], ALU.subtract).then_inc(kpm_ready, 1)
                    pool.wait_ge(kpm_part_ready[0], b + 1)
                    if b > 0:
                        pool.wait_ge(kpm_part_ready[2], b)
                    nc.gpsimd.tensor_tensor(kpm_rest, kpm, kpm_part[b % 2][0], ALU.subtract).then_inc(kpm_rest_ready, 1)

                def last_part(b):
                    pool.wait_ge(kpm_part_ready[1], b + 1)
                    if b >= 2:
                        pool.wait_ge(parts_out[b % 2], 16 * BATCH_DMAS * (b // 2))
                    nc.gpsimd.tensor_tensor(kpm_part[b % 2][2], kpm_rest, kpm_part[b % 2][1], ALU.subtract
                                            ).then_inc(kpm_part_ready[2], 1)

                for b in range(B + 2):
                    if b < B:
                        inverse_deviation(b, 0)
                    if b >= 2:
                        last_part(b - 2)
                    if b < B:
                        pool.wait_ge(normed2, b + 1)
                        nc.gpsimd.tensor_tensor(batch(X, b), batch(X, b), batch(acc, b), ALU.add).then_inc(x_added, 1)
                        inverse_deviation(b, 1)
                        pool.wait_ge(x_added, b + 1)
                        nc.gpsimd.tensor_copy(batch(acc, b), wide(ob_b[:, :])).then_inc(acc_set, 1)
                    if b == 0:
                        pool.wait_ge(init3v, 2)
                        for v in v_cols:
                            nc.gpsimd.memset(v[:, :, :, KD:KD + 1], 1.0).then_inc(init3v, 1)
                    if 1 <= b <= B:
                        keys(b - 1)
                pool.wait_ge(init3v, 4)
                pool.wait_ge(acc_set, B)

            @block.scalar
            def _(act):
                for b in range(B):
                    nc.scalar.activation(batch(acc, b), batch(acc, b), ACT.Tanh).then_inc(tanh2, 1)
                for v in (*v_cols, *q_rows, *k_rows, *kpm_rows):
                    flat = v.rearrange("p t j c -> p (t j c)") if len(v.shape) == 4 else v.rearrange("p j t -> p (j t)").bitcast(F32)
                    nc.scalar.activation(flat, ident[:, 0:1].to_broadcast([P, flat.shape[1]]), ACT.Copy, scale=0.0
                                         ).then_inc(init3v if len(v.shape) == 4 else init3, 1)
                for v in (*ow_rows, out_norm):
                    nc.scalar.activation(v, ident[:, 0:1].to_broadcast([P, v.shape[1]]), ACT.Copy, scale=0.0
                                         ).then_inc(init3, 1)
                act.wait_ge(init3, 9)
                act.wait_ge(init3h, 2)
                for v in k_rows:
                    nc.scalar.copy(v[MAXROW:MAXROW + PARTS * GH, :, :],
                                   head_rows[MAXROW:MAXROW + PARTS * GH, :].unsqueeze(2).to_broadcast([PARTS * GH, GH, S])
                                   ).then_inc(init3k, 1)

                def queries_keys(b):
                    m = b % 2
                    act.wait_ge(hsT_ps, b + 1)
                    if b >= 2:
                        act.wait_ge(lv_ps, b - 1)
                    nc.scalar.copy(hsT[m], bank(2 * m, 2)).then_inc(hsT_ready, 1)
                    act.wait_ge(qk_ps, b + 1)
                    if b >= 2:
                        act.wait_ge(rest_ready, b - 1)
                        act.wait_ge(kpm_ready, b - 1)
                        act.wait_ge(parts_out[m], 16 * BATCH_DMAS * (b // 2))
                    nc.scalar.activation(qk[m], bank(4, 2), ACT.Identity, bias=b_lat[:, 0:1]).then_inc(qk_ready, 1)
                    nc.scalar.activation(qk_part[m][0], bank(4, 2), ACT.Identity, bias=b_lat[:, 0:1]
                                         ).then_inc(part_ready[0], 1)

                def parts(b):
                    m = b % 2
                    act.wait_ge(kpm_ready, b + 1)
                    nc.scalar.copy(kpm_part[m][0], kpm).then_inc(kpm_part_ready[0], 1)
                    act.wait_ge(rest_ready, b + 1)
                    nc.scalar.copy(qk_part[m][1], qk_rest).then_inc(part_ready[1], 1)
                    act.wait_ge(kpm_rest_ready, b + 1)
                    nc.scalar.copy(kpm_part[m][1], kpm_rest).then_inc(kpm_part_ready[1], 1)

                for b in range(B):
                    queries_keys(b)
                    parts(b)

            @block.tensor
            def _(pe):
                for b in range(B):
                    m = b % 2
                    pe.wait_ge(hs_ready, b + 1)
                    for t in range(T):
                        last = nc.tensor.transpose(bank(2 * m, 2)[:, t * P:(t + 1) * P], hs[:, b * T + t, :], ident[:, :])
                    last.then_inc(hsT_ps, 1)
                    pe.wait_ge(hsT_ready, b + 1)
                    if b > 0:
                        pe.wait_ge(part_ready[0], b)
                    for half in range(2):
                        last = nc.tensor.matmul(bank(4 + half), w_lat[:, :], hsT[m][:, half * HALF:(half + 1) * HALF],
                                                start=True, stop=True)
                    last.then_inc(qk_ps, 1)
                    if b >= 2:
                        pe.wait_ge(lv_ready, b - 1)
                    for t in range(T):
                        last = nc.tensor.matmul(bank(6 + m)[:, t * LAT:(t + 1) * LAT], hsT[m][:, t * P:(t + 1) * P], w_lv[:, :],
                                                start=True, stop=True, skip_group_check=True)
                    last.then_inc(lv_ps, 1)

            @block.sync
            def _(sp):
                def thrice(v):
                    return v.unsqueeze(1).to_broadcast([LAT, PARTS, S])

                for b in range(B):
                    m = b % 2
                    for c in range(PARTS):
                        sp.wait_ge(part_ready[c], b + 1)
                        sp.dma_start(q_dram[b, c, :, :], qk_part[m][c][0:LAT, :]).then_inc(parts_out[m], 16)
                        sp.dma_start(k_dram[b, c, :, :, :].rearrange("c r t -> r c t"), thrice(qk_part[m][c][LAT:, :])
                                     ).then_inc(parts_out[m], 16)
                        sp.wait_ge(kpm_part_ready[c], b + 1)
                        sp.dma_start(kpm_dram[b, c, :, :, :].rearrange("c r t -> r c t"), thrice(kpm_part[m][c][LAT:, :])
                                     ).then_inc(parts_out[m], 16)
                for m in range(2):
                    sp.wait_ge(parts_out[m], 16 * BATCH_DMAS * B // 2)

        a3 = Arena(a2k)
        e_probs = [a3.take(GH * HALF).rearrange("p (j t) -> p j t", j=GH) for _ in range(2)]
        tops = a3.take(T * GH)
        top_rest = a3.take(T * GH)
        top_parts = a3.take(T * PARTS * GH // 2, BF16).rearrange("p (t c j) -> p t c j", t=T, c=PARTS)
        gap = a3.take(HALF)
        outT = a3.take(HALF)
        out_rden = a3.take(HALF // 32)
        aoT = a3.take(HALF)

        MX = [bank(0, 2), bank(2, 2)]
        TS = [bank(4), bank(5), bank(6)]
        OT = bank(7)
        PROJECT1, TURN1, PROJECT0, TURN0 = 3, 6, 11, 14
        EXTRAS = (PROJECT1, TURN1, PROJECT0, TURN0)

        def slots(u):
            x = sum(e < u for e in EXTRAS)
            return MX[x % 2], MX[(x + 1) % 2], MX[(x + 1 + (u in EXTRAS)) % 2]

        TOPT, PO = slots(TURN1)[1][:, 0:HALF], slots(PROJECT1)[1][:, 0:HALF]

        d3s, gap_ready, tops_ready = sem("d3s"), sem("gap_ready"), sem("tops_ready")
        qk_in = [sem(f"qk_in{m}") for m in range(2)]
        ow_in = [sem(f"ow_in{m}") for m in range(2)]
        q_clear, v_ready, t_done, e_done, lpv_done = (sem("q_clear"), sem("v_ready"), sem("t_done"), sem("e_done"),
                                                      sem("lpv_done"))
        mx_done, top_done, parts_ready, topT_done, topT_read = (sem("mx_done"), sem("top_done"), sem("parts_ready"),
                                                                sem("topT_done"), sem("topT_read"))
        out_read, ao_ready, proj3_done, proj3_added, d3 = (sem("out_read"), sem("ao_ready"), sem("proj3_done"),
                                                           sem("proj3_added"), sem("d3"))
        STEPS3 = 2 * T
        QK_DMAS = PARTS + 2
        UNITS = T * GH
        D3 = 10
        AHEAD = 24

        def unit(n, u):
            m = AHEAD + 2 * u
            return n + m // UNITS, m % UNITS

        def batch_tiles(v, n, first, count):
            if isinstance(n, int):
                at = (n // GROUPS) * T + first
                return v[:, at:at + count, :]
            return v[:, bass.ds((n // GROUPS) * T + first, count), :]

        with nc.Block() as block:
            @block.sync
            def _(sp):
                def load_qk(n, par):
                    b, heads = bass.ds(n // GROUPS, 1), bass.ds((n % GROUPS) * GH, GH)
                    q = q_dram[b, :, :, :].rearrange("o c (d h) t -> (o c d) h t", h=H2)[:, heads, :]
                    for a in range(PARTS):
                        sp.dma_start(q_rows[par][a * PARTS * KD:(a + 1) * PARTS * KD, :, :], q).then_inc(qk_in[par], 16)
                    for dst, src in ((kpm_rows, kpm_dram), (k_rows, k_dram)):
                        k = src[b, :, :, :, :].rearrange("o a c (d h) t -> (o a c d) h t", h=H2)[:, heads, :]
                        sp.dma_start(dst[par][0:PROD, :, :], k).then_inc(qk_in[par], 16)

                def load_ow(n, par):
                    at = (n % GROUPS) * GH * KD
                    for j in range(GH):
                        row = at + j * KD
                        src = o_w[row:row + KD, :] if isinstance(n, int) else o_w[bass.ds(row, KD), :]
                        sp.dma_start(ow_rows[par][32 * j:32 * j + KD, :], src).then_inc(ow_in[par], 16)

                def group(n, par, first=False, last=False):
                    if not last:
                        if not first:
                            sp.wait_ge(t_done, 64 * n)
                        load_qk(n + 1, 1 - par)
                        if not first:
                            sp.wait_ge(proj3_done, 2 * n)
                        load_ow(n + 1, 1 - par)

                load_qk(0, 0)
                load_ow(0, 0)
                group(0, 0, first=True)
                group(1, 1)
                with sp.Fori(1, N2 // 2 - 1) as k:
                    for par in range(2):
                        group(2 * k + par, par)
                group(N2 - 2, 0)
                group(N2 - 1, 1, last=True)

            @block.gpsimd
            def _(pool):
                def take_values(n, par):
                    at = (n % GROUPS) * GH * KD
                    v = batch_tiles(lat_vals, n, 0, T)
                    v = v[:, :, at:at + GH * KD] if isinstance(n, int) else v[:, :, bass.ds(at, GH * KD)]
                    nc.gpsimd.tensor_copy(v_cols[par][:, :, :, 0:KD], v.rearrange("p t (j d) -> p t j d", d=KD)
                                          ).then_inc(v_ready, 1)

                def turn(n, par):
                    pool.wait_ge(v_ready, n)
                    wait_apart(pool, t_done, 64 * (n - 1))
                    nc.gpsimd.memset(q_rows[par][MAXROW:MAXROW + PARTS * GH, :, :].rearrange("p j t -> p (j t)").bitcast(F32),
                                     0.0).then_inc(q_clear, 1)
                    pool.wait_ge(q_clear, n - 1)
                    pool.wait_ge(lpv_done, STEPS3 * (n - 1))
                    take_values(n, par)

                for n in range(2):
                    take_values(n, n)
                with pool.Fori(1, N2 // 2) as k:
                    for par in range(2):
                        turn(2 * k + par, par)

            @block.tensor
            def _(pe):
                def scores(n, par, u, j):
                    half, kt, at = u // T, u % T, GH * u + j
                    upto(pe, e_done, 64 * n + (at - 2 if at >= 3 else (0, -2, -1)[at]))
                    nc.tensor.matmul(TS[at % 3], k_rows[par][:, j, kt * P:(kt + 1) * P],
                                     q_rows[par][:, j, half * HALF:(half + 1) * HALF],
                                     start=True, stop=True).then_inc(t_done, 1)

                def values(n, par, u):
                    half, kt = u // T, u % T
                    pe.wait_ge(e_done, 64 * n + 4 * u + 4)
                    if kt == 0:
                        upto(pe, out_read, 2 * n + half)
                        if half == 0:
                            pe.wait_ge(v_ready, n + 1)
                    for j in range(GH):
                        last = nc.tensor.matmul(OT[32 * j:32 * (j + 1), :], v_cols[par][:, kt, j, :], e_probs[u % 2][:, j, :],
                                                start=(kt == 0), stop=(kt == T - 1), skip_group_check=True)
                    last.then_inc(lpv_done, 1)

                def maxima(par, m, slot):
                    qt, j = m // GH, m % GH
                    k = kpm_rows[par] if m % 2 else k_rows[par]
                    for h in range(2):
                        last = nc.tensor.matmul(slot[:, h * HALF:(h + 1) * HALF], q_rows[par][:, j, qt * P:(qt + 1) * P],
                                                k[:, j, h * HALF:(h + 1) * HALF], start=True, stop=True)
                    last.then_inc(mx_done, 1)

                def turn_tops(n, h):
                    pe.wait_ge(parts_ready, 2 * n + h + 1)
                    for t in range(4):
                        last = nc.tensor.transpose(TOPT.bitcast(BF16)[MAXROW:MAXROW + PARTS * GH, t * P:(t + 1) * P],
                                                   top_parts[:, 4 * h + t, :, :].rearrange("p c j -> p (c j)"), identb[:, :])
                    last.then_inc(topT_done, 1)

                def project(n, par, h):
                    pe.wait_ge(ao_ready, 2 * n + h + 1)
                    if h == 0:
                        pe.wait_ge(ow_in[par], 64 * (n // 2 + 1))
                    for t in range(4):
                        last = nc.tensor.matmul(PO[:, t * P:(t + 1) * P], aoT[:, t * P:(t + 1) * P], ow_rows[par],
                                                start=True, stop=True, skip_group_check=True)
                    last.then_inc(proj3_done, 1)

                def group(n, par, first=False, last=False):
                    for u in range(STEPS3):
                        if u % T == 0:
                            pe.wait_ge(tops_ready, 2 * n + u // T + 1)
                        g, m = unit(0, u)
                        units = not (last and g)
                        before = UNITS * n + AHEAD + 2 * u
                        if g and m == 0 and not last:
                            pe.wait_ge(qk_in[1 - par], 16 * QK_DMAS * ((n + 1) // 2 + 1))
                            if not first:
                                pe.wait_ge(q_clear, n)
                        for j in range(3):
                            scores(n, par, u, j)
                        def products():
                            if u > 0:
                                values(n, par, u - 1)
                            elif not first:
                                values(n - 1, 1 - par, STEPS3 - 1)

                        if u - 1 in EXTRAS:
                            products()
                        if u == PROJECT1 + 1 and not first:
                            pe.wait_ge(proj3_added, 2 * n)
                        elif u == TURN1 + 1:
                            pe.wait_ge(topT_read, 2 * n + 2)
                        elif u == PROJECT0 + 1:
                            pe.wait_ge(proj3_added, 2 * n + 1)
                        elif u == TURN0 + 1 and not last:
                            pe.wait_ge(topT_read, 2 * n + 3)
                        elif units:
                            pe.wait_ge(top_done, before - 1)
                        if units:
                            maxima((par + g) % 2, m, slots(u)[0])
                        if u - 1 not in EXTRAS:
                            products()
                        if units and u in EXTRAS:
                            pe.wait_ge(top_done, before)
                        if u == PROJECT1 and not first:
                            project(n - 1, 1 - par, 1)
                        if u == TURN1:
                            turn_tops(n, 1)
                        if u == PROJECT0:
                            project(n, par, 0)
                        if u == TURN0 and not last:
                            turn_tops(n + 1, 0)
                        scores(n, par, u, 3)
                        if units:
                            pe.wait_ge(top_done, before + (u in EXTRAS))
                            maxima((par + g) % 2, m + 1, slots(u)[2])

                pe.wait_ge(qk_in[0], 16 * QK_DMAS)
                for m in range(AHEAD):
                    if m >= 2:
                        pe.wait_ge(top_done, m - 1)
                    maxima(0, m, MX[m % 2])
                pe.wait_ge(top_done, AHEAD - 1)
                turn_tops(0, 0)
                group(0, 0, first=True)
                group(1, 1)
                with pe.Fori(1, N2 // 2 - 1) as k:
                    for par in range(2):
                        group(2 * k + par, par)
                group(N2 - 2, 0)
                group(N2 - 1, 1, last=True)
                values(N2 - 1, 1, STEPS3 - 1)
                project(N2 - 1, 1, 1)

            @block.scalar
            def _(act):
                def difference_sizes(n, m, slot):
                    act.wait_ge(mx_done, UNITS * n + m + 1)
                    nc.scalar.activation(gap, slot[:, HALF:], ACT.Abs).then_inc(gap_ready, 1)

                def exp(n, u, j):
                    act.wait_ge(t_done, 64 * n + 4 * u + j + 1)
                    if j == 0:
                        if not isinstance(n, int) or n > 0 or u >= 2:
                            act.wait_ge(lpv_done, STEPS3 * n + u - 1)
                    nc.scalar.activation(e_probs[u % 2][:, j, :], TS[(GH * u + j) % 3], ACT.Exp, scale=KD ** -0.5
                                         ).then_inc(e_done, 1)

                def top_rows_out(n, par, h):
                    act.wait_ge(topT_done, 2 * n + h + 1)
                    nc.scalar.copy(q_rows[par][MAXROW:MAXROW + PARTS * GH, 0, h * HALF:(h + 1) * HALF],
                                   TOPT.bitcast(BF16)[MAXROW:MAXROW + PARTS * GH, 0:HALF]).then_inc(topT_read, 1)

                def group(n, par, last=False):
                    for u in range(STEPS3):
                        for j in range(3):
                            exp(n, u, j)
                        if u == TURN1:
                            top_rows_out(n, par, 1)
                        if u == TURN0 and not last:
                            top_rows_out(n + 1, 1 - par, 0)
                        exp(n, u, 3)
                        g, m = unit(0, u)
                        if not (last and g):
                            difference_sizes(n + g, m + 1, slots(u)[2])

                for m in range(1, AHEAD, 2):
                    difference_sizes(0, m, MX[1])
                top_rows_out(0, 0, 0)
                group(0, 0)
                group(1, 1)
                with act.Fori(1, N2 // 2 - 1) as k:
                    for par in range(2):
                        group(2 * k + par, par)
                group(N2 - 2, 0)
                group(N2 - 1, 1, last=True)

            @block.vector
            def _(dve):
                def maxima(n, m, slot):
                    if m in (0, UNITS // 2):
                        if not isinstance(n, int) or n > 0:
                            dve.wait_ge(parts_ready, 2 * n - 1 + (m > 0))
                    if m % 2 == 1:
                        wait_apart(dve, gap_ready, (UNITS * n + m + 1) // 2)
                        nc.vector.tensor_tensor_reduce(
                            out=gap, in0=slot[:, 0:HALF], in1=gap, scale=0.5, scalar=LOWEST, op0=ALU.add, op1=ALU.max,
                            accum_out=tops[:, m:m + 1]).then_inc(top_done, 1)
                    else:
                        dve.wait_ge(mx_done, UNITS * n + m + 1)
                        nc.vector.tensor_reduce(tops[:, m:m + 1], slot, AX.X, ALU.max).then_inc(top_done, 1)

                def half_tops(v, h):
                    return v[:, 16 * h:16 * h + 16].rearrange("p (t j) -> p t j", j=GH)

                def half_part(c, h):
                    return top_parts[:, 4 * h:4 * h + 4, c, :]

                def top_part0(n, h, steps):
                    dve.wait_ge(top_done, UNITS * n + 16 * (h + 1))
                    if not isinstance(n, int) or n > 0:
                        dve.wait_ge(topT_done, 2 * n - 1 + h)
                    steps.done(nc.vector.tensor_scalar(half_part(0, h), half_tops(tops, h), -1.0, None, ALU.mult))

                def top_left(h, steps):
                    steps.now()
                    steps.done(nc.vector.scalar_tensor_tensor(half_tops(top_rest, h), half_tops(tops, h), -1.0,
                                                              half_part(0, h), ALU.mult, ALU.subtract))

                def top_part1(h, steps):
                    steps.now()
                    steps.done(nc.vector.tensor_copy(half_part(1, h), half_tops(top_rest, h)))

                def top_part2(h, steps):
                    steps.now()
                    nc.vector.tensor_tensor(half_part(2, h), half_tops(top_rest, h), half_part(1, h), ALU.subtract
                                            ).then_inc(parts_ready, 1)

                def spread_tops(n, par, h):
                    dve.wait_ge(topT_read, 2 * n + h + 1)
                    rows = q_rows[par][MAXROW:MAXROW + PARTS * GH, :, h * HALF:(h + 1) * HALF]
                    nc.vector.tensor_copy(rows[:, 1:, :], rows[:, 0:1, :].to_broadcast([PARTS * GH, GH - 1, HALF])
                                          ).then_inc(tops_ready, 1)

                def read_outputs(n, h):
                    dve.wait_ge(lpv_done, STEPS3 * n + T * (h + 1))
                    nc.vector.transpose(outT, OT).then_inc(out_read, 1)

                def invert(n, h, steps):
                    dve.wait_ge(out_read, 2 * n + h + 1)
                    steps.done(nc.vector.reciprocal(out_rden, outT.rearrange("p (b r) -> p b r", r=32)[:, :, KD]))

                def normalise(n, h, steps):
                    steps.now()
                    if not isinstance(n, int) or n > 0 or h > 0:
                        dve.wait_ge(proj3_done, 2 * n + h)
                    steps.done(nc.vector.tensor_tensor(
                        out_norm.rearrange("p (b r) -> p b r", r=32)[:, :, 0:KD],
                        outT.rearrange("p (b r) -> p b r", r=32)[:, :, 0:KD],
                        out_rden.unsqueeze(2).to_broadcast([P, HALF // 32, KD]), ALU.mult))

                def turn_outputs(steps):
                    steps.now()
                    nc.vector.transpose(aoT, out_norm).then_inc(ao_ready, 1)

                def add(n, h):
                    dve.wait_ge(proj3_done, 2 * n + h + 1)
                    upto(dve, proj3_added, 2 * n + h)
                    v = batch_tiles(acc, n, 4 * h, 4)
                    nc.vector.tensor_tensor(v, PO.rearrange("p (t c) -> p t c", t=4), v, ALU.add).then_inc(proj3_added, 1)

                def group(n, par, first=False, last=False):
                    steps = Steps(dve, d3, D3, n)
                    if not first:
                        steps.base = steps.base - 2
                    for u in range(STEPS3):
                        g, m = unit(0, u)
                        units = not (last and g)
                        if u == TURN1 + 1:
                            spread_tops(n, par, 1)
                        if u == TURN0 + 1 and not last:
                            spread_tops(n + 1, 1 - par, 0)
                        if units:
                            maxima(n + g, m, slots(u)[0])
                        if u == TURN1 - 2:
                            top_part0(n, 1, steps)
                        if u == TURN1 - 1:
                            top_part1(1, steps)
                        if u == TURN0 - 2 and not last:
                            top_part0(n + 1, 0, steps)
                        if u == TURN0 - 1 and not last:
                            top_part1(0, steps)
                        if u == 0 and not first:
                            read_outputs(n - 1, 1)
                        if u == 1 and not first:
                            normalise(n - 1, 1, steps)
                        if u == PROJECT1 and not first:
                            add(n - 1, 1)
                        if u == T:
                            read_outputs(n, 0)
                        if u == T + 1:
                            normalise(n, 0, steps)
                        if u == PROJECT0:
                            add(n, 0)
                        if units:
                            maxima(n + g, m + 1, slots(u)[2])
                        if u == TURN1 - 2:
                            top_left(1, steps)
                        if u == TURN1 - 1:
                            top_part2(1, steps)
                        if u == TURN0 - 2 and not last:
                            top_left(0, steps)
                        if u == TURN0 - 1 and not last:
                            top_part2(0, steps)
                        if u == 0 and not first:
                            invert(n - 1, 1, steps)
                        if u == 1 and not first:
                            turn_outputs(steps)
                        if u == T:
                            invert(n, 0, steps)
                        if u == T + 1:
                            turn_outputs(steps)
                    assert steps.n == D3 - 2 * first - 3 * last, steps.n

                start = Steps(dve, d3s)
                for m in range(AHEAD):
                    maxima(0, m, MX[m % 2])
                    if m == UNITS // 2 - 1:
                        top_part0(0, 0, start)
                        top_left(0, start)
                        top_part1(0, start)
                        top_part2(0, start)
                spread_tops(0, 0, 0)
                group(0, 0, first=True)
                group(1, 1)
                with dve.Fori(1, N2 // 2 - 1) as k:
                    for par in range(2):
                        group(2 * k + par, par)
                group(N2 - 2, 0)
                group(N2 - 1, 1, last=True)
                read_outputs(N2 - 1, 1)
                end = Steps(dve, d3s, 3, 1)
                invert(N2 - 1, 1, end)
                normalise(N2 - 1, 1, end)
                turn_outputs(end)
                add(N2 - 1, 1)

        def tiles(v, b, count=T, first=0):
            return v[:, bass.ds(b * T + first, count), :]

        a4 = Arena()
        mT = a4.take(B * S, F16).rearrange("p (h t) -> p h t", h=2)
        w1_parts = a4.take(E * F, F16).rearrange("p (e h f) -> p e h f", e=E, h=2)
        cw = a4.take(E * NT).rearrange("p (e t) -> p e t", e=E)
        c_tok = a4.take(NT * E).rearrange("p (t e) -> p t e", t=NT)
        a4k = a4.at
        w1_in = a4.take(E * F).rearrange("p (e f) -> p e f", e=E)
        m_b = a4.take(S).rearrange("p (t d) -> p t d", t=T)
        mT_b = a4.take(S)
        logits = a4.take(NT * E).rearrange("p (t e) -> p t e", t=NT)
        sorted8 = a4.take(NT * E).rearrange("p (t e) -> p t e", t=NT)
        index8 = a4.take(NT * E, U32).rearrange("p (t e) -> p t e", t=NT)
        index_f = a4.take(NT * 2).rearrange("p (t k) -> p t k", t=NT)
        picked = a4.take(NT * E).rearrange("p (t e) -> p t e", t=NT)
        row_top, row_sum, row_rcp = (a4.take(NT) for _ in range(3))

        w1_got, hi4, lo4, m_ready, mT_ps, mT_ready, lg_ps, lg_ready = (
            sem("w1_got"), sem("hi4"), sem("lo4"), sem("m_ready"), sem("mT_ps"), sem("mT_ready"), sem("lg_ps"),
            sem("lg_ready"))
        mhi_ready, mlo_ready, w1hi, exp4, cen4, d4 = (sem("mhi_ready"), sem("mlo_ready"), sem("w1hi"), sem("exp4"),
                                                      sem("cen4"), sem("d4"))

        def over_e(col):
            return col.unsqueeze(2).to_broadcast([P, NT, E])

        with nc.Block() as block:
            @block.sync
            def _(sp):
                sp.dma_start(w1_in, w1.rearrange("e d f -> d e f")).then_inc(w1_got, 16)
                sp.wait_ge(w1_got, 16)

            @block.tensor
            def _(pe):
                with pe.Fori(0, B) as b:
                    pe.wait_ge(m_ready, b + 1)
                    for t in range(T):
                        last = nc.tensor.transpose(bank(0, 2)[:, t * P:(t + 1) * P], m_b[:, t, :], ident[:, :])
                    last.then_inc(mT_ps, 1)
                    pe.wait_ge(mT_ready, b + 1)
                    for t in range(T):
                        last = nc.tensor.matmul(bank(2)[:, t * E:(t + 1) * E], mT_b[:, t * P:(t + 1) * P], w_router[:, :],
                                                start=True, stop=True, skip_group_check=True)
                    last.then_inc(lg_ps, 1)
                    pe.wait_ge(mhi_ready, b + 1)
                    pe.wait_ge(lg_ready, b + 1)

            @block.scalar
            def _(act):
                with act.Fori(0, B) as b:
                    act.wait_ge(mT_ps, b + 1)
                    nc.scalar.copy(mT_b, bank(0, 2)).then_inc(mT_ready, 1)
                    nc.scalar.copy(mT[:, 0, bass.ds(b * S, S)], bank(0, 2)).then_inc(mhi_ready, 1)
                    act.wait_ge(mlo_ready, b + 1)
                    act.wait_ge(lg_ps, b + 1)
                act.wait_ge(w1_got, 16)
                nc.scalar.activation(w1_parts[:, :, 0, :], w1_in, ACT.Copy, scale=WSCALE).then_inc(w1hi, 1)
                act.wait_ge(cen4, 1)
                nc.scalar.activation(logits, logits, ACT.Exp).then_inc(exp4, 1)

            @block.vector
            def _(dve):
                with dve.Fori(0, B) as b:
                    nc.vector.tensor_copy(m_b, tiles(acc, b)).then_inc(m_ready, 1)
                    dve.wait_ge(mhi_ready, b + 1)
                    nc.vector.tensor_tensor(mT[:, 1, bass.ds(b * S, S)], mT_b, mT[:, 0, bass.ds(b * S, S)],
                                            ALU.subtract).then_inc(mlo_ready, 1)
                    dve.wait_ge(lg_ps, b + 1)
                    nc.vector.tensor_tensor(tiles(logits, b), bank(2)[:, 0:T * E].rearrange("p (t e) -> p t e", t=T),
                                            wide(rb_b[:, :]), ALU.add).then_inc(lg_ready, 1)
                dve.wait_ge(w1hi, 1)
                nc.vector.scalar_tensor_tensor(w1_parts[:, :, 1, :], w1_in, WSCALE, w1_parts[:, :, 0, :],
                                               ALU.mult, ALU.subtract)
                dve.wait_ge(lg_ready, B)
                steps = Steps(dve, d4)

                def step(ins):
                    steps.done(ins)
                    steps.now()

                step(nc.vector.tensor_reduce(row_top, logits, AX.X, ALU.max))
                nc.vector.tensor_tensor(logits, logits, over_e(row_top), ALU.subtract).then_inc(cen4, 1)
                dve.wait_ge(exp4, 1)
                step(nc.vector.tensor_reduce(row_sum, logits, AX.X, ALU.add))
                step(nc.vector.reciprocal(row_rcp, row_sum))
                step(nc.vector.tensor_tensor(logits, logits, over_e(row_rcp), ALU.mult))
                for t in range(NT):
                    steps.done(nc.vector.max(sorted8[:, t, :], logits[:, t, :]))
                steps.now()
                for t in range(NT):
                    steps.done(nc.vector.max_index(index8[:, t, :], sorted8[:, t, :], logits[:, t, :]))
                steps.now()
                step(nc.vector.tensor_copy(index_f, index8[:, :, 0:2]))
                step(nc.vector.scalar_tensor_tensor(row_sum, sorted8[:, :, 0], 1e-8, sorted8[:, :, 1], ALU.add, ALU.add))
                step(nc.vector.reciprocal(row_rcp, row_sum))
                for k, dst in ((0, c_tok), (1, picked)):
                    step(nc.vector.tensor_tensor(dst, wide(iota_e[:, :], NT), over_e(index_f[:, :, k]), ALU.is_equal))
                    step(nc.vector.tensor_tensor(dst, dst, over_e(sorted8[:, :, k]), ALU.mult))
                step(nc.vector.tensor_tensor(c_tok, c_tok, picked, ALU.add))
                step(nc.vector.tensor_scalar(row_rcp, row_rcp, 0.3, None, ALU.mult))
                step(nc.vector.tensor_tensor(c_tok, c_tok, over_e(row_rcp), ALU.mult))
                step(nc.vector.tensor_copy(cw.rearrange("p e t -> p t e"), c_tok))

        a4b = Arena(a4k)
        w1_e = [a4b.take(F, F16).rearrange("p (h f) -> p h f", h=2) for _ in range(2)]
        w2_e = [a4b.take(FC * D).rearrange("p (c d) -> p c d", c=FC) for _ in range(2)]
        act_e = [[a4b.take(S) for _ in range(FC)] for _ in range(2)]
        c_rows = a4b.take(S)
        HP = [bank(0, 2), bank(2, 2)]
        YP = [bank(4, 2), bank(6, 2)]

        w1_ready = [sem(f"w1_ready{m}") for m in range(2)]
        w2_ready = [sem(f"w2_ready{m}") for m in range(2)]
        h_done, gelu_done, y_done, y_added = sem("h_done"), sem("gelu_done"), sem("y_done"), sem("y_added")
        cT_ps, cT_ready, b2_done, b2_added = sem("cT_ps"), sem("cT_ready"), sem("b2_done"), sem("b2_added")
        N4 = E * B

        with nc.Block() as block:
            @block.sync
            def _(sp):
                def load(e, par):
                    sp.dma_start(w1_e[par], w1_parts[:, bass.ds(e, 1), :, :].rearrange("p a h f -> p (a h) f")
                                 ).then_inc(w1_ready[par], 16)
                    src = w2[bass.ds(e, 1), :, :].rearrange("a (c p) d -> p (a c) d", p=P)
                    sp.dma_start(w2_e[par], src).then_inc(w2_ready[par], 16)

                def next_load(e, par):
                    sp.wait_ge(y_done, B * (e - 1))
                    load(e, par)

                for e in range(2):
                    load(e, e)
                with sp.Fori(1, E // 2) as k:
                    for par in range(2):
                        next_load(2 * k + par, par)

            @block.tensor
            def _(pe):
                def hidden(e, par, b, first):
                    n = B * e + b
                    if b == 0:
                        pe.wait_ge(w1_ready[par], 16 * (e // 2 + 1))
                    for c in range(FC):
                        if not first:
                            pe.wait_ge(gelu_done, FC * (n - 1) + c + 1)
                        for half in range(2):
                            tok = slice(b * S + half * HALF, b * S + (half + 1) * HALF)
                            passes = ((0, 0), (0, 1), (1, 0))
                            for m, (w, x) in enumerate(passes):
                                last = nc.tensor.matmul(HP[c][:, half * HALF:(half + 1) * HALF],
                                                        w1_e[par][:, w, c * P:(c + 1) * P], mT[:, x, tok],
                                                        start=(m == 0), stop=(m == 2))
                        last.then_inc(h_done, 1)

                def output(n, par, slot):
                    pe.wait_ge(gelu_done, FC * (n + 1))
                    if not isinstance(n, int) or n >= 2:
                        pe.wait_ge(y_added, n - 1)
                    pe.wait_ge(w2_ready[par], 16 * (n // (2 * B) + 1))
                    for t in range(T):
                        for c in range(FC):
                            last = nc.tensor.matmul(YP[slot][:, t * P:(t + 1) * P], act_e[slot][c][:, t * P:(t + 1) * P],
                                                    w2_e[par][:, c, :], start=(c == 0), stop=(c == FC - 1))
                    last.then_inc(y_done, 1)

                def expert(e, par, first=False):
                    for b in range(B):
                        hidden(e, par, b, first and b == 0)
                        if b > 0:
                            output(B * e + b - 1, par, (b - 1) % 2)
                        elif not first:
                            output(B * e - 1, 1 - par, 1)

                for e in range(2):
                    expert(e, e, first=(e == 0))
                with pe.Fori(1, E // 2) as k:
                    for par in range(2):
                        expert(2 * k + par, par)
                output(N4 - 1, 1, 1)
                for b in range(B):
                    if b > 0:
                        pe.wait_ge(cT_ready, b)
                    for t in range(T):
                        last = nc.tensor.transpose(HP[0][0:E, t * P:(t + 1) * P], c_tok[:, b * T + t, :], ident[:, :])
                    last.then_inc(cT_ps, 1)
                    pe.wait_ge(cT_ready, b + 1)
                    if b < 2:
                        pe.wait_ge(y_added, N4 - 1 + b)
                    else:
                        pe.wait_ge(b2_added, b - 1)
                    for t in range(T):
                        last = nc.tensor.matmul(YP[b % 2][:, t * P:(t + 1) * P], c_rows[0:E, t * P:(t + 1) * P],
                                                b2_sb[0:E, :], start=True, stop=True)
                    last.then_inc(b2_done, 1)

            @block.scalar
            def _(act):
                def unit(e, b):
                    n = B * e + b
                    for c in range(FC):
                        if c == 0 and (not isinstance(n, int) or n >= 2):
                            act.wait_ge(y_done, n - 1)
                        wait_apart(act, h_done, FC * n + c + 1)
                        at = FC * e + c
                        bias = b1T[:, at:at + 1] if isinstance(e, int) else b1T[:, bass.ds(at, 1)]
                        nc.scalar.activation(act_e[b % 2][c], HP[c], ACT.Gelu, scale=1.0 / WSCALE, bias=bias
                                             ).then_inc(gelu_done, 1)

                for e in range(2):
                    for b in range(B):
                        unit(e, b)
                with act.Fori(2, E) as e:
                    for b in range(B):
                        unit(e, b)
                for b in range(B):
                    act.wait_ge(cT_ps, b + 1)
                    if b > 0:
                        act.wait_ge(b2_done, b)
                    nc.scalar.copy(c_rows[0:E, :], HP[0][0:E, :]).then_inc(cT_ready, 1)

            @block.vector
            def _(dve):
                def add(e, b):
                    n = B * e + b
                    dve.wait_ge(y_done, n + 1)
                    if not isinstance(n, int) or n >= B:
                        dve.wait_ge(y_added, n - B + 1)
                    for t in range(b * T, (b + 1) * T):
                        c = cw[:, e, t:t + 1] if isinstance(e, int) else cw[:, bass.ds(e, 1), t]
                        last = nc.vector.scalar_tensor_tensor(hs[:, t, :], YP[b % 2][:, (t % T) * P:(t % T + 1) * P], c,
                                                              hs[:, t, :], ALU.mult, ALU.add)
                    last.then_inc(y_added, 1)

                for b in range(B):
                    add(0, b)
                with dve.Fori(1, E) as e:
                    for b in range(B):
                        add(e, b)
                for b in range(B):
                    dve.wait_ge(b2_done, b + 1)
                    dve.wait_ge(y_added, N4 - B + b + 1)
                    v = hs[:, b * T:(b + 1) * T, :]
                    nc.vector.tensor_tensor(v, YP[b % 2].rearrange("p (t d) -> p t d", t=T), v, ALU.add
                                            ).then_inc(b2_added, 1)

        stats5, pow5, rstd5, out_ready, d5 = sem("stats5"), sem("pow5"), sem("rstd5"), sem("out_ready"), sem("d5")
        stored = sem("stored")
        with nc.Block() as block:
            @block.vector
            def _(dve):
                steps = Steps(dve, d5)
                for b in range(B):
                    norm_stats(dve, steps, lambda t: hs[:, b * T + t, :], b).then_inc(stats5, 1)
                for b in range(B):
                    dve.wait_ge(rstd5, b + 1)
                    for t in range(b * T, (b + 1) * T):
                        last = nc.vector.tensor_scalar(hs[:, t, :], hs[:, t, :], mv[:, t, 0:1], rstd[:, t:t + 1],
                                                       ALU.subtract, ALU.mult)
                    steps.done(last)
                    steps.now()
                    now = slice(b * T, (b + 1) * T)
                    nc.vector.tensor_tensor(X[:, now, :], X[:, now, :], hs[:, now, :], ALU.add).then_inc(out_ready, 1)

            @block.gpsimd
            def _(pool):
                for b in range(B):
                    now = slice(b * T, (b + 1) * T)
                    pool.wait_ge(stats5, b + 1)
                    nc.gpsimd.tensor_scalar(rstd[:, now], mv[:, now, 1], EPS, None, ALU.add).then_inc(pow5, 1)
                    pool.wait_ge(pow5, b + 1)
                    nc.gpsimd.tensor_tensor(rstd[:, now], rstd[:, now], mhalf[:, now], ALU.pow).then_inc(rstd5, 1)

            @block.sync
            def _(sp):
                for b in range(B):
                    now = slice(b * T, (b + 1) * T)
                    sp.wait_ge(out_ready, b + 1)
                    sp.dma_start(out_dram[:, now, :], X[:, now, :]).then_inc(stored, 16)
                sp.wait_ge(stored, 16 * B)


_INS = ["L0_attn_states", "L0_attn_Wq", "L0_attn_bq", "L0_attn_Wk", "L0_attn_bk", "L0_attn_Wv", "L0_attn_bv",
        "L0_attn_Wo", "L0_attn_bo", "L0_ffn_q_w", "L0_ffn_q_b", "L0_ffn_k_w", "L0_ffn_k_b", "L0_ffn_v_w",
        "L0_ffn_v_b", "L0_ffn_o_w", "L0_ffn_o_b", "L0_ffn_router_w", "L0_ffn_router_b", "L0_ffn_w1", "L0_ffn_b1",
        "L0_ffn_w2", "L0_ffn_b2"]


def kernel(**inputs):
    import numpy as np
    from concourse import bacc
    from concourse.bass_utils import run_bass_kernel_spmd

    nc = bacc.Bacc("TRN2", target_bir_lowering=False, num_devices=1)
    arrays, args = {}, []
    for name in _INS:
        a = np.ascontiguousarray(inputs[name])
        arrays[f"in_{name}"] = a
        args.append(nc.dram_tensor(f"in_{name}", a.shape, mybir.dt.from_np(a.dtype), kind="ExternalInput").ap())
    out = nc.dram_tensor("out_x", (B, S, D), F32, kind="ExternalOutput").ap()
    build(nc, *args, out)
    r = run_bass_kernel_spmd(nc, [arrays], core_ids=[0])
    return r.results[0]["out_x"]
```

```python
from contextlib import ExitStack

import concourse.bass as bass
from concourse import mybir

F32 = mybir.dt.float32
F16 = mybir.dt.float16
BF16 = mybir.dt.bfloat16
U32 = mybir.dt.uint32
ALU = mybir.AluOpType
ACT = mybir.ActivationFunctionType
AX = mybir.AxisListType

P = 128
B, S, D = 4, 1024, 128
T = S // P
NT = B * T
HALF = 512
H1, DH = 16, 64
PAIRS = H1 // 2
N1 = B * PAIRS
WSCALE = 64.0
H2, KD = 16, 4
LAT = H2 * KD
GH = 4
GROUPS = H2 // GH
N2 = B * GROUPS
PARTS = 3
PROD = PARTS * PARTS * KD
MAXROW = 64
E, F = 8, 256
FC = F // P
EPS = 1e-5
LOWEST = -3.4e38

CAUSAL = [
    [(0, 0, 512, 0), (1, 128, 384, 512), (3, 384, 128, 896)],
    [(0, 512, 512, 0), (1, 512, 512, 512)],
    [(2, 512, 512, 0), (3, 512, 512, 512)],
    [(4, 512, 512, 0), (5, 640, 384, 512), (7, 896, 128, 896)],
    [(2, 256, 256, 0), (6, 768, 256, 256)],
]
WIDTH = [1024, 1024, 1024, 1024, 512]
QSLOT, KSLOT, VSLOT, NSLOT = 0, 2, 4, 7


class Steps:

    def __init__(self, eng, sem, per=0, turn=0):
        self.eng, self.sem, self.n, self.turn = eng, sem, 0, turn
        self.base = turn * per

    def done(self, ins):
        self.n += 1
        ins.then_inc(self.sem, 1)
        return self.n

    def now(self, n=None):
        self.eng.wait_ge(self.sem, self.count(n))

    def count(self, n=None):
        return self.base + (self.n if n is None else n)


def upto(eng, sem, count):
    if not isinstance(count, int) or count > 0:
        eng.wait_ge(sem, count)


def build(nc, states, Wq, bq, Wk, bk, Wv, bv, Wo, bo, q_w, q_b, k_w, k_b, v_w, v_b, o_w, o_b,
          router_w, router_b, w1, b1, w2, b2, out):
    x_dram = states.rearrange("b (t p) d -> p (b t) d", p=P)
    out_dram = out.rearrange("b (t p) d -> p (b t) d", p=P)
    q_dram = nc.dram_tensor("latent_q", (B, PARTS, LAT, S), BF16, kind="Internal").ap()
    k_dram = nc.dram_tensor("latent_k", (B, PARTS, PARTS, LAT, S), BF16, kind="Internal").ap()
    kpm_dram = nc.dram_tensor("latent_kpm", (B, PARTS, PARTS, LAT, S), BF16, kind="Internal").ap()

    with ExitStack() as ctx:
        def sb(name, shape, dt=F32):
            return ctx.enter_context(nc.sbuf_tensor(name, shape, dt))

        def sem(name):
            return ctx.enter_context(nc.semaphore(name))

        apart = sem("apart")

        def wait_apart(eng, semaphore, count):
            if not isinstance(count, int) or count > 0:
                eng.wait_ge(semaphore, count)
                eng.sem_inc(apart, 1)

        psum = ctx.enter_context(nc.psum_tensor("psum", [P, 8 * HALF], F32))

        def bank(n, count=1):
            return psum[:, n * HALF:(n + count) * HALF]

        X = sb("X", [P, NT, D])
        acc = sb("acc", [P, NT, D])
        hs = sb("hs", [P, NT, D])
        ident = sb("ident", [P, P])
        identb = sb("identb", [P, P], BF16)
        stats = sb("stats", [P, NT, 6])
        mv = sb("mv", [P, NT, 2])
        rstd = sb("rstd", [P, NT])
        mhalf = sb("mhalf", [P, NT])
        bo_b = sb("bo_b", [P, D])
        vb_b = sb("vb_b", [P, LAT])
        ob_b = sb("ob_b", [P, D])
        rb_b = sb("rb_b", [P, E])
        w_lat = sb("w_lat", [P, 2 * LAT])
        w_lat_in = sb("w_lat_in", [P, 2 * LAT])
        b_lat = sb("b_lat", [P, 1])
        w_lv = sb("w_lv", [P, LAT])
        w_router = sb("w_router", [P, E])
        b1_in = sb("b1_in", [P, P])
        b1T = sb("b1T", [P, E * FC])
        iota_e = sb("iota_e", [P, E])
        ARENA, TOP = 37300, 3 * E * F
        arena = sb("arena", [P, ARENA])

        class Arena:
            def __init__(self, at=0, end=ARENA - TOP):
                self.at, self.end = at, end

            def take(self, words, dt=F32):
                v = arena[:, self.at:self.at + words]
                self.at += words
                assert self.at <= self.end, self.at
                return v if dt == F32 else v.bitcast(dt)

        a1 = Arena()
        xT_all = a1.take(B * S, F16).rearrange("p (b h s) -> p b h s", b=B, h=2)
        W_all = a1.take(PAIRS * NSLOT * P // 2, F16).rearrange("p (n j c) -> p n j c", n=PAIRS, j=NSLOT)
        qk_bias = a1.take(2 * PAIRS).rearrange("p (t n) -> p t n", t=2)
        pick_bias = a1.take(P // 2, F16)
        ones = a1.take(DH)
        a0 = Arena(a1.at)
        w_in = a0.take(3 * H1 * DH).rearrange("p (t n) -> p t n", t=3)
        w_hi = a0.take(H1 * DH // 2, F16)
        bias_in = a0.take(2 * P).rearrange("p (t n) -> p t n", t=2)
        vbias = a0.take(H1 * DH)
        vb_hi = a0.take(H1 * DH // 2, F16)

        x_in = [sem(f"x_in{b}") for b in range(B)]
        small_in, w_got, b_got = sem("small_in"), sem("w_got"), sem("b_got")
        consts0, consts = sem("consts0"), sem("consts")
        SMALL = 4 + 5 + 2 * KD
        d0, p0, a0s = sem("d0"), sem("p0"), sem("a0s")
        rstd0, xn0, xt_ps, xt_hi, xt_lo = sem("rstd0"), sem("xn0"), sem("xt_ps"), sem("xt_hi"), sem("xt_lo")
        biasT_ps, whi_done, wlo_done, mv0 = sem("biasT_ps"), sem("whi_done"), sem("wlo_done"), sem("mv0")

        def norm_stats(dve, steps, src, b):
            for t in range(T):
                steps.done(nc.vector.bn_stats(stats[:, b * T + t, :], src(t)))
            steps.now()
            for t in range(b * T, (b + 1) * T):
                last = nc.vector.bn_aggr(mv[:, t, :], stats[:, t, :])
            return last

        with nc.Block() as block:
            @block.sync
            def _(sp):
                for b in range(B):
                    sp.dma_start(X[:, b * T:(b + 1) * T, :], x_dram[:, b * T:(b + 1) * T, :]).then_inc(x_in[b], 16)
                HD = D // H2
                for dst, src in ((w_lat_in[:, 0:LAT], q_w.rearrange("d (h r) -> d h r", r=HD)[:, :, 0:KD]),
                                 (w_lat_in[:, LAT:], k_w), (w_lv[:, :], v_w), (w_router[:, :], router_w),
                                 (b1_in[0:E * FC, :], b1.rearrange("e (c f) -> (e c) f", c=FC))):
                    sp.dma_start(dst, src).then_inc(small_in, 16)
                for d in range(KD):
                    for at, src, step in ((0, q_b, HD), (LAT, k_b, KD)):
                        sp.dma_start(b_lat[at + d * H2:at + (d + 1) * H2, :],
                                     src.rearrange("(h r) -> h r", r=step)[:, d:d + 1], allow_slow_non_contiguous=True).then_inc(small_in, 16)

            @block.scalar
            def _(act):
                for t, w in enumerate((Wq, Wk, Wv)):
                    act.dma_start(w_in[:, t, :], w).then_inc(w_got, 16)
                act.wait_ge(consts, 4)
                for t, w in enumerate((bq, bk)):
                    act.dma_start(bias_in[0:PAIRS, t, :], w.rearrange("(n c) -> n c", n=PAIRS)).then_inc(b_got, 16)
                for row in (0, 32):
                    act.dma_start(vbias[row:row + 1, :], bv.rearrange("(a n) -> a n", a=1)).then_inc(b_got, 16)
                for dst, src in ((bo_b, bo), (vb_b, v_b), (ob_b, o_b), (rb_b, router_b)):
                    act.dma_start(dst[:, :], src.partition_broadcast(P)).then_inc(small_in, 16)
                act.wait_ge(w_got, 48)
                for t, slot in enumerate((QSLOT, KSLOT, VSLOT)):
                    nc.scalar.activation(W_all[:, :, slot, :], w_in[:, t, :].rearrange("p (n c) -> p n c", n=PAIRS),
                                         ACT.Copy, scale=WSCALE).then_inc(whi_done, 1)
                act.wait_ge(b_got, 64)
                nc.scalar.activation(vb_hi[0:64, :], vbias[0:64, :], ACT.Copy, scale=WSCALE).then_inc(whi_done, 1)
                for b in range(B):
                    act.wait_ge(xt_ps, b + 1)
                    nc.scalar.copy(xT_all[:, b, 0, :], bank(2 * b, 2)).then_inc(xt_hi, 1)
                act.wait_ge(biasT_ps, 1)
                act.wait_ge(xt_lo, 1)
                nc.scalar.copy(qk_bias, bank(0)[:, 0:2 * PAIRS].rearrange("p (t n) -> p t n", t=2)).then_inc(a0s, 1)
                nc.scalar.copy(b1T[:, :], bank(0)[:, 2 * PAIRS:2 * PAIRS + E * FC]).then_inc(a0s, 1)
                act.wait_ge(small_in, 16 * SMALL)
                for t in range(2):
                    half = slice(t * LAT, (t + 1) * LAT)
                    nc.scalar.copy(w_lat[:, half].rearrange("p (d h) -> p d h", d=KD),
                                   w_lat_in[:, half].rearrange("p (h d) -> p d h", d=KD)).then_inc(a0s, 1)
                nc.scalar.copy(acc[:, :, :], bo_b[:, :].unsqueeze(1).to_broadcast([P, NT, D])).then_inc(a0s, 1)
                act.wait_ge(a0s, 5)

            @block.gpsimd
            def _(pool):
                nc.gpsimd.memset(ident[:, :], 0.0).then_inc(consts0, 1)
                pool.wait_ge(consts0, 1)
                nc.gpsimd.affine_select(out=ident[:, :], in_=ident[:, :], compare_op=ALU.not_equal, fill=1.0,
                                        base=0, pattern=[[-1, P]], channel_multiplier=1).then_inc(consts, 1)
                nc.gpsimd.memset(vbias, 0.0).then_inc(consts, 1)
                nc.gpsimd.memset(bias_in, 0.0).then_inc(consts, 1)
                nc.gpsimd.memset(mhalf[:, :], -0.5).then_inc(consts, 1)
                nc.gpsimd.memset(ones, 1.0).then_inc(consts, 1)
                pool.wait_ge(consts, 1)
                nc.gpsimd.tensor_copy(identb[:, :], ident[:, :]).then_inc(consts, 1)
                pool.wait_ge(consts, 6)
                for b in range(B):
                    now = slice(b * T, (b + 1) * T)
                    pool.wait_ge(mv0, b + 1)
                    nc.gpsimd.tensor_scalar(rstd[:, now], mv[:, now, 1], EPS, None, ALU.add).then_inc(p0, 1)
                    pool.wait_ge(p0, b + 1)
                    nc.gpsimd.tensor_tensor(rstd[:, now], rstd[:, now], mhalf[:, now], ALU.pow).then_inc(rstd0, 1)

            @block.vector
            def _(dve):
                steps = Steps(dve, d0)
                steps.done(nc.vector.memset(pick_bias, 0.0))
                steps.now()
                for row in (0, 32):
                    steps.done(nc.vector.memset(pick_bias[row:row + 1, :], 1.0))
                for e in range(E):
                    nc.vector.memset(iota_e[:, e:e + 1], float(e))
                for b in range(B):
                    dve.wait_ge(x_in[b], 16)
                    norm_stats(dve, steps, lambda t: X[:, b * T + t, :], b).then_inc(mv0, 1)
                dve.wait_ge(w_got, 48)
                dve.wait_ge(whi_done, 4)
                for t, slot in enumerate((QSLOT, KSLOT, VSLOT)):
                    nc.vector.scalar_tensor_tensor(
                        W_all[:, :, slot + 1, :], w_in[:, t, :].rearrange("p (n c) -> p n c", n=PAIRS), WSCALE,
                        W_all[:, :, slot, :], ALU.mult, ALU.subtract)
                steps.done(nc.vector.memset(W_all[:, :, VSLOT + 2, :], 0.0))
                steps.now()
                rows = vb_hi.rearrange("p (n c) -> p n c", n=PAIRS)
                nc.vector.tensor_copy(W_all[0:32, :, VSLOT + 2, :], rows[0:32]).then_inc(wlo_done, 1)
                nc.vector.scalar_tensor_tensor(
                    W_all[32:64, :, VSLOT + 2, :], vbias[32:64, :].rearrange("p (n c) -> p n c", n=PAIRS), WSCALE,
                    rows[32:64], ALU.mult, ALU.subtract).then_inc(wlo_done, 1)
                for b in range(B):
                    dve.wait_ge(rstd0, b + 1)
                    for t in range(b * T, (b + 1) * T):
                        last = nc.vector.tensor_scalar(hs[:, t, :], X[:, t, :], mv[:, t, 0:1], rstd[:, t:t + 1],
                                                       ALU.subtract, ALU.mult)
                    last.then_inc(xn0, 1)
                for b in range(B):
                    dve.wait_ge(xt_hi, b + 1)
                    nc.vector.tensor_tensor(xT_all[:, b, 1, :], bank(2 * b, 2), xT_all[:, b, 0, :],
                                            ALU.subtract).then_inc(xt_lo, 1)

            @block.tensor
            def _(pe):
                pe.wait_ge(consts, 1)
                for b in range(B):
                    pe.wait_ge(xn0, b + 1)
                    for t in range(T):
                        last = nc.tensor.transpose(bank(2 * b, 2)[:, t * P:(t + 1) * P], hs[:, b * T + t, :], ident[:, :])
                    last.then_inc(xt_ps, 1)
                pe.wait_ge(b_got, 64)
                pe.wait_ge(xt_lo, 1)
                for t in range(2):
                    last = nc.tensor.transpose(bank(0)[:, t * PAIRS:(t + 1) * PAIRS], bias_in[0:PAIRS, t, :],
                                               ident[0:PAIRS, 0:PAIRS])
                pe.wait_ge(small_in, 16 * SMALL)
                last = nc.tensor.transpose(bank(0)[:, 2 * PAIRS:2 * PAIRS + E * FC], b1_in[0:E * FC, :],
                                           ident[0:E * FC, 0:E * FC])
                last.then_inc(biasT_ps, 1)

        a1b = Arena(a1.at, ARENA)
        w_qk = a1b.take(4 * P // 2, F16).rearrange("p (j c) -> p j c", j=4)
        w_v = a1b.take(3 * P // 2, F16).rearrange("p (j c) -> p j c", j=3)
        w_o = a1b.take(D)
        xT = a1b.take(S, F16).rearrange("p (h s) -> p h s", h=2)
        probs = [[a1b.take(w) for w in WIDTH] for _ in range(2)]
        q_hi = [[a1b.take(S // 2, F16) for _ in range(2)] for _ in range(2)]
        q_lo = [[a1b.take(S // 2, F16) for _ in range(2)] for _ in range(2)]
        k_hl = [[a1b.take(S // 2, F16) for _ in range(2)] for _ in range(2)]
        qk_f32 = [a1b.take(S) for _ in range(2)]
        qk_hi = [a1b.take(S // 2, F16) for _ in range(2)]
        qk_lo = [a1b.take(S // 2, F16) for _ in range(2)]
        sum_full = [a1b.take(S) for _ in range(2)]
        sum_hi = [a1b.take(HALF) for _ in range(2)]
        sum_lo = [a1b.take(HALF) for _ in range(2)]
        denT = a1b.take(S)
        rden_col = a1b.take(S // 32)
        spare = hs[:, :, :].rearrange("p t d -> p (t d)")
        vals = [spare[:, m * S:(m + 1) * S].rearrange("p (t c) -> p t c", t=T) for m in range(2)]
        ctxT = spare[:, 2 * S:3 * S]
        rden = spare[:, 3 * S:4 * S]

        SC = [bank(0, 2), bank(2, 2)]
        PJ = bank(4, 2)
        OUT = [bank(6), bank(7)]

        wqk_in, wv_in, wo_in, xt_in = sem("wqk_in"), sem("wv_in"), sem("wo_in"), sem("xt_in")
        qk_done, tanh_done, lo_done = sem("qk_done"), sem("tanh_done"), sem("lo_done")
        head_in = [[sem(f"head_in{m}{s}") for s in range(2)] for m in range(2)]
        vproj_done, vals_ready = sem("vproj_done"), sem("vals_ready")
        scores_done, exp_done, masked, full_summed = (sem("scores_done"), sem("exp_done"), sem("masked"),
                                                      sem("full_summed"))
        pv_done, sums_done, den_done, den_read = sem("pv_done"), sem("sums_done"), sem("den_done"), sem("den_read")
        ctx_ready, wo_done, acc_added, d1 = sem("ctx_ready"), sem("wo_done"), sem("acc_added"), sem("d1")
        lo_summed = sem("lo_summed")
        HEAD_DMAS = 6
        D1 = 15

        def each_pair(engine, pair):
            pair(0, 0, first=True)
            pair(1, 1)
            with engine.Fori(1, N1 // 2 - 1) as k:
                for par in range(2):
                    pair(2 * k + par, par)
            pair(N1 - 2, 0)
            pair(N1 - 1, 1, last=True)

        with nc.Block() as block:
            @block.sync
            def _(sp):
                def load_inputs(n):
                    if not isinstance(n, int) or n > 0:
                        sp.wait_ge(qk_done, 2 * n)
                    at = bass.ds(n % PAIRS, 1)
                    sp.dma_start(xT, xT_all[:, bass.ds(n // PAIRS, 1), :, :].rearrange("p a h s -> p (a h) s")
                                 ).then_inc(xt_in, 16)
                    sp.dma_start(w_v, W_all[:, at, VSLOT:NSLOT, :].rearrange("p a j c -> p (a j) c")).then_inc(wv_in, 16)
                    sp.dma_start(w_qk, W_all[:, at, 0:VSLOT, :].rearrange("p a j c -> p (a j) c")).then_inc(wqk_in, 16)

                def heads(n, par):
                    if not isinstance(n, int) or n > 1:
                        sp.wait_ge(scores_done, 10 * (n - 1))
                    for j, dst in ((0, (q_hi[par], q_lo[par])), (1, (k_hl[par], k_hl[par]))):
                        for part, (src, ready) in enumerate(((qk_hi[j], tanh_done), (qk_lo[j], lo_done))):
                            sp.wait_ge(ready, (4 * n + 2 * j + 1) if part == 0 else (2 * n + j + 1))
                            for s in range(2):
                                rows = (0, 1) if j == 0 else (part,)
                                for r in rows:
                                    sp.dma_start(dst[part][s][r * DH:(r + 1) * DH, :], src[s * DH:(s + 1) * DH, :]
                                                 ).then_inc(head_in[par][s], 16)

                def load_o(n):
                    upto(sp, wo_done, n)
                    sp.dma_start(w_o, Wo[bass.ds((n % PAIRS) * P, P), :]).then_inc(wo_in, 16)

                def pair(i, par, first=False, last=False):
                    if not first:
                        load_o(i - 1)
                    if not last:
                        heads(i + 1, 1 - par)
                        if not isinstance(i, int) or i < N1 - 2:
                            load_inputs(i + 2)

                load_inputs(0)
                heads(0, 0)
                load_inputs(1)
                each_pair(sp, pair)
                load_o(N1 - 1)

            @block.tensor
            def _(pe):
                def project(n, j):
                    if j == 0:
                        pe.wait_ge(wqk_in, 16 * (n + 1))
                        pe.wait_ge(vals_ready, n + 1)
                    else:
                        pe.wait_ge(tanh_done, 4 * n + 2)
                    for half in range(2):
                        passes = ((0, 0), (0, 1), (1, 0))
                        for m, (w, x) in enumerate(passes):
                            last = nc.tensor.matmul(PJ[:, half * HALF:(half + 1) * HALF], w_qk[:, 2 * j + w, :],
                                                    xT[:, x, half * HALF:(half + 1) * HALF], start=(m == 0), stop=(m == 2))
                    last.then_inc(qk_done, 1)

                def values(n):
                    pe.wait_ge(wv_in, 16 * (n + 1))
                    pe.wait_ge(xt_in, 16 * (n + 1))
                    for t in range(T):
                        if t in (0, T // 2):
                            upto(pe, den_read, 2 * n - 3 + 2 * t // T)
                        tok = slice(t * P, (t + 1) * P)
                        o = PJ[:, tok]
                        nc.tensor.matmul(o, xT[:, 0, tok], w_v[:, 0, :], start=True, stop=False)
                        nc.tensor.matmul(o, xT[:, 0, tok], w_v[:, 1, :], start=False, stop=False)
                        nc.tensor.matmul(o, xT[:, 1, tok], w_v[:, 0, :], start=False, stop=False)
                        last = nc.tensor.matmul(o, pick_bias, w_v[:, 2, :], start=False, stop=True)
                    last.then_inc(vproj_done, 1)

                def scores(s, g, par):
                    for kt, q0, n, c in CAUSAL[g]:
                        k = k_hl[par][s][:, kt * P:(kt + 1) * P]
                        nc.tensor.matmul(SC[s][:, c:c + n], k, q_hi[par][s][:, q0:q0 + n], start=True, stop=False,
                                         skip_group_check=True)
                        last = nc.tensor.matmul(SC[s][:, c:c + n], k, q_lo[par][s][:, q0:q0 + n], start=False, stop=True,
                                                skip_group_check=True)
                    last.then_inc(scores_done, 1)

                def context(g, par):
                    for kt, q0, n, c in CAUSAL[g]:
                        half = q0 // HALF
                        first = g == half and kt == 0
                        for s in range(2):
                            last = nc.tensor.matmul(
                                OUT[half][s * DH:(s + 1) * DH, q0 - half * HALF:q0 - half * HALF + n],
                                vals[par][:, kt, s * DH:(s + 1) * DH], probs[s][g][:, c:c + n],
                                start=first, stop=(g == 4), skip_group_check=True)
                    last.then_inc(pv_done, 1)

                def denominators(n):
                    pe.wait_ge(sums_done, n + 1)
                    for half, sums in enumerate((sum_lo, sum_hi)):
                        for s in range(2):
                            last = nc.tensor.matmul(PJ[s * DH:(s + 1) * DH, half * HALF:(half + 1) * HALF],
                                                    ones, sums[s], start=True, stop=True, skip_group_check=True)
                        last.then_inc(den_done, 1)

                def output(n):
                    pe.wait_ge(ctx_ready, n + 1)
                    pe.wait_ge(wo_in, 16 * (n + 1))
                    for t in range(T):
                        last = nc.tensor.matmul(PJ[:, t * P:(t + 1) * P], ctxT[:, t * P:(t + 1) * P], w_o,
                                                start=True, stop=True)
                    last.then_inc(wo_done, 1)

                def begin(n, par):
                    for s in range(2):
                        pe.wait_ge(head_in[par][s], 16 * HEAD_DMAS * (n // 2 + 1))
                        upto(pe, exp_done, 10 * n - 1 + s)
                        scores(s, 0, par)

                def pair(i, par, first=False, last=False):
                    def next_scores(s, g):
                        pe.wait_ge(exp_done, 10 * i + 2 * g - 1 + s)
                        scores(s, g, par)

                    next_scores(0, 1)
                    next_scores(1, 1)
                    if not last:
                        values(i + 1)
                    next_scores(0, 2)
                    next_scores(1, 2)
                    if not last:
                        project(i + 1, 0)
                    pe.wait_ge(masked, 6 * i + 2)
                    upto(pe, ctx_ready, i)
                    context(0, par)
                    next_scores(0, 3)
                    next_scores(1, 3)
                    if not last:
                        project(i + 1, 1)
                    context(1, par)
                    context(2, par)
                    if not first:
                        if last:
                            pe.wait_ge(den_read, 2 * i)
                        else:
                            pe.wait_ge(tanh_done, 4 * (i + 1) + 4)
                        output(i - 1)
                    next_scores(0, 4)
                    next_scores(1, 4)
                    pe.wait_ge(masked, 6 * i + 4)
                    context(3, par)
                    if not last:
                        begin(i + 1, 1 - par)
                    pe.wait_ge(masked, 6 * i + 6)
                    context(4, par)
                    if first:
                        pe.wait_ge(tanh_done, 4 * (i + 1) + 4)
                    else:
                        pe.wait_ge(acc_added, i)
                    denominators(i)

                values(0)
                project(0, 0)
                project(0, 1)
                pe.wait_ge(tanh_done, 4)
                begin(0, 0)
                each_pair(pe, pair)
                pe.wait_ge(den_read, 2 * N1)
                output(N1 - 1)

            @block.scalar
            def _(act):
                def tanh(n, j, par):
                    act.wait_ge(qk_done, 2 * n + j + 1)
                    for s in range(2):
                        wait_apart(act, head_in[1 - par][s], 16 * HEAD_DMAS * ((n + 1) // 2))
                    bias = qk_bias[:, j, bass.ds(n % PAIRS, 1)]
                    nc.scalar.activation(qk_hi[j], PJ, ACT.Tanh, scale=1.0 / WSCALE, bias=bias).then_inc(tanh_done, 1)
                    wait_apart(act, lo_done, 2 * (n - 1) + j + 1)
                    nc.scalar.activation(qk_f32[j], PJ, ACT.Tanh, scale=1.0 / WSCALE, bias=bias).then_inc(tanh_done, 1)

                def value_tanh(n, par):
                    act.wait_ge(vproj_done, n + 1)
                    if not isinstance(n, int) or n > 1:
                        act.wait_ge(pv_done, 5 * (n - 1))
                    nc.scalar.activation(vals[par], PJ.rearrange("p (t c) -> p t c", t=T), ACT.Tanh,
                                         scale=1.0 / WSCALE).then_inc(vals_ready, 1)

                def exp(i, s, g):
                    if s == 0 and (not isinstance(i, int) or i > 0):
                        act.wait_ge(pv_done, 5 * (i - 1) + g + 1)
                        if g == 0:
                            act.wait_ge(lo_summed, 2 * i)
                        elif g < 3:
                            act.wait_ge(full_summed, 2 * i)
                        else:
                            act.wait_ge(sums_done, i)
                    act.wait_ge(scores_done, 10 * i + 2 * g + s + 1)
                    nc.scalar.activation(probs[s][g], SC[s][:, 0:WIDTH[g]], ACT.Exp,
                                         scale=DH ** -0.5).then_inc(exp_done, 1)

                def pair(i, par, first=False, last=False):
                    for g in range(2):
                        for s in range(2):
                            exp(i, s, g)
                    if not last:
                        value_tanh(i + 1, 1 - par)
                    exp(i, 0, 2)
                    exp(i, 1, 2)
                    if not last:
                        tanh(i + 1, 0, 1 - par)
                    exp(i, 0, 3)
                    exp(i, 1, 3)
                    if not last:
                        tanh(i + 1, 1, 1 - par)
                    for s in range(2):
                        exp(i, s, 4)

                value_tanh(0, 0)
                tanh(0, 0, 0)
                tanh(0, 1, 0)
                each_pair(act, pair)

            @block.gpsimd
            def _(pool):
                def keep_causal(v, blocks):
                    return nc.gpsimd.affine_select(out=v, in_=v, compare_op=ALU.is_ge, fill=0.0, base=0,
                                                   pattern=([[0, blocks]] if blocks > 1 else []) + [[1, P]], channel_multiplier=-1)

                def mask(i, s, g):
                    wait_apart(pool, exp_done, 10 * i + 2 * g + s + 1)
                    tiles = probs[s][g].rearrange("p (a c) -> p a c", a=2)[:, :, 0:P]
                    last = keep_causal(tiles, 2)
                    if g < 4:
                        last = keep_causal(probs[s][g][:, 7 * P:], 1)
                    last.then_inc(masked, 1)

                def pair(i, par, first=False, last=False):
                    for s in range(2):
                        mask(i, s, 0)
                    upto(pool, sums_done, i)
                    for s in range(2):
                        pool.wait_ge(exp_done, 10 * i + 5 + s)
                        nc.gpsimd.tensor_tensor(sum_full[s], probs[s][1], probs[s][2], ALU.add).then_inc(full_summed, 1)
                    for g in (3, 4):
                        for s in range(2):
                            mask(i, s, g)

                each_pair(pool, pair)

            @block.vector
            def _(dve):
                def low_part(n, j, par):
                    dve.wait_ge(tanh_done, 4 * n + 2 * j + 2)
                    for s in range(2):
                        upto(dve, head_in[1 - par][s], 16 * HEAD_DMAS * ((n + 1) // 2))
                    nc.vector.tensor_tensor(qk_lo[j], qk_f32[j], qk_hi[j], ALU.subtract).then_inc(lo_done, 1)

                def add_output(n):
                    dve.wait_ge(wo_done, n + 1)
                    upto(dve, acc_added, n)
                    if isinstance(n, int):
                        v = acc[:, (n // PAIRS) * T:(n // PAIRS + 1) * T, :]
                    else:
                        v = acc[:, bass.ds((n // PAIRS) * T, T), :]
                    nc.vector.tensor_tensor(v, PJ.rearrange("p (t c) -> p t c", t=T), v, ALU.add).then_inc(acc_added, 1)

                def normalise(n, steps):
                    for half in range(2):
                        dve.wait_ge(den_done, 2 * n + half + 1)
                        now = slice(half * HALF, (half + 1) * HALF)
                        nc.vector.transpose(denT[:, now], PJ[:, now]).then_inc(den_read, 1)
                    dve.wait_ge(den_read, 2 * n + 2)
                    steps.done(nc.vector.reciprocal(rden_col, denT.rearrange("p (b c) -> p b c", c=32)[:, :, 0]))
                    steps.now()
                    steps.done(nc.vector.transpose(rden.rearrange("p (b c) -> p b c", c=32),
                                                   rden_col.unsqueeze(2).to_broadcast([P, S // 32, 32])))
                    steps.now()
                    dve.wait_ge(pv_done, 5 * (n + 1))
                    upto(dve, wo_done, n)
                    nc.vector.tensor_tensor(ctxT[:, 0:HALF], OUT[0], rden[:, 0:HALF], ALU.mult)
                    nc.vector.tensor_tensor(ctxT[:, HALF:], OUT[1], rden[:, HALF:], ALU.mult).then_inc(ctx_ready, 1)

                def pair(i, par, first=False, last=False):
                    steps = Steps(dve, d1, D1, i)
                    if not first:
                        steps.base = steps.base - 2
                        normalise(i - 1, steps)
                    n0 = steps.n
                    for s in range(2):
                        dve.wait_ge(masked, 6 * i + 1 + s)
                        nc.vector.tensor_copy(sum_lo[s][:, 0:P], probs[s][0][:, 0:P])
                        steps.done(nc.vector.tensor_tensor(sum_lo[s][:, P:], probs[s][0][:, HALF:HALF + 3 * P],
                                                           probs[s][0][:, P:HALF], ALU.add))
                    for s in range(2):
                        steps.now(n0 + 1 + s)
                        v = sum_lo[s][:, 3 * P:]
                        nc.vector.tensor_tensor(v, v, probs[s][0][:, 7 * P:], ALU.add).then_inc(lo_summed, 1)
                    if not last:
                        low_part(i + 1, 0, 1 - par)
                    for s in range(2):
                        dve.wait_ge(full_summed, 2 * i + 1 + s)
                        steps.done(nc.vector.tensor_tensor(sum_hi[s], sum_full[s][:, 0:HALF], sum_full[s][:, HALF:],
                                                           ALU.add))
                    if not last:
                        low_part(i + 1, 1, 1 - par)
                    for m, (q, c, n) in enumerate(((0, 0, 4 * P), (P, 4 * P, 3 * P), (3 * P, 7 * P, P))):
                        for s in range(2):
                            if m == 0:
                                dve.wait_ge(masked, 6 * i + 3 + s)
                            steps.now(n0 + 3 + 2 * m + s)
                            v = sum_hi[s][:, q:q + n]
                            steps.done(nc.vector.tensor_tensor(v, v, probs[s][3][:, c:c + n], ALU.add))
                    if not first:
                        add_output(i - 1)
                    for s in range(2):
                        dve.wait_ge(masked, 6 * i + 5 + s)
                        v = sum_lo[s][:, 2 * P:]
                        dve.wait_ge(lo_summed, 2 * i + 1 + s)
                        steps.done(nc.vector.tensor_tensor(v, v, probs[s][4][:, 0:2 * P], ALU.add))
                    for s in range(2):
                        v = sum_hi[s][:, 2 * P:]
                        steps.now(n0 + 9 + s)
                        ins = nc.vector.tensor_tensor(v, v, probs[s][4][:, 2 * P:], ALU.add)
                        if s == 0:
                            steps.done(ins)
                        else:
                            ins.then_inc(sums_done, 1)
                    assert steps.n == D1 - 2 * first, steps.n

                low_part(0, 0, 0)
                low_part(0, 1, 0)
                each_pair(dve, pair)
                steps = Steps(dve, d1, D1, N1)
                steps.base -= 2
                normalise(N1 - 1, steps)
                add_output(N1 - 1)

        top = Arena(ARENA - TOP, ARENA)
        experts_in = top.take(E * F).rearrange("p (e f) -> p e f", e=E)
        w1_parts, w2_parts = (top.take(E * F, F16).rearrange("p (e h f) -> p e h f", e=E, h=2) for _ in range(2))
        experts_got, w_split = sem("experts_got"), sem("w_split")
        a2 = Arena()
        lat_vals = a2.take(NT * LAT).rearrange("p (t c) -> p t c", t=NT)
        q_rows = [a2.take(GH * S // 2, BF16).rearrange("p (j t) -> p j t", j=GH) for _ in range(2)]
        k_rows = [a2.take(GH * S // 2, BF16).rearrange("p (j t) -> p j t", j=GH) for _ in range(2)]
        kpm_rows = [a2.take(GH * S // 2, BF16).rearrange("p (j t) -> p j t", j=GH) for _ in range(2)]
        v_cols = [a2.take(T * GH * 32).rearrange("p (t j c) -> p t j c", t=T, j=GH) for _ in range(2)]
        ow_rows = [a2.take(D) for _ in range(2)]
        out_norm = a2.take(HALF)
        head_rows = a2.take(GH)
        a2k = a2.at
        hsT = [a2.take(S) for _ in range(2)]
        qk = [a2.take(S) for _ in range(2)]
        qk_rest = a2.take(S)
        qk_part = [[a2.take(S // 2, BF16) for _ in range(PARTS)] for _ in range(2)]
        kpm = a2.take(S)
        kpm_rest = a2.take(S)
        kpm_part = [[a2.take(S // 2, BF16) for _ in range(PARTS)] for _ in range(2)]

        pow2, stats2, rstd2, tanh2, normed2, x_added = (sem("pow2"), sem("stats2"), sem("rstd2"), sem("tanh2"),
                                                        sem("normed2"), sem("x_added"))
        d2 = sem("d2")
        hs_ready, hsT_ps, hsT_ready, qk_ps, lv_ps = (sem("hs_ready"), sem("hsT_ps"), sem("hsT_ready"), sem("qk_ps"),
                                                     sem("lv_ps"))
        qk_ready, rest_ready, lv_ready = sem("qk_ready"), sem("rest_ready"), sem("lv_ready")
        part_ready = [sem(f"part_ready{c}") for c in range(PARTS)]
        kpm_ready, kpm_rest_ready = sem("kpm_ready"), sem("kpm_rest_ready")
        kpm_part_ready = [sem(f"kpm_part_ready{c}") for c in range(PARTS)]
        parts_out = [sem(f"parts_out{m}") for m in range(2)]
        BATCH_DMAS = 3 * PARTS
        init3, init3k, init3v, init3h = sem("init3"), sem("init3k"), sem("init3v"), sem("init3h")
        acc_set = sem("acc_set")

        def wide(row, count=T):
            return row.unsqueeze(1).to_broadcast([P, count, row.shape[-1]])

        def batch(v, b):
            return v[:, b * T:(b + 1) * T, :]

        with nc.Block() as block:
            @block.vector
            def _(dve):
                steps = Steps(dve, d2)

                def moments(src, b, turn):
                    at = 2 * b + turn
                    slot = (at % B) * T
                    for t in range(T):
                        steps.done(nc.vector.bn_stats(stats[:, slot + t, :], src[:, t, :]))
                    steps.now()
                    if at >= B:
                        dve.wait_ge(rstd2, at - B + 1)
                    for t in range(T):
                        last = nc.vector.bn_aggr(mv[:, slot + t, :], stats[:, slot + t, :])
                    last.then_inc(stats2, 1)

                def normed(dst, src, b, turn):
                    slot = ((2 * b + turn) % B) * T
                    dve.wait_ge(rstd2, 2 * b + turn + 1)
                    for t in range(T):
                        last = nc.vector.tensor_scalar(dst[:, t, :], src[:, t, :], mv[:, slot + t, 0:1],
                                                       rstd[:, slot + t:slot + t + 1], ALU.subtract, ALU.mult)
                    return last

                def latent(b):
                    dve.wait_ge(lv_ps, b + 1)
                    nc.vector.tensor_tensor(batch(lat_vals, b), bank(6 + b % 2).rearrange("p (t c) -> p t c", t=T),
                                            wide(vb_b[:, :]), ALU.add).then_inc(lv_ready, 1)
                    dve.wait_ge(part_ready[0], b + 1)
                    if b > 0:
                        dve.wait_ge(part_ready[2], b)
                    nc.vector.tensor_tensor(qk_rest, qk[b % 2], qk_part[b % 2][0], ALU.subtract).then_inc(rest_ready, 1)

                def last_part(b):
                    dve.wait_ge(part_ready[1], b + 1)
                    if b >= 2:
                        dve.wait_ge(parts_out[b % 2], 16 * BATCH_DMAS * (b // 2))
                    nc.vector.tensor_tensor(qk_part[b % 2][2], qk_rest, qk_part[b % 2][1], ALU.subtract
                                            ).then_inc(part_ready[2], 1)

                for b in range(B + 2):
                    if b < B:
                        dve.wait_ge(tanh2, b + 1)
                        moments(batch(acc, b), b, 0)
                    if b == 0:
                        nc.vector.tensor_tensor(head_rows, ident[:, MAXROW:MAXROW + GH], ident[:, MAXROW + GH:MAXROW + 2 * GH],
                                                ALU.add).then_inc(init3h, 1)
                        dve.wait_ge(init3h, 1)
                        nc.vector.tensor_tensor(head_rows, head_rows, ident[:, MAXROW + 2 * GH:MAXROW + 3 * GH],
                                                ALU.add).then_inc(init3h, 1)
                    if 1 <= b <= B:
                        normed(batch(hs, b - 1), batch(X, b - 1), b - 1, 1).then_inc(hs_ready, 1)
                    if b < B:
                        normed(batch(acc, b), batch(acc, b), b, 0).then_inc(normed2, 1)
                    if b >= 2:
                        last_part(b - 2)
                    if b < B:
                        dve.wait_ge(x_added, b + 1)
                        moments(batch(X, b), b, 1)
                    if 1 <= b <= B:
                        latent(b - 1)

            @block.gpsimd
            def _(pool):
                def inverse_deviation(b, turn):
                    at = 2 * b + turn
                    now = slice((at % B) * T, (at % B + 1) * T)
                    pool.wait_ge(stats2, at + 1)
                    if at >= B:
                        pool.wait_ge(normed2 if turn == 0 else hs_ready, (at - B) // 2 + 1)
                    nc.gpsimd.tensor_scalar(rstd[:, now], mv[:, now, 1], EPS, None, ALU.add).then_inc(pow2, 1)
                    pool.wait_ge(pow2, at + 1)
                    nc.gpsimd.tensor_tensor(rstd[:, now], rstd[:, now], mhalf[:, now], ALU.pow).then_inc(rstd2, 1)

                def keys(b):
                    pool.wait_ge(qk_ready, b + 1)
                    if b > 0:
                        pool.wait_ge(kpm_rest_ready, b)
                    k = qk[b % 2]
                    nc.gpsimd.tensor_tensor(kpm[:, 0:HALF], k[:, 0:HALF], k[:, HALF:], ALU.add)
                    nc.gpsimd.tensor_tensor(kpm[:, HALF:], k[:, 0:HALF], k[:, HALF:], ALU.subtract).then_inc(kpm_ready, 1)
                    pool.wait_ge(kpm_part_ready[0], b + 1)
                    if b > 0:
                        pool.wait_ge(kpm_part_ready[2], b)
                    nc.gpsimd.tensor_tensor(kpm_rest, kpm, kpm_part[b % 2][0], ALU.subtract).then_inc(kpm_rest_ready, 1)

                def last_part(b):
                    pool.wait_ge(kpm_part_ready[1], b + 1)
                    if b >= 2:
                        pool.wait_ge(parts_out[b % 2], 16 * BATCH_DMAS * (b // 2))
                    nc.gpsimd.tensor_tensor(kpm_part[b % 2][2], kpm_rest, kpm_part[b % 2][1], ALU.subtract
                                            ).then_inc(kpm_part_ready[2], 1)

                for b in range(B + 2):
                    if b < B:
                        inverse_deviation(b, 0)
                    if b >= 2:
                        last_part(b - 2)
                    if b < B:
                        pool.wait_ge(normed2, b + 1)
                        nc.gpsimd.tensor_tensor(batch(X, b), batch(X, b), batch(acc, b), ALU.add).then_inc(x_added, 1)
                        inverse_deviation(b, 1)
                        pool.wait_ge(x_added, b + 1)
                        nc.gpsimd.tensor_copy(batch(acc, b), wide(ob_b[:, :])).then_inc(acc_set, 1)
                    if b == 0:
                        pool.wait_ge(init3v, 2)
                        for v in v_cols:
                            nc.gpsimd.memset(v[:, :, :, KD:KD + 1], 1.0).then_inc(init3v, 1)
                    if 1 <= b <= B:
                        keys(b - 1)
                pool.wait_ge(init3v, 4)
                pool.wait_ge(acc_set, B)

            @block.scalar
            def _(act):
                for b in range(B):
                    nc.scalar.activation(batch(acc, b), batch(acc, b), ACT.Tanh).then_inc(tanh2, 1)
                for v in (*v_cols, *q_rows, *k_rows, *kpm_rows):
                    flat = v.rearrange("p t j c -> p (t j c)") if len(v.shape) == 4 else v.rearrange("p j t -> p (j t)").bitcast(F32)
                    nc.scalar.activation(flat, ident[:, 0:1].to_broadcast([P, flat.shape[1]]), ACT.Copy, scale=0.0
                                         ).then_inc(init3v if len(v.shape) == 4 else init3, 1)
                for v in (*ow_rows, out_norm):
                    nc.scalar.activation(v, ident[:, 0:1].to_broadcast([P, v.shape[1]]), ACT.Copy, scale=0.0
                                         ).then_inc(init3, 1)
                act.wait_ge(init3, 9)
                act.wait_ge(init3h, 2)
                for v in k_rows:
                    nc.scalar.copy(v[MAXROW:MAXROW + PARTS * GH, :, :],
                                   head_rows[MAXROW:MAXROW + PARTS * GH, :].unsqueeze(2).to_broadcast([PARTS * GH, GH, S])
                                   ).then_inc(init3k, 1)

                def queries_keys(b):
                    m = b % 2
                    act.wait_ge(hsT_ps, b + 1)
                    if b >= 2:
                        act.wait_ge(lv_ps, b - 1)
                    nc.scalar.copy(hsT[m], bank(2 * m, 2)).then_inc(hsT_ready, 1)
                    act.wait_ge(qk_ps, b + 1)
                    if b >= 2:
                        act.wait_ge(rest_ready, b - 1)
                        act.wait_ge(kpm_ready, b - 1)
                        act.wait_ge(parts_out[m], 16 * BATCH_DMAS * (b // 2))
                    nc.scalar.activation(qk[m], bank(4, 2), ACT.Identity, bias=b_lat[:, 0:1]).then_inc(qk_ready, 1)
                    nc.scalar.activation(qk_part[m][0], bank(4, 2), ACT.Identity, bias=b_lat[:, 0:1]
                                         ).then_inc(part_ready[0], 1)

                def parts(b):
                    m = b % 2
                    act.wait_ge(kpm_ready, b + 1)
                    nc.scalar.copy(kpm_part[m][0], kpm).then_inc(kpm_part_ready[0], 1)
                    act.wait_ge(rest_ready, b + 1)
                    nc.scalar.copy(qk_part[m][1], qk_rest).then_inc(part_ready[1], 1)
                    act.wait_ge(kpm_rest_ready, b + 1)
                    nc.scalar.copy(kpm_part[m][1], kpm_rest).then_inc(kpm_part_ready[1], 1)

                for b in range(B):
                    queries_keys(b)
                    parts(b)

            @block.tensor
            def _(pe):
                for b in range(B):
                    m = b % 2
                    pe.wait_ge(hs_ready, b + 1)
                    for t in range(T):
                        last = nc.tensor.transpose(bank(2 * m, 2)[:, t * P:(t + 1) * P], hs[:, b * T + t, :], ident[:, :])
                    last.then_inc(hsT_ps, 1)
                    pe.wait_ge(hsT_ready, b + 1)
                    if b > 0:
                        pe.wait_ge(part_ready[0], b)
                    for half in range(2):
                        last = nc.tensor.matmul(bank(4 + half), w_lat[:, :], hsT[m][:, half * HALF:(half + 1) * HALF],
                                                start=True, stop=True)
                    last.then_inc(qk_ps, 1)
                    if b >= 2:
                        pe.wait_ge(lv_ready, b - 1)
                    for t in range(T):
                        last = nc.tensor.matmul(bank(6 + m)[:, t * LAT:(t + 1) * LAT], hsT[m][:, t * P:(t + 1) * P], w_lv[:, :],
                                                start=True, stop=True, skip_group_check=True)
                    last.then_inc(lv_ps, 1)

            @block.sync
            def _(sp):
                sp.dma_start(experts_in, w1.rearrange("e d f -> d e f")).then_inc(experts_got, 16)

                def thrice(v):
                    return v.unsqueeze(1).to_broadcast([LAT, PARTS, S])

                for b in range(B):
                    m = b % 2
                    for c in range(PARTS):
                        sp.wait_ge(part_ready[c], b + 1)
                        sp.dma_start(q_dram[b, c, :, :], qk_part[m][c][0:LAT, :]).then_inc(parts_out[m], 16)
                        sp.dma_start(k_dram[b, c, :, :, :].rearrange("c r t -> r c t"), thrice(qk_part[m][c][LAT:, :])
                                     ).then_inc(parts_out[m], 16)
                        sp.wait_ge(kpm_part_ready[c], b + 1)
                        sp.dma_start(kpm_dram[b, c, :, :, :].rearrange("c r t -> r c t"), thrice(kpm_part[m][c][LAT:, :])
                                     ).then_inc(parts_out[m], 16)
                for m in range(2):
                    sp.wait_ge(parts_out[m], 16 * BATCH_DMAS * B // 2)

        a3 = Arena(a2k)
        e_probs = [a3.take(GH * HALF).rearrange("p (j t) -> p j t", j=GH) for _ in range(2)]
        tops = a3.take(T * GH)
        top_rest = a3.take(T * GH)
        top_parts = a3.take(T * PARTS * GH // 2, BF16).rearrange("p (t c j) -> p t c j", t=T, c=PARTS)
        gap = a3.take(HALF)
        outT = a3.take(HALF)
        out_rden = a3.take(HALF // 32)
        aoT = a3.take(HALF)

        MX = [bank(0, 2), bank(2, 2)]
        TS = [bank(4), bank(5), bank(6)]
        OT = bank(7)
        PROJECT1, TURN1, PROJECT0, TURN0 = 3, 6, 11, 14
        EXTRAS = (PROJECT1, TURN1, PROJECT0, TURN0)

        def slots(u):
            x = sum(e < u for e in EXTRAS)
            return MX[x % 2], MX[(x + 1) % 2], MX[(x + 1 + (u in EXTRAS)) % 2]

        TOPT, PO = slots(TURN1)[1][:, 0:HALF], slots(PROJECT1)[1][:, 0:HALF]

        d3s, gap_ready, tops_ready = sem("d3s"), sem("gap_ready"), sem("tops_ready")
        qk_in = [sem(f"qk_in{m}") for m in range(2)]
        ow_in = [sem(f"ow_in{m}") for m in range(2)]
        q_clear, v_ready, t_done, e_done, lpv_done = (sem("q_clear"), sem("v_ready"), sem("t_done"), sem("e_done"),
                                                      sem("lpv_done"))
        mx_done, top_done, parts_ready, topT_done, topT_read = (sem("mx_done"), sem("top_done"), sem("parts_ready"),
                                                                sem("topT_done"), sem("topT_read"))
        out_read, ao_ready, proj3_done, proj3_added, d3 = (sem("out_read"), sem("ao_ready"), sem("proj3_done"),
                                                           sem("proj3_added"), sem("d3"))
        STEPS3 = 2 * T
        QK_DMAS = PARTS + 2
        UNITS = T * GH
        D3 = 10
        AHEAD = 24

        def unit(n, u):
            m = AHEAD + 2 * u
            return n + m // UNITS, m % UNITS

        def batch_tiles(v, n, first, count):
            if isinstance(n, int):
                at = (n // GROUPS) * T + first
                return v[:, at:at + count, :]
            return v[:, bass.ds((n // GROUPS) * T + first, count), :]

        with nc.Block() as block:
            @block.sync
            def _(sp):
                def load_qk(n, par):
                    b, heads = bass.ds(n // GROUPS, 1), bass.ds((n % GROUPS) * GH, GH)
                    q = q_dram[b, :, :, :].rearrange("o c (d h) t -> (o c d) h t", h=H2)[:, heads, :]
                    for a in range(PARTS):
                        sp.dma_start(q_rows[par][a * PARTS * KD:(a + 1) * PARTS * KD, :, :], q).then_inc(qk_in[par], 16)
                    for dst, src in ((kpm_rows, kpm_dram), (k_rows, k_dram)):
                        k = src[b, :, :, :, :].rearrange("o a c (d h) t -> (o a c d) h t", h=H2)[:, heads, :]
                        sp.dma_start(dst[par][0:PROD, :, :], k).then_inc(qk_in[par], 16)

                def load_ow(n, par):
                    at = (n % GROUPS) * GH * KD
                    for j in range(GH):
                        row = at + j * KD
                        src = o_w[row:row + KD, :] if isinstance(n, int) else o_w[bass.ds(row, KD), :]
                        sp.dma_start(ow_rows[par][32 * j:32 * j + KD, :], src).then_inc(ow_in[par], 16)

                def group(n, par, first=False, last=False):
                    if not last:
                        if not first:
                            sp.wait_ge(t_done, 64 * n)
                        load_qk(n + 1, 1 - par)
                        if not first:
                            sp.wait_ge(proj3_done, 2 * n)
                        load_ow(n + 1, 1 - par)

                load_qk(0, 0)
                load_ow(0, 0)
                group(0, 0, first=True)
                sp.wait_ge(w_split, 3)
                sp.dma_start(experts_in.rearrange("p e (c d) -> p (e c) d", c=FC),
                             w2.rearrange("e (c p) d -> p (e c) d", p=P)).then_inc(experts_got, 16)
                group(1, 1)
                with sp.Fori(1, N2 // 2 - 1) as k:
                    for par in range(2):
                        group(2 * k + par, par)
                group(N2 - 2, 0)
                group(N2 - 1, 1, last=True)

            @block.gpsimd
            def _(pool):
                def take_values(n, par):
                    at = (n % GROUPS) * GH * KD
                    v = batch_tiles(lat_vals, n, 0, T)
                    v = v[:, :, at:at + GH * KD] if isinstance(n, int) else v[:, :, bass.ds(at, GH * KD)]
                    nc.gpsimd.tensor_copy(v_cols[par][:, :, :, 0:KD], v.rearrange("p t (j d) -> p t j d", d=KD)
                                          ).then_inc(v_ready, 1)

                def turn(n, par):
                    pool.wait_ge(v_ready, n)
                    wait_apart(pool, t_done, 64 * (n - 1))
                    nc.gpsimd.memset(q_rows[par][MAXROW:MAXROW + PARTS * GH, :, :].rearrange("p j t -> p (j t)").bitcast(F32),
                                     0.0).then_inc(q_clear, 1)
                    pool.wait_ge(q_clear, n - 1)
                    pool.wait_ge(lpv_done, STEPS3 * (n - 1))
                    take_values(n, par)

                for n in range(2):
                    take_values(n, n)
                for k, parts in enumerate((w1_parts, w2_parts)):
                    pool.wait_ge(experts_got, 16 * (k + 1))
                    nc.gpsimd.tensor_scalar(experts_in, experts_in, WSCALE, None, ALU.mult).then_inc(w_split, 1)
                    pool.wait_ge(w_split, 3 * k + 1)
                    nc.gpsimd.tensor_copy(parts[:, :, 0, :], experts_in).then_inc(w_split, 1)
                    pool.wait_ge(w_split, 3 * k + 2)
                    nc.gpsimd.tensor_tensor(parts[:, :, 1, :], experts_in, parts[:, :, 0, :], ALU.subtract
                                            ).then_inc(w_split, 1)
                    pool.wait_ge(w_split, 3 * k + 3)
                with pool.Fori(1, N2 // 2) as k:
                    for par in range(2):
                        turn(2 * k + par, par)

            @block.tensor
            def _(pe):
                def scores(n, par, u, j):
                    half, kt, at = u // T, u % T, GH * u + j
                    upto(pe, e_done, 64 * n + (at - 2 if at >= 3 else (0, -2, -1)[at]))
                    nc.tensor.matmul(TS[at % 3], k_rows[par][:, j, kt * P:(kt + 1) * P],
                                     q_rows[par][:, j, half * HALF:(half + 1) * HALF],
                                     start=True, stop=True).then_inc(t_done, 1)

                def values(n, par, u):
                    half, kt = u // T, u % T
                    pe.wait_ge(e_done, 64 * n + 4 * u + 4)
                    if kt == 0:
                        upto(pe, out_read, 2 * n + half)
                        if half == 0:
                            pe.wait_ge(v_ready, n + 1)
                    for j in range(GH):
                        last = nc.tensor.matmul(OT[32 * j:32 * (j + 1), :], v_cols[par][:, kt, j, :], e_probs[u % 2][:, j, :],
                                                start=(kt == 0), stop=(kt == T - 1), skip_group_check=True)
                    last.then_inc(lpv_done, 1)

                def maxima(par, m, slot):
                    qt, j = m // GH, m % GH
                    k = kpm_rows[par] if m % 2 else k_rows[par]
                    for h in range(2):
                        last = nc.tensor.matmul(slot[:, h * HALF:(h + 1) * HALF], q_rows[par][:, j, qt * P:(qt + 1) * P],
                                                k[:, j, h * HALF:(h + 1) * HALF], start=True, stop=True)
                    last.then_inc(mx_done, 1)

                def turn_tops(n, h):
                    pe.wait_ge(parts_ready, 2 * n + h + 1)
                    for t in range(4):
                        last = nc.tensor.transpose(TOPT.bitcast(BF16)[MAXROW:MAXROW + PARTS * GH, t * P:(t + 1) * P],
                                                   top_parts[:, 4 * h + t, :, :].rearrange("p c j -> p (c j)"), identb[:, :])
                    last.then_inc(topT_done, 1)

                def project(n, par, h):
                    pe.wait_ge(ao_ready, 2 * n + h + 1)
                    if h == 0:
                        pe.wait_ge(ow_in[par], 64 * (n // 2 + 1))
                    for t in range(4):
                        last = nc.tensor.matmul(PO[:, t * P:(t + 1) * P], aoT[:, t * P:(t + 1) * P], ow_rows[par],
                                                start=True, stop=True, skip_group_check=True)
                    last.then_inc(proj3_done, 1)

                def group(n, par, first=False, last=False):
                    for u in range(STEPS3):
                        if u % T == 0:
                            pe.wait_ge(tops_ready, 2 * n + u // T + 1)
                        g, m = unit(0, u)
                        units = not (last and g)
                        before = UNITS * n + AHEAD + 2 * u
                        if g and m == 0 and not last:
                            pe.wait_ge(qk_in[1 - par], 16 * QK_DMAS * ((n + 1) // 2 + 1))
                            if not first:
                                pe.wait_ge(q_clear, n)
                        for j in range(3):
                            scores(n, par, u, j)
                        def products():
                            if u > 0:
                                values(n, par, u - 1)
                            elif not first:
                                values(n - 1, 1 - par, STEPS3 - 1)

                        if u - 1 in EXTRAS:
                            products()
                        if u == PROJECT1 + 1 and not first:
                            pe.wait_ge(proj3_added, 2 * n)
                        elif u == TURN1 + 1:
                            pe.wait_ge(topT_read, 2 * n + 2)
                        elif u == PROJECT0 + 1:
                            pe.wait_ge(proj3_added, 2 * n + 1)
                        elif u == TURN0 + 1 and not last:
                            pe.wait_ge(topT_read, 2 * n + 3)
                        elif units:
                            pe.wait_ge(top_done, before - 1)
                        if units:
                            maxima((par + g) % 2, m, slots(u)[0])
                        if u - 1 not in EXTRAS:
                            products()
                        if units and u in EXTRAS:
                            pe.wait_ge(top_done, before)
                        if u == PROJECT1 and not first:
                            project(n - 1, 1 - par, 1)
                        if u == TURN1:
                            turn_tops(n, 1)
                        if u == PROJECT0:
                            project(n, par, 0)
                        if u == TURN0 and not last:
                            turn_tops(n + 1, 0)
                        scores(n, par, u, 3)
                        if units:
                            pe.wait_ge(top_done, before + (u in EXTRAS))
                            maxima((par + g) % 2, m + 1, slots(u)[2])

                pe.wait_ge(qk_in[0], 16 * QK_DMAS)
                for m in range(AHEAD):
                    if m >= 2:
                        pe.wait_ge(top_done, m - 1)
                    maxima(0, m, MX[m % 2])
                pe.wait_ge(top_done, AHEAD - 1)
                turn_tops(0, 0)
                group(0, 0, first=True)
                group(1, 1)
                with pe.Fori(1, N2 // 2 - 1) as k:
                    for par in range(2):
                        group(2 * k + par, par)
                group(N2 - 2, 0)
                group(N2 - 1, 1, last=True)
                values(N2 - 1, 1, STEPS3 - 1)
                project(N2 - 1, 1, 1)

            @block.scalar
            def _(act):
                def difference_sizes(n, m, slot):
                    act.wait_ge(mx_done, UNITS * n + m + 1)
                    nc.scalar.activation(gap, slot[:, HALF:], ACT.Abs).then_inc(gap_ready, 1)

                def exp(n, u, j):
                    act.wait_ge(t_done, 64 * n + 4 * u + j + 1)
                    if j == 0:
                        if not isinstance(n, int) or n > 0 or u >= 2:
                            act.wait_ge(lpv_done, STEPS3 * n + u - 1)
                    nc.scalar.activation(e_probs[u % 2][:, j, :], TS[(GH * u + j) % 3], ACT.Exp, scale=KD ** -0.5
                                         ).then_inc(e_done, 1)

                def top_rows_out(n, par, h):
                    act.wait_ge(topT_done, 2 * n + h + 1)
                    nc.scalar.copy(q_rows[par][MAXROW:MAXROW + PARTS * GH, 0, h * HALF:(h + 1) * HALF],
                                   TOPT.bitcast(BF16)[MAXROW:MAXROW + PARTS * GH, 0:HALF]).then_inc(topT_read, 1)

                def group(n, par, last=False):
                    for u in range(STEPS3):
                        for j in range(3):
                            exp(n, u, j)
                        if u == TURN1:
                            top_rows_out(n, par, 1)
                        if u == TURN0 and not last:
                            top_rows_out(n + 1, 1 - par, 0)
                        exp(n, u, 3)
                        g, m = unit(0, u)
                        if not (last and g):
                            difference_sizes(n + g, m + 1, slots(u)[2])

                for m in range(1, AHEAD, 2):
                    difference_sizes(0, m, MX[1])
                top_rows_out(0, 0, 0)
                group(0, 0)
                group(1, 1)
                with act.Fori(1, N2 // 2 - 1) as k:
                    for par in range(2):
                        group(2 * k + par, par)
                group(N2 - 2, 0)
                group(N2 - 1, 1, last=True)

            @block.vector
            def _(dve):
                def maxima(n, m, slot):
                    if m in (0, UNITS // 2):
                        if not isinstance(n, int) or n > 0:
                            dve.wait_ge(parts_ready, 2 * n - 1 + (m > 0))
                    if m % 2 == 1:
                        wait_apart(dve, gap_ready, (UNITS * n + m + 1) // 2)
                        nc.vector.tensor_tensor_reduce(
                            out=gap, in0=slot[:, 0:HALF], in1=gap, scale=0.5, scalar=LOWEST, op0=ALU.add, op1=ALU.max,
                            accum_out=tops[:, m:m + 1]).then_inc(top_done, 1)
                    else:
                        dve.wait_ge(mx_done, UNITS * n + m + 1)
                        nc.vector.tensor_reduce(tops[:, m:m + 1], slot, AX.X, ALU.max).then_inc(top_done, 1)

                def half_tops(v, h):
                    return v[:, 16 * h:16 * h + 16].rearrange("p (t j) -> p t j", j=GH)

                def half_part(c, h):
                    return top_parts[:, 4 * h:4 * h + 4, c, :]

                def top_part0(n, h, steps):
                    dve.wait_ge(top_done, UNITS * n + 16 * (h + 1))
                    if not isinstance(n, int) or n > 0:
                        dve.wait_ge(topT_done, 2 * n - 1 + h)
                    steps.done(nc.vector.tensor_scalar(half_part(0, h), half_tops(tops, h), -1.0, None, ALU.mult))

                def top_left(h, steps):
                    steps.now()
                    steps.done(nc.vector.scalar_tensor_tensor(half_tops(top_rest, h), half_tops(tops, h), -1.0,
                                                              half_part(0, h), ALU.mult, ALU.subtract))

                def top_part1(h, steps):
                    steps.now()
                    steps.done(nc.vector.tensor_copy(half_part(1, h), half_tops(top_rest, h)))

                def top_part2(h, steps):
                    steps.now()
                    nc.vector.tensor_tensor(half_part(2, h), half_tops(top_rest, h), half_part(1, h), ALU.subtract
                                            ).then_inc(parts_ready, 1)

                def spread_tops(n, par, h):
                    dve.wait_ge(topT_read, 2 * n + h + 1)
                    rows = q_rows[par][MAXROW:MAXROW + PARTS * GH, :, h * HALF:(h + 1) * HALF]
                    nc.vector.tensor_copy(rows[:, 1:, :], rows[:, 0:1, :].to_broadcast([PARTS * GH, GH - 1, HALF])
                                          ).then_inc(tops_ready, 1)

                def read_outputs(n, h):
                    dve.wait_ge(lpv_done, STEPS3 * n + T * (h + 1))
                    nc.vector.transpose(outT, OT).then_inc(out_read, 1)

                def invert(n, h, steps):
                    dve.wait_ge(out_read, 2 * n + h + 1)
                    steps.done(nc.vector.reciprocal(out_rden, outT.rearrange("p (b r) -> p b r", r=32)[:, :, KD]))

                def normalise(n, h, steps):
                    steps.now()
                    if not isinstance(n, int) or n > 0 or h > 0:
                        dve.wait_ge(proj3_done, 2 * n + h)
                    steps.done(nc.vector.tensor_tensor(
                        out_norm.rearrange("p (b r) -> p b r", r=32)[:, :, 0:KD],
                        outT.rearrange("p (b r) -> p b r", r=32)[:, :, 0:KD],
                        out_rden.unsqueeze(2).to_broadcast([P, HALF // 32, KD]), ALU.mult))

                def turn_outputs(steps):
                    steps.now()
                    nc.vector.transpose(aoT, out_norm).then_inc(ao_ready, 1)

                def add(n, h):
                    dve.wait_ge(proj3_done, 2 * n + h + 1)
                    upto(dve, proj3_added, 2 * n + h)
                    v = batch_tiles(acc, n, 4 * h, 4)
                    nc.vector.tensor_tensor(v, PO.rearrange("p (t c) -> p t c", t=4), v, ALU.add).then_inc(proj3_added, 1)

                def group(n, par, first=False, last=False):
                    steps = Steps(dve, d3, D3, n)
                    if not first:
                        steps.base = steps.base - 2
                    for u in range(STEPS3):
                        g, m = unit(0, u)
                        units = not (last and g)
                        if u == TURN1 + 1:
                            spread_tops(n, par, 1)
                        if u == TURN0 + 1 and not last:
                            spread_tops(n + 1, 1 - par, 0)
                        if units:
                            maxima(n + g, m, slots(u)[0])
                        if u == TURN1 - 2:
                            top_part0(n, 1, steps)
                        if u == TURN1 - 1:
                            top_part1(1, steps)
                        if u == TURN0 - 2 and not last:
                            top_part0(n + 1, 0, steps)
                        if u == TURN0 - 1 and not last:
                            top_part1(0, steps)
                        if u == 0 and not first:
                            read_outputs(n - 1, 1)
                        if u == 1 and not first:
                            normalise(n - 1, 1, steps)
                        if u == PROJECT1 and not first:
                            add(n - 1, 1)
                        if u == T:
                            read_outputs(n, 0)
                        if u == T + 1:
                            normalise(n, 0, steps)
                        if u == PROJECT0:
                            add(n, 0)
                        if units:
                            maxima(n + g, m + 1, slots(u)[2])
                        if u == TURN1 - 2:
                            top_left(1, steps)
                        if u == TURN1 - 1:
                            top_part2(1, steps)
                        if u == TURN0 - 2 and not last:
                            top_left(0, steps)
                        if u == TURN0 - 1 and not last:
                            top_part2(0, steps)
                        if u == 0 and not first:
                            invert(n - 1, 1, steps)
                        if u == 1 and not first:
                            turn_outputs(steps)
                        if u == T:
                            invert(n, 0, steps)
                        if u == T + 1:
                            turn_outputs(steps)
                    assert steps.n == D3 - 2 * first - 3 * last, steps.n

                start = Steps(dve, d3s)
                for m in range(AHEAD):
                    maxima(0, m, MX[m % 2])
                    if m == UNITS // 2 - 1:
                        top_part0(0, 0, start)
                        top_left(0, start)
                        top_part1(0, start)
                        top_part2(0, start)
                spread_tops(0, 0, 0)
                group(0, 0, first=True)
                group(1, 1)
                with dve.Fori(1, N2 // 2 - 1) as k:
                    for par in range(2):
                        group(2 * k + par, par)
                group(N2 - 2, 0)
                group(N2 - 1, 1, last=True)
                read_outputs(N2 - 1, 1)
                end = Steps(dve, d3s, 3, 1)
                invert(N2 - 1, 1, end)
                normalise(N2 - 1, 1, end)
                turn_outputs(end)
                add(N2 - 1, 1)

        a4 = Arena()
        TC = P // E
        mT = a4.take(B * S, F16).rearrange("p (h t) -> p h t", h=2)
        mT_b = [a4.take(S) for _ in range(B)]
        cw = a4.take(E * NT).rearrange("p (e t) -> p e t", e=E)
        c_tok = a4.take(NT * E).rearrange("p (t e) -> p t e", t=NT)
        logits = a4.take(NT * E).rearrange("p (t e) -> p t e", t=NT)
        sorted8 = a4.take(NT * E).rearrange("p (t e) -> p t e", t=NT)
        index8 = a4.take(NT * E, U32).rearrange("p (t e) -> p t e", t=NT)
        index_f = a4.take(NT * 2).rearrange("p (t k) -> p t k", t=NT)
        picked = a4.take(NT * E).rearrange("p (t e) -> p t e", t=NT)
        row_top, row_sum, row_rcp = (a4.take(NT) for _ in range(3))
        shift = a4.take(NT)
        w1_e = [a4.take(F, F16).rearrange("p (h f) -> p h f", h=2) for _ in range(2)]
        w2_e = [a4.take(FC * D, F16).rearrange("p (h c d) -> p h c d", h=2, c=FC) for _ in range(2)]
        act_f32 = [[a4.take(S) for _ in range(FC)] for _ in range(2)]
        act_hi = [[a4.take(S // 2, F16) for _ in range(FC)] for _ in range(2)]
        act_lo = [[a4.take(S // 2, F16) for _ in range(FC)] for _ in range(2)]
        cT = a4.take(2 * P)
        b2_diag = a4.take(TC * D).rearrange("p (t d) -> p t d", t=TC)
        HP = [bank(0, 2), bank(2, 2)]
        YP = [bank(4, 2), bank(6, 2)]
        LOGITS = [bank(n)[:, 0:T * E] for n in (4, 6, 5, 7)]
        TURNED = [*YP, *HP]

        mT_ps, mT_ready, mhi_ready, mlo_ready = sem("mT_ps"), sem("mT_ready"), sem("mhi_ready"), sem("mlo_ready")
        lg_ps, lg_ready, exp4, cen4, d4, cw_ready = (sem("lg_ps"), sem("lg_ready"), sem("exp4"), sem("cen4"), sem("d4"),
                                                     sem("cw_ready"))
        w1_ready = [sem(f"w1_ready{m}") for m in range(2)]
        w2_ready = [sem(f"w2_ready{m}") for m in range(2)]
        h_done, gelu_done, y_done, y_added = sem("h_done"), sem("gelu_done"), sem("y_done"), sem("y_added")
        act_split = sem("act_split")
        diag_clear, cT_ps, cT_ready, b2_done, b2_added = (sem("diag_clear"), sem("cT_ps"), sem("cT_ready"), sem("b2_done"),
                                                          sem("b2_added"))
        stats5, pow5, rstd5, normed5, out_ready, d5 = (sem("stats5"), sem("pow5"), sem("rstd5"), sem("normed5"),
                                                       sem("out_ready"), sem("d5"))
        dve_normed5, b2_in, stored = sem("dve_normed5"), sem("b2_in"), sem("stored")
        last_out_ready = sem("last_out_ready")
        N4 = E * B
        BIASES_AT = 2
        HT = T // 2

        def over_e(col):
            return col.unsqueeze(2).to_broadcast([P, NT, E])

        with nc.Block() as block:
            @block.sync
            def _(sp):
                def load(e, par):
                    sp.dma_start(w1_e[par], w1_parts[:, bass.ds(e, 1), :, :].rearrange("p a h f -> p (a h) f")
                                 ).then_inc(w1_ready[par], 16)
                    sp.dma_start(w2_e[par].rearrange("p h c d -> p h (c d)"),
                                 w2_parts[:, bass.ds(e, 1), :, :].rearrange("p a h f -> p (a h) f")
                                 ).then_inc(w2_ready[par], 16)

                for e in range(2):
                    load(e, e)
                sp.wait_ge(diag_clear, 1)
                for t in range(TC):
                    sp.dma_start(b2_diag[t * E:(t + 1) * E, t, :], b2).then_inc(b2_in, 16)
                with sp.Fori(1, E // 2) as k:
                    for par in range(2):
                        sp.wait_ge(y_done, B * (2 * k + par - 1))
                        load(2 * k + par, par)
                for b in range(B):
                    now = slice(b * T, (b + 1) * T)
                    if b < B - 1:
                        sp.wait_ge(out_ready, b + 1)
                    else:
                        sp.wait_ge(last_out_ready, 1)
                    sp.dma_start(out_dram[:, now, :], X[:, now, :]).then_inc(stored, 16)
                sp.wait_ge(stored, 16 * B)

            @block.tensor
            def _(pe):
                def turn_inputs(b):
                    for t in range(T):
                        last = nc.tensor.transpose(TURNED[b][:, t * P:(t + 1) * P], acc[:, b * T + t, :], ident[:, :])
                    last.then_inc(mT_ps, 1)

                def route(b):
                    pe.wait_ge(mT_ready, b + 1)
                    pe.wait_ge(mhi_ready, b % 2 + 1)
                    for t in range(T):
                        last = nc.tensor.matmul(LOGITS[b][:, t * E:(t + 1) * E], mT_b[b][:, t * P:(t + 1) * P],
                                                w_router[:, :], start=True, stop=True, skip_group_check=True)
                    last.then_inc(lg_ps, 1)

                def hidden(e, par, b, first):
                    n = B * e + b
                    if b == 0:
                        pe.wait_ge(w1_ready[par], 16 * (e // 2 + 1))
                    if isinstance(e, int) and e == 0:
                        pe.wait_ge(mlo_ready, b + 1)
                    for c in range(FC):
                        if first:
                            pe.wait_ge(mhi_ready, c + 3)
                        elif c == 0 and isinstance(n, int) and n == B:
                            pe.wait_ge(cT_ready, 1)
                        else:
                            pe.wait_ge(gelu_done, FC * (n - 1) + c + 1)
                        for half in range(2):
                            tok = slice(b * S + half * HALF, b * S + (half + 1) * HALF)
                            passes = ((0, 0), (0, 1), (1, 0))
                            for m, (w, x) in enumerate(passes):
                                last = nc.tensor.matmul(HP[c][:, half * HALF:(half + 1) * HALF],
                                                        w1_e[par][:, w, c * P:(c + 1) * P], mT[:, x, tok],
                                                        start=(m == 0), stop=(m == 2))
                        last.then_inc(h_done, 1)

                def output(n, par, slot):
                    pe.wait_ge(act_split, FC * (n + 1))
                    if isinstance(n, int) and n < 2:
                        pe.wait_ge(lg_ready, n + 3)
                    elif isinstance(n, int) and BIASES_AT < n <= BIASES_AT + B:
                        pe.wait_ge(b2_added, n - BIASES_AT)
                    else:
                        pe.wait_ge(y_added, n - 1)
                    pe.wait_ge(w2_ready[par], 16 * (n // (2 * B) + 1))
                    for t in range(T):
                        tok = slice(t * P, (t + 1) * P)
                        for c in range(FC):
                            passes = ((act_hi, 0), (act_hi, 1), (act_lo, 0))
                            for m, (h, w) in enumerate(passes):
                                last = nc.tensor.matmul(YP[slot][:, tok], h[slot][c][:, tok], w2_e[par][:, w, c, :],
                                                        start=(c == 0 and m == 0), stop=(c == FC - 1 and m == 2))
                    last.then_inc(y_done, 1)

                def turn_weights():
                    pe.wait_ge(cw_ready, 1)
                    pe.wait_ge(gelu_done, FC * B - 1)
                    for k in range(2):
                        last = nc.tensor.transpose(HP[0][:, k * P:(k + 1) * P],
                                                   c_tok[:, k * TC:(k + 1) * TC, :].rearrange("p t e -> p (t e)"), ident[:, :])
                    last.then_inc(cT_ps, 1)

                def bias(b):
                    pe.wait_ge(y_added, BIASES_AT + b)
                    if b == 0:
                        pe.wait_ge(b2_in, 16 * TC)
                        pe.wait_ge(cT_ready, 1)
                    k, at = b * T // TC, b * T % TC
                    for half in range(2):
                        first = at + half * T // 2
                        last = nc.tensor.matmul(YP[(b + 1) % 2][:, half * HALF:(half + 1) * HALF], cT[:, k * P:(k + 1) * P],
                                                b2_diag[:, first:first + T // 2, :].rearrange("p t d -> p (t d)"),
                                                start=True, stop=True)
                    last.then_inc(b2_done, 1)

                def expert(e, par, biases=False):
                    for b in range(B):
                        hidden(e, par, b, False)
                        output(B * e + b - 1, par if b > 0 else 1 - par, (b - 1) % 2)
                        if biases and b < B - 1:
                            bias(b + 1)

                for b in range(B):
                    turn_inputs(b)
                for b in range(B):
                    route(b)
                hidden(0, 0, 0, True)
                hidden(0, 0, 1, False)
                output(0, 0, 0)
                hidden(0, 0, 2, False)
                output(1, 0, 1)
                hidden(0, 0, 3, False)
                turn_weights()
                output(2, 0, 0)
                bias(0)
                expert(1, 1, biases=True)
                with pe.Fori(1, E // 2) as k:
                    for par in range(2):
                        expert(2 * k + par, par)
                output(N4 - 1, 1, 1)

            @block.scalar
            def _(act):
                def inputs(b):
                    act.wait_ge(mT_ps, b + 1)
                    nc.scalar.copy(mT_b[b], TURNED[b]).then_inc(mT_ready, 1)

                def inputs_hi(b):
                    nc.scalar.copy(mT[:, 0, b * S:(b + 1) * S], TURNED[b]).then_inc(mhi_ready, 1)

                def unit(e, b):
                    n = B * e + b
                    for c in range(FC):
                        if c == 0 and (not isinstance(n, int) or n >= 2):
                            act.wait_ge(y_done, n - 1)
                        wait_apart(act, h_done, FC * n + c + 1)
                        at = FC * e + c
                        bias = b1T[:, at:at + 1] if isinstance(e, int) else b1T[:, bass.ds(at, 1)]
                        nc.scalar.activation(act_hi[b % 2][c], HP[c], ACT.Gelu, scale=1.0 / WSCALE, bias=bias)
                        nc.scalar.activation(act_f32[b % 2][c], HP[c], ACT.Gelu, scale=1.0 / WSCALE, bias=bias
                                             ).then_inc(gelu_done, 1)

                def normed(b, tiles):
                    act.wait_ge(rstd5, 2 * b + 2)
                    for t in range(b * T, b * T + tiles):
                        last = nc.scalar.activation(hs[:, t, :], hs[:, t, :], ACT.Identity, scale=rstd[:, t:t + 1],
                                                    bias=shift[:, t:t + 1])
                    last.then_inc(normed5, 1)

                inputs(0)
                inputs_hi(0)
                inputs(1)
                inputs_hi(1)
                inputs(2)
                inputs(3)
                inputs_hi(2)
                inputs_hi(3)
                act.wait_ge(cen4, 1)
                nc.scalar.activation(logits, logits, ACT.Exp).then_inc(exp4, 1)
                for e in range(2):
                    for b in range(B):
                        unit(e, b)
                    if e == 0:
                        act.wait_ge(cT_ps, 1)
                        nc.scalar.copy(cT, HP[0][:, 0:2 * P]).then_inc(cT_ready, 1)
                with act.Fori(2, E) as e:
                    for b in range(B):
                        unit(e, b)
                for b in range(B - 1):
                    normed(b, T)
                normed(B - 1, HT)

            @block.gpsimd
            def _(pool):
                nc.gpsimd.memset(b2_diag, 0.0).then_inc(diag_clear, 1)

                def residual(b):
                    pool.wait_ge(normed5, b + 1)
                    nc.gpsimd.tensor_tensor(batch(X, b), batch(X, b), batch(hs, b), ALU.add).then_inc(out_ready, 1)

                for b in range(B):
                    now = slice(b * T, (b + 1) * T)
                    pool.wait_ge(stats5, b + 1)
                    nc.gpsimd.tensor_scalar(shift[:, now], mv[:, now, 0], -1.0, None, ALU.mult).then_inc(pow5, 1)
                    nc.gpsimd.tensor_scalar(rstd[:, now], mv[:, now, 1], EPS, None, ALU.add).then_inc(pow5, 1)
                    pool.wait_ge(pow5, 2 * b + 2)
                    nc.gpsimd.tensor_tensor(rstd[:, now], rstd[:, now], mhalf[:, now], ALU.pow).then_inc(rstd5, 1)
                    pool.wait_ge(rstd5, 2 * b + 1)
                    nc.gpsimd.tensor_tensor(shift[:, now], shift[:, now], rstd[:, now], ALU.mult).then_inc(rstd5, 1)
                    if b > 0:
                        residual(b - 1)

            @block.vector
            def _(dve):
                steps = Steps(dve, d4)

                def step(ins):
                    steps.done(ins)
                    steps.now()

                def low(b):
                    dve.wait_ge(mhi_ready, b + 1)
                    nc.vector.tensor_tensor(mT[:, 1, b * S:(b + 1) * S], mT_b[b], mT[:, 0, b * S:(b + 1) * S],
                                            ALU.subtract).then_inc(mlo_ready, 1)

                def take_logits(b):
                    dve.wait_ge(lg_ps, b + 1)
                    nc.vector.tensor_tensor(batch(logits, b), LOGITS[b].rearrange("p (t e) -> p t e", t=T),
                                            wide(rb_b[:, :]), ALU.add).then_inc(lg_ready, 1)

                def low_act(n, slot):
                    for c in range(FC):
                        dve.wait_ge(gelu_done, FC * n + c + 1)
                        nc.vector.tensor_tensor(act_lo[slot][c], act_f32[slot][c], act_hi[slot][c], ALU.subtract
                                                ).then_inc(act_split, 1)

                def add(e, b):
                    n = B * e + b
                    dve.wait_ge(y_done, n + 1)
                    if isinstance(e, int) and e == 1:
                        dve.wait_ge(b2_added, b + 1)
                    elif not isinstance(n, int) or n >= B:
                        dve.wait_ge(y_added, n - B + 1)
                    for t in range(b * T, (b + 1) * T):
                        c = cw[:, e, t:t + 1] if isinstance(e, int) else cw[:, bass.ds(e, 1), t]
                        last = nc.vector.scalar_tensor_tensor(hs[:, t, :], YP[b % 2][:, (t % T) * P:(t % T + 1) * P], c,
                                                              hs[:, t, :], ALU.mult, ALU.add)
                    last.then_inc(y_added, 1)

                low(0)
                take_logits(0)
                low(1)
                take_logits(1)
                take_logits(2)
                take_logits(3)
                dve.wait_ge(lg_ready, B)
                step(nc.vector.tensor_reduce(row_top, logits, AX.X, ALU.max))
                nc.vector.tensor_tensor(logits, logits, over_e(row_top), ALU.subtract).then_inc(cen4, 1)
                low(2)
                low(3)
                dve.wait_ge(exp4, 1)
                step(nc.vector.tensor_reduce(row_sum, logits, AX.X, ALU.add))
                step(nc.vector.reciprocal(row_rcp, row_sum))
                step(nc.vector.tensor_tensor(logits, logits, over_e(row_rcp), ALU.mult))
                for t in range(NT):
                    steps.done(nc.vector.max(sorted8[:, t, :], logits[:, t, :]))
                steps.now()
                low_act(0, 0)
                for t in range(NT):
                    steps.done(nc.vector.max_index(index8[:, t, :], sorted8[:, t, :], logits[:, t, :]))
                steps.now()
                low_act(1, 1)
                step(nc.vector.tensor_copy(index_f, index8[:, :, 0:2]))
                step(nc.vector.scalar_tensor_tensor(row_sum, sorted8[:, :, 0], 1e-8, sorted8[:, :, 1], ALU.add, ALU.add))
                step(nc.vector.reciprocal(row_rcp, row_sum))
                for k, dst in ((0, c_tok), (1, picked)):
                    step(nc.vector.tensor_tensor(dst, wide(iota_e[:, :], NT), over_e(index_f[:, :, k]), ALU.is_equal))
                    step(nc.vector.tensor_tensor(dst, dst, over_e(sorted8[:, :, k]), ALU.mult))
                step(nc.vector.tensor_tensor(c_tok, c_tok, picked, ALU.add))
                step(nc.vector.tensor_scalar(row_rcp, row_rcp, 0.3, None, ALU.mult))
                nc.vector.tensor_tensor(c_tok, c_tok, over_e(row_rcp), ALU.mult).then_inc(cw_ready, 1)
                low_act(2, 0)
                dve.wait_ge(cw_ready, 1)
                step(nc.vector.tensor_scalar(cw.rearrange("p e t -> p t e"), c_tok, 1.0 / WSCALE, None, ALU.mult))

                def add_bias(b):
                    dve.wait_ge(b2_done, b + 1)
                    dve.wait_ge(y_added, b + 1)
                    v = batch(hs, b)
                    nc.vector.tensor_tensor(v, YP[(b + 1) % 2].rearrange("p (t d) -> p t d", t=T), v, ALU.add
                                            ).then_inc(b2_added, 1)

                def finish(b):
                    dve.wait_ge(rstd5, 2 * b + 1)
                    for t in range(b * T + HT, (b + 1) * T):
                        last = nc.vector.tensor_scalar(hs[:, t, :], hs[:, t, :], mv[:, t, 0:1], rstd[:, t:t + 1],
                                                       ALU.subtract, ALU.mult)
                    last.then_inc(dve_normed5, 1)
                    dve.wait_ge(dve_normed5, 1)
                    dve.wait_ge(normed5, b + 1)
                    nc.vector.tensor_tensor(batch(X, b), batch(X, b), batch(hs, b), ALU.add).then_inc(last_out_ready, 1)

                for e in range(2):
                    for b in range(B):
                        if B * e + b > 1:
                            low_act(B * e + b + 1, (b + 1) % 2)
                        add(e, b)
                        if BIASES_AT <= B * e + b < BIASES_AT + B:
                            add_bias(B * e + b - BIASES_AT)
                with dve.Fori(2, E - 1) as e:
                    for b in range(B):
                        low_act(B * e + b + 1, (b + 1) % 2)
                        add(e, b)
                for b in range(B):
                    if b < B - 1:
                        low_act(N4 - B + b + 1, (b + 1) % 2)
                    add(E - 1, b)
                    dve.wait_ge(y_added, N4 - B + b + 1)
                    for t in range(b * T, (b + 1) * T):
                        steps.done(nc.vector.bn_stats(stats[:, t, :], hs[:, t, :]))
                    steps.now()
                    for t in range(b * T, (b + 1) * T):
                        last = nc.vector.bn_aggr(mv[:, t, :], stats[:, t, :])
                    last.then_inc(stats5, 1)
                finish(B - 1)


_INS = ["L0_attn_states", "L0_attn_Wq", "L0_attn_bq", "L0_attn_Wk", "L0_attn_bk", "L0_attn_Wv", "L0_attn_bv",
        "L0_attn_Wo", "L0_attn_bo", "L0_ffn_q_w", "L0_ffn_q_b", "L0_ffn_k_w", "L0_ffn_k_b", "L0_ffn_v_w",
        "L0_ffn_v_b", "L0_ffn_o_w", "L0_ffn_o_b", "L0_ffn_router_w", "L0_ffn_router_b", "L0_ffn_w1", "L0_ffn_b1",
        "L0_ffn_w2", "L0_ffn_b2"]


def kernel(**inputs):
    import numpy as np
    from concourse import bacc
    from concourse.bass_utils import run_bass_kernel_spmd

    nc = bacc.Bacc("TRN2", target_bir_lowering=False, num_devices=1)
    arrays, args = {}, []
    for name in _INS:
        a = np.ascontiguousarray(inputs[name])
        arrays[f"in_{name}"] = a
        args.append(nc.dram_tensor(f"in_{name}", a.shape, mybir.dt.from_np(a.dtype), kind="ExternalInput").ap())
    out = nc.dram_tensor("out_x", (B, S, D), F32, kind="ExternalOutput").ap()
    build(nc, *args, out)
    r = run_bass_kernel_spmd(nc, [arrays], core_ids=[0])
    return r.results[0]["out_x"]
```

```python
from contextlib import ExitStack

import concourse.bass as bass
from concourse import mybir

F32 = mybir.dt.float32
F16 = mybir.dt.float16
BF16 = mybir.dt.bfloat16
U32 = mybir.dt.uint32
ALU = mybir.AluOpType
ACT = mybir.ActivationFunctionType
AX = mybir.AxisListType

P = 128
B, S, D = 4, 1024, 128
T = S // P
NT = B * T
HALF = 512
H1, DH = 16, 64
PAIRS = H1 // 2
N1 = B * PAIRS
WSCALE = 64.0
H2, KD = 16, 4
LAT = H2 * KD
GH = 4
GROUPS = H2 // GH
N2 = B * GROUPS
PARTS = 3
PROD = PARTS * PARTS * KD
MAXROW = 64
E, F = 8, 256
FC = F // P
EPS = 1e-5
LOWEST = -3.4e38

CAUSAL = [
    [(0, 0, 512, 0), (1, 128, 384, 512), (3, 384, 128, 896)],
    [(0, 512, 512, 0), (1, 512, 512, 512)],
    [(2, 512, 512, 0), (3, 512, 512, 512)],
    [(4, 512, 512, 0), (5, 640, 384, 512), (7, 896, 128, 896)],
    [(2, 256, 256, 0), (6, 768, 256, 256)],
]
WIDTH = [1024, 1024, 1024, 1024, 512]
QSLOT, KSLOT, VSLOT, OSLOT, NSLOT = 0, 2, 4, 7, 9


class Steps:

    def __init__(self, eng, sem, per=0, turn=0):
        self.eng, self.sem, self.n, self.turn = eng, sem, 0, turn
        self.base = turn * per

    def done(self, ins):
        self.n += 1
        ins.then_inc(self.sem, 1)
        return self.n

    def now(self, n=None):
        self.eng.wait_ge(self.sem, self.count(n))

    def count(self, n=None):
        return self.base + (self.n if n is None else n)


def upto(eng, sem, count):
    if not isinstance(count, int) or count > 0:
        eng.wait_ge(sem, count)


def build(nc, states, Wq, bq, Wk, bk, Wv, bv, Wo, bo, q_w, q_b, k_w, k_b, v_w, v_b, o_w, o_b,
          router_w, router_b, w1, b1, w2, b2, out):
    x_dram = states.rearrange("b (t p) d -> p (b t) d", p=P)
    out_dram = out.rearrange("b (t p) d -> p (b t) d", p=P)
    q_dram = nc.dram_tensor("latent_q", (B, PARTS, LAT, S), BF16, kind="Internal").ap()
    k_dram = nc.dram_tensor("latent_k", (B, PARTS, PARTS, LAT, S), BF16, kind="Internal").ap()
    kpm_dram = nc.dram_tensor("latent_kpm", (B, PARTS, PARTS, LAT, S), BF16, kind="Internal").ap()

    with ExitStack() as ctx:
        def sb(name, shape, dt=F32):
            return ctx.enter_context(nc.sbuf_tensor(name, shape, dt))

        def sem(name):
            return ctx.enter_context(nc.semaphore(name))

        apart = sem("apart")

        def wait_apart(eng, semaphore, count):
            if not isinstance(count, int) or count > 0:
                eng.wait_ge(semaphore, count)
                eng.sem_inc(apart, 1)

        psum = ctx.enter_context(nc.psum_tensor("psum", [P, 8 * HALF], F32))

        def bank(n, count=1):
            return psum[:, n * HALF:(n + count) * HALF]

        X = sb("X", [P, NT, D])
        acc = sb("acc", [P, NT, D])
        hs = sb("hs", [P, NT, D])
        ident = sb("ident", [P, P])
        identb = sb("identb", [P, P], BF16)
        stats = sb("stats", [P, NT, 6])
        mv = sb("mv", [P, NT, 2])
        rstd = sb("rstd", [P, NT])
        mhalf = sb("mhalf", [P, NT])
        bo_b = sb("bo_b", [P, D])
        vb_b = sb("vb_b", [P, LAT])
        ob_b = sb("ob_b", [P, D])
        rb_b = sb("rb_b", [P, E])
        w_lat = sb("w_lat", [P, 2 * LAT])
        w_lat_in = sb("w_lat_in", [P, 2 * LAT])
        b_lat = sb("b_lat", [P, 1])
        w_lv = sb("w_lv", [P, LAT])
        w_router = sb("w_router", [P, E])
        b1_in = sb("b1_in", [P, P])
        b1T = sb("b1T", [P, E * FC])
        iota_e = sb("iota_e", [P, E])
        ARENA, TOP = 38400, 3 * E * F
        arena = sb("arena", [P, ARENA])

        class Arena:
            def __init__(self, at=0, end=ARENA - TOP):
                self.at, self.end = at, end

            def take(self, words, dt=F32):
                v = arena[:, self.at:self.at + words]
                self.at += words
                assert self.at <= self.end, self.at
                return v if dt == F32 else v.bitcast(dt)

        a1 = Arena()
        xT_all = a1.take(B * S, F16).rearrange("p (b h s) -> p b h s", b=B, h=2)
        W_all = a1.take(PAIRS * NSLOT * P // 2, F16).rearrange("p (n j c) -> p n j c", n=PAIRS, j=NSLOT)
        qk_bias = a1.take(2 * PAIRS).rearrange("p (t n) -> p t n", t=2)
        pick_bias = a1.take(P // 2, F16)
        ones = a1.take(DH)
        a0 = Arena(a1.at)
        w_in = a0.take(3 * H1 * DH).rearrange("p (t n) -> p t n", t=3)
        wo_in0 = a0.take(PAIRS * D).rearrange("p (n d) -> p n d", n=PAIRS)
        bias_in = a0.take(2 * P).rearrange("p (t n) -> p t n", t=2)
        vbias = a0.take(H1 * DH)
        vb_hi = a0.take(H1 * DH // 2, F16)
        shift0 = a0.take(NT)

        x_in = [sem(f"x_in{b}") for b in range(B)]
        wo_got, wo_split = sem("wo_got"), sem("wo_split")
        small_in, w_got, b_got = sem("small_in"), sem("w_got"), sem("b_got")
        consts0, consts = sem("consts0"), sem("consts")
        SMALL = 4 + 5 + 2 * KD
        d0, p0, a0s = sem("d0"), sem("p0"), sem("a0s")
        shift_half, shift_done, xn_act = sem("shift_half"), sem("shift_done"), sem("xn_act")
        rstd0, xn0, xt_ps, xt_hi, xt_lo = sem("rstd0"), sem("xn0"), sem("xt_ps"), sem("xt_hi"), sem("xt_lo")
        biasT_ps, whi_done, wlo_done, mv0 = sem("biasT_ps"), sem("whi_done"), sem("wlo_done"), sem("mv0")

        def norm_stats(dve, steps, src, b):
            for t in range(T):
                steps.done(nc.vector.bn_stats(stats[:, b * T + t, :], src(t)))
            steps.now()
            for t in range(b * T, (b + 1) * T):
                last = nc.vector.bn_aggr(mv[:, t, :], stats[:, t, :])
            return last

        with nc.Block() as block:
            @block.sync
            def _(sp):
                for b in range(B):
                    sp.dma_start(X[:, b * T:(b + 1) * T, :], x_dram[:, b * T:(b + 1) * T, :]).then_inc(x_in[b], 16)
                sp.dma_start(wo_in0, Wo.rearrange("(n r) d -> r n d", n=PAIRS)).then_inc(wo_got, 16)
                HD = D // H2
                for dst, src in ((w_lat_in[:, 0:LAT], q_w.rearrange("d (h r) -> d h r", r=HD)[:, :, 0:KD]),
                                 (w_lat_in[:, LAT:], k_w), (w_lv[:, :], v_w), (w_router[:, :], router_w),
                                 (b1_in[0:E * FC, :], b1.rearrange("e (c f) -> (e c) f", c=FC))):
                    sp.dma_start(dst, src).then_inc(small_in, 16)
                for d in range(KD):
                    for at, src, step in ((0, q_b, HD), (LAT, k_b, KD)):
                        sp.dma_start(b_lat[at + d * H2:at + (d + 1) * H2, :],
                                     src.rearrange("(h r) -> h r", r=step)[:, d:d + 1], allow_slow_non_contiguous=True).then_inc(small_in, 16)

            @block.scalar
            def _(act):
                for t, w in enumerate((Wq, Wk, Wv)):
                    act.dma_start(w_in[:, t, :], w).then_inc(w_got, 16)
                act.wait_ge(consts, 4)
                for t, w in enumerate((bq, bk)):
                    act.dma_start(bias_in[0:PAIRS, t, :], w.rearrange("(n c) -> n c", n=PAIRS)).then_inc(b_got, 16)
                for row in (0, 32):
                    act.dma_start(vbias[row:row + 1, :], bv.rearrange("(a n) -> a n", a=1)).then_inc(b_got, 16)
                for dst, src in ((bo_b, bo), (vb_b, v_b), (ob_b, o_b), (rb_b, router_b)):
                    act.dma_start(dst[:, :], src.partition_broadcast(P)).then_inc(small_in, 16)
                act.wait_ge(w_got, 48)
                for t, slot in enumerate((QSLOT, KSLOT, VSLOT)):
                    nc.scalar.activation(W_all[:, :, slot, :], w_in[:, t, :].rearrange("p (n c) -> p n c", n=PAIRS),
                                         ACT.Copy, scale=WSCALE).then_inc(whi_done, 1)
                act.wait_ge(b_got, 64)
                nc.scalar.activation(vb_hi[0:64, :], vbias[0:64, :], ACT.Copy, scale=WSCALE).then_inc(whi_done, 1)
                for b in range(B // 2, B):
                    act.wait_ge(shift_done, b + 1)
                    for t in range(b * T, (b + 1) * T):
                        last = nc.scalar.activation(hs[:, t, :], X[:, t, :], ACT.Identity, scale=rstd[:, t:t + 1],
                                                    bias=shift0[:, t:t + 1])
                    last.then_inc(xn_act, 1)
                for b in range(B):
                    act.wait_ge(xt_ps, b + 1)
                    nc.scalar.copy(xT_all[:, b, 0, :], bank(2 * b, 2)).then_inc(xt_hi, 1)
                act.wait_ge(biasT_ps, 1)
                act.wait_ge(xt_lo, 1)
                nc.scalar.copy(qk_bias, bank(0)[:, 0:2 * PAIRS].rearrange("p (t n) -> p t n", t=2)).then_inc(a0s, 1)
                nc.scalar.copy(b1T[:, :], bank(0)[:, 2 * PAIRS:2 * PAIRS + E * FC]).then_inc(a0s, 1)
                act.wait_ge(small_in, 16 * SMALL)
                for t in range(2):
                    half = slice(t * LAT, (t + 1) * LAT)
                    nc.scalar.copy(w_lat[:, half].rearrange("p (d h) -> p d h", d=KD),
                                   w_lat_in[:, half].rearrange("p (h d) -> p d h", d=KD)).then_inc(a0s, 1)
                nc.scalar.activation(acc[:, :, :], bo_b[:, :].unsqueeze(1).to_broadcast([P, NT, D]), ACT.Copy, scale=WSCALE
                                     ).then_inc(a0s, 1)
                act.wait_ge(a0s, 5)

            @block.gpsimd
            def _(pool):
                nc.gpsimd.memset(ident[:, :], 0.0).then_inc(consts0, 1)
                pool.wait_ge(consts0, 1)
                nc.gpsimd.affine_select(out=ident[:, :], in_=ident[:, :], compare_op=ALU.not_equal, fill=1.0,
                                        base=0, pattern=[[-1, P]], channel_multiplier=1).then_inc(consts, 1)
                nc.gpsimd.memset(vbias, 0.0).then_inc(consts, 1)
                nc.gpsimd.memset(bias_in, 0.0).then_inc(consts, 1)
                nc.gpsimd.memset(mhalf[:, :], -0.5).then_inc(consts, 1)
                nc.gpsimd.memset(ones, 1.0).then_inc(consts, 1)
                pool.wait_ge(consts, 1)
                nc.gpsimd.tensor_copy(identb[:, :], ident[:, :]).then_inc(consts, 1)
                pool.wait_ge(consts, 6)
                for b in range(B):
                    now = slice(b * T, (b + 1) * T)
                    pool.wait_ge(mv0, b + 1)
                    nc.gpsimd.tensor_scalar(rstd[:, now], mv[:, now, 1], EPS, None, ALU.add).then_inc(p0, 1)
                    pool.wait_ge(p0, b + 1)
                    nc.gpsimd.tensor_tensor(rstd[:, now], rstd[:, now], mhalf[:, now], ALU.pow).then_inc(rstd0, 1)
                    pool.wait_ge(rstd0, b + 1)
                    nc.gpsimd.tensor_scalar(shift0[:, now], mv[:, now, 0], -1.0, None, ALU.mult).then_inc(shift_half, 1)
                    pool.wait_ge(shift_half, b + 1)
                    nc.gpsimd.tensor_tensor(shift0[:, now], shift0[:, now], rstd[:, now], ALU.mult).then_inc(shift_done, 1)
                pool.wait_ge(wo_got, 16)
                nc.gpsimd.tensor_scalar(wo_in0, wo_in0, WSCALE, None, ALU.mult).then_inc(wo_split, 1)
                pool.wait_ge(wo_split, 1)
                nc.gpsimd.tensor_copy(W_all[:, :, OSLOT, :], wo_in0).then_inc(wo_split, 1)
                pool.wait_ge(wo_split, 2)
                nc.gpsimd.tensor_tensor(W_all[:, :, OSLOT + 1, :], wo_in0, W_all[:, :, OSLOT, :], ALU.subtract
                                        ).then_inc(wo_split, 1)
                pool.wait_ge(wo_split, 3)

            @block.vector
            def _(dve):
                steps = Steps(dve, d0)
                steps.done(nc.vector.memset(pick_bias, 0.0))
                steps.now()
                for row in (0, 32):
                    steps.done(nc.vector.memset(pick_bias[row:row + 1, :], 1.0))
                for e in range(E):
                    nc.vector.memset(iota_e[:, e:e + 1], float(e))
                for b in range(B):
                    dve.wait_ge(x_in[b], 16)
                    norm_stats(dve, steps, lambda t: X[:, b * T + t, :], b).then_inc(mv0, 1)
                for b in range(B // 2):
                    dve.wait_ge(rstd0, b + 1)
                    for t in range(b * T, (b + 1) * T):
                        last = nc.vector.tensor_scalar(hs[:, t, :], X[:, t, :], mv[:, t, 0:1], rstd[:, t:t + 1],
                                                       ALU.subtract, ALU.mult)
                    last.then_inc(xn0, 1)
                dve.wait_ge(w_got, 48)
                dve.wait_ge(whi_done, 4)
                for t, slot in enumerate((QSLOT, KSLOT, VSLOT)):
                    nc.vector.scalar_tensor_tensor(
                        W_all[:, :, slot + 1, :], w_in[:, t, :].rearrange("p (n c) -> p n c", n=PAIRS), WSCALE,
                        W_all[:, :, slot, :], ALU.mult, ALU.subtract)
                steps.done(nc.vector.memset(W_all[:, :, VSLOT + 2, :], 0.0))
                steps.now()
                rows = vb_hi.rearrange("p (n c) -> p n c", n=PAIRS)
                nc.vector.tensor_copy(W_all[0:32, :, VSLOT + 2, :], rows[0:32]).then_inc(wlo_done, 1)
                nc.vector.scalar_tensor_tensor(
                    W_all[32:64, :, VSLOT + 2, :], vbias[32:64, :].rearrange("p (n c) -> p n c", n=PAIRS), WSCALE,
                    rows[32:64], ALU.mult, ALU.subtract).then_inc(wlo_done, 1)
                for b in range(B):
                    dve.wait_ge(xt_hi, b + 1)
                    nc.vector.tensor_tensor(xT_all[:, b, 1, :], bank(2 * b, 2), xT_all[:, b, 0, :],
                                            ALU.subtract).then_inc(xt_lo, 1)

            @block.tensor
            def _(pe):
                pe.wait_ge(consts, 1)
                for b in range(B):
                    if b < B // 2:
                        pe.wait_ge(xn0, b + 1)
                    else:
                        pe.wait_ge(xn_act, b - B // 2 + 1)
                    for t in range(T):
                        last = nc.tensor.transpose(bank(2 * b, 2)[:, t * P:(t + 1) * P], hs[:, b * T + t, :], ident[:, :])
                    last.then_inc(xt_ps, 1)
                pe.wait_ge(b_got, 64)
                pe.wait_ge(xt_lo, 1)
                for t in range(2):
                    last = nc.tensor.transpose(bank(0)[:, t * PAIRS:(t + 1) * PAIRS], bias_in[0:PAIRS, t, :],
                                               ident[0:PAIRS, 0:PAIRS])
                pe.wait_ge(small_in, 16 * SMALL)
                last = nc.tensor.transpose(bank(0)[:, 2 * PAIRS:2 * PAIRS + E * FC], b1_in[0:E * FC, :],
                                           ident[0:E * FC, 0:E * FC])
                last.then_inc(biasT_ps, 1)

        a1b = Arena(a1.at, ARENA)
        w_qk = a1b.take(4 * P // 2, F16).rearrange("p (j c) -> p j c", j=4)
        w_v = a1b.take(3 * P // 2, F16).rearrange("p (j c) -> p j c", j=3)
        w_o = a1b.take(2 * D // 2, F16).rearrange("p (j d) -> p j d", j=2)
        xT = a1b.take(S, F16).rearrange("p (h s) -> p h s", h=2)
        probs = [[a1b.take(w) for w in WIDTH] for _ in range(2)]
        q_hi = [[a1b.take(S // 2, F16) for _ in range(2)] for _ in range(2)]
        q_lo = [[a1b.take(S // 2, F16) for _ in range(2)] for _ in range(2)]
        k_hl = [[a1b.take(S // 2, F16) for _ in range(2)] for _ in range(2)]
        qk_f32 = [a1b.take(S) for _ in range(2)]
        qk_hi = [a1b.take(S // 2, F16) for _ in range(2)]
        qk_lo = [a1b.take(S // 2, F16) for _ in range(2)]
        sum_full = [a1b.take(S) for _ in range(2)]
        sum_hi = [a1b.take(HALF) for _ in range(2)]
        sum_lo = [a1b.take(HALF) for _ in range(2)]
        denT = a1b.take(S)
        rden_col = a1b.take(S // 32)
        ctx_hi, ctx_lo = a1b.take(S // 2, F16), a1b.take(S // 2, F16)
        tile = a1b.take(D)
        tile_st, tile_mv, tile_rstd = a1b.take(6), a1b.take(2), a1b.take(1)
        spare = hs[:, :, :].rearrange("p t d -> p (t d)")
        vals = [spare[:, m * S:(m + 1) * S].rearrange("p (t c) -> p t c", t=T) for m in range(2)]
        ctxT = spare[:, 2 * S:3 * S]
        rden = spare[:, 3 * S:4 * S]

        SC = [bank(0, 2), bank(2, 2)]
        PJ = bank(4, 2)
        OUT = [bank(6), bank(7)]

        wqk_in, wv_in, wo_in, xt_in = sem("wqk_in"), sem("wv_in"), sem("wo_in"), sem("xt_in")
        qk_done, tanh_done, lo_done = sem("qk_done"), sem("tanh_done"), sem("lo_done")
        head_in = [[sem(f"head_in{m}{s}") for s in range(2)] for m in range(2)]
        vproj_done, vals_ready = sem("vproj_done"), sem("vals_ready")
        scores_done, exp_done, masked, full_summed = (sem("scores_done"), sem("exp_done"), sem("masked"),
                                                      sem("full_summed"))
        pv_done, sums_done, den_done, den_read = sem("pv_done"), sem("sums_done"), sem("den_done"), sem("den_read")
        ctx_ready, wo_done, acc_added, d1 = sem("ctx_ready"), sem("wo_done"), sem("acc_added"), sem("d1")
        lo_summed, ctx_read = sem("lo_summed"), sem("ctx_read")
        tile_tanh, tile_stats, tile_pow, tile_normed, tile_added, tile_reset = (
            sem("tile_tanh"), sem("tile_stats"), sem("tile_pow"), sem("tile_normed"), sem("tile_added"), sem("tile_reset"))
        HEAD_DMAS = 6
        D1 = 15

        NORM_FROM = PAIRS + 2
        NORMED = N1 - NORM_FROM

        def each_pair(engine, pair):
            pair(0, 0, first=True)
            pair(1, 1)
            with engine.Fori(1, NORM_FROM // 2) as k:
                for par in range(2):
                    pair(2 * k + par, par)
            with engine.Fori(NORM_FROM // 2, N1 // 2 - 1) as k:
                for par in range(2):
                    pair(2 * k + par, par, norm=True)
            pair(N1 - 2, 0, norm=True)
            pair(N1 - 1, 1, last=True, norm=True)

        pow2, stats2, rstd2, hs_ready, d2 = sem("pow2"), sem("stats2"), sem("rstd2"), sem("hs_ready"), sem("d2")

        def batch(v, b):
            return v[:, b * T:(b + 1) * T, :]

        def moments(steps, src, dst, first, count):
            for t in range(first, first + count):
                steps.done(nc.vector.bn_stats(stats[:, t, :], src[:, t, :]))
            steps.now()
            for t in range(count):
                last = nc.vector.bn_aggr(dst[:, t, :], stats[:, first + t, :])
            return last

        def input_moments(steps, b):
            moments(steps, X, batch(mv, b), b * T, T).then_inc(stats2, 1)

        def input_deviation(pool, b):
            now = slice(b * T, (b + 1) * T)
            pool.wait_ge(stats2, b + 1)
            nc.gpsimd.tensor_scalar(rstd[:, now], mv[:, now, 1], EPS, None, ALU.add).then_inc(pow2, 1)
            pool.wait_ge(pow2, b + 1)
            nc.gpsimd.tensor_tensor(rstd[:, now], rstd[:, now], mhalf[:, now], ALU.pow).then_inc(rstd2, 1)

        def inputs(dve, b):
            dve.wait_ge(rstd2, b + 1)
            for t in range(b * T, (b + 1) * T):
                last = nc.vector.tensor_scalar(hs[:, t, :], X[:, t, :], mv[:, t, 0:1], rstd[:, t:t + 1],
                                               ALU.subtract, ALU.mult)
            last.then_inc(hs_ready, 1)

        def one_tile(v, t):
            return (v[:, t:t + 1, :] if isinstance(t, int) else v[:, bass.ds(t, 1), :]).rearrange("p a d -> p (a d)")

        with nc.Block() as block:
            @block.sync
            def _(sp):
                def load_inputs(n):
                    if not isinstance(n, int) or n > 0:
                        sp.wait_ge(qk_done, 2 * n)
                        if isinstance(n, int) and n == 1:
                            sp.wait_ge(vproj_done, 1)
                    at = bass.ds(n % PAIRS, 1)
                    sp.dma_start(xT, xT_all[:, bass.ds(n // PAIRS, 1), :, :].rearrange("p a h s -> p (a h) s")
                                 ).then_inc(xt_in, 16)
                    sp.dma_start(w_qk, W_all[:, at, 0:VSLOT, :].rearrange("p a j c -> p (a j) c")).then_inc(wqk_in, 16)
                    sp.dma_start(w_v, W_all[:, at, VSLOT:OSLOT, :].rearrange("p a j c -> p (a j) c")).then_inc(wv_in, 16)

                def heads(n, par):
                    if not isinstance(n, int) or n > 1:
                        sp.wait_ge(scores_done, 10 * (n - 1))
                    for j, dst in ((0, (q_hi[par], q_lo[par])), (1, (k_hl[par], k_hl[par]))):
                        for part, (src, ready) in enumerate(((qk_hi[j], tanh_done), (qk_lo[j], lo_done))):
                            sp.wait_ge(ready, (4 * n + 2 * j + 1) if part == 0 else (2 * n + j + 1))
                            for s in range(2):
                                rows = (0, 1) if j == 0 else (part,)
                                for r in rows:
                                    sp.dma_start(dst[part][s][r * DH:(r + 1) * DH, :], src[s * DH:(s + 1) * DH, :]
                                                 ).then_inc(head_in[par][s], 16)

                def load_o(n):
                    upto(sp, wo_done, n)
                    sp.dma_start(w_o, W_all[:, bass.ds(n % PAIRS, 1), OSLOT:, :].rearrange("p a j d -> p (a j) d")
                                 ).then_inc(wo_in, 16)

                def pair(i, par, first=False, last=False, norm=False):
                    if not first:
                        load_o(i - 1)
                    if not last:
                        heads(i + 1, 1 - par)
                        if not isinstance(i, int) or i < N1 - 2:
                            load_inputs(i + 2)

                load_inputs(0)
                heads(0, 0)
                load_inputs(1)
                each_pair(sp, pair)
                load_o(N1 - 1)

            @block.tensor
            def _(pe):
                def project(n, j):
                    if j == 0:
                        pe.wait_ge(wqk_in, 16 * (n + 1))
                        pe.wait_ge(xt_in, 16 * (n + 1))
                        if not isinstance(n, int) or n > 0:
                            pe.wait_ge(vals_ready, n + 1)
                    else:
                        pe.wait_ge(tanh_done, 4 * n + 2)
                    for half in range(2):
                        passes = ((0, 0), (0, 1), (1, 0))
                        for m, (w, x) in enumerate(passes):
                            last = nc.tensor.matmul(PJ[:, half * HALF:(half + 1) * HALF], w_qk[:, 2 * j + w, :],
                                                    xT[:, x, half * HALF:(half + 1) * HALF], start=(m == 0), stop=(m == 2))
                    last.then_inc(qk_done, 1)

                def values(n):
                    pe.wait_ge(wv_in, 16 * (n + 1))
                    pe.wait_ge(xt_in, 16 * (n + 1))
                    for t in range(T):
                        if t in (0, T // 2):
                            upto(pe, den_read, 2 * n - 3 + 2 * t // T)
                        tok = slice(t * P, (t + 1) * P)
                        o = PJ[:, tok]
                        nc.tensor.matmul(o, xT[:, 0, tok], w_v[:, 0, :], start=True, stop=False)
                        nc.tensor.matmul(o, xT[:, 0, tok], w_v[:, 1, :], start=False, stop=False)
                        nc.tensor.matmul(o, xT[:, 1, tok], w_v[:, 0, :], start=False, stop=False)
                        last = nc.tensor.matmul(o, pick_bias, w_v[:, 2, :], start=False, stop=True)
                    last.then_inc(vproj_done, 1)

                def scores(s, g, par):
                    for kt, q0, n, c in CAUSAL[g]:
                        k = k_hl[par][s][:, kt * P:(kt + 1) * P]
                        nc.tensor.matmul(SC[s][:, c:c + n], k, q_hi[par][s][:, q0:q0 + n], start=True, stop=False,
                                         skip_group_check=True)
                        last = nc.tensor.matmul(SC[s][:, c:c + n], k, q_lo[par][s][:, q0:q0 + n], start=False, stop=True,
                                                skip_group_check=True)
                    last.then_inc(scores_done, 1)

                def context(g, par):
                    for kt, q0, n, c in CAUSAL[g]:
                        half = q0 // HALF
                        first = g == half and kt == 0
                        for s in range(2):
                            last = nc.tensor.matmul(
                                OUT[half][s * DH:(s + 1) * DH, q0 - half * HALF:q0 - half * HALF + n],
                                vals[par][:, kt, s * DH:(s + 1) * DH], probs[s][g][:, c:c + n],
                                start=first, stop=(g == 4), skip_group_check=True)
                    last.then_inc(pv_done, 1)

                def denominators(n):
                    if isinstance(n, int) and n == 0:
                        pe.wait_ge(tanh_done, 4 * (n + 1) + 4)
                    else:
                        pe.wait_ge(acc_added, n)
                    pe.wait_ge(sums_done, n + 1)
                    for half, sums in enumerate((sum_lo, sum_hi)):
                        for s in range(2):
                            last = nc.tensor.matmul(PJ[s * DH:(s + 1) * DH, half * HALF:(half + 1) * HALF],
                                                    ones, sums[s], start=True, stop=True, skip_group_check=True)
                        last.then_inc(den_done, 1)

                def output(n):
                    pe.wait_ge(ctx_ready, n + 1)
                    pe.wait_ge(wo_in, 16 * (n + 1))
                    for t in range(T):
                        tok = slice(t * P, (t + 1) * P)
                        passes = ((ctx_hi, 0), (ctx_hi, 1), (ctx_lo, 0))
                        for m, (c, w) in enumerate(passes):
                            last = nc.tensor.matmul(PJ[:, tok], c[:, tok], w_o[:, w, :], start=(m == 0), stop=(m == 2))
                    last.then_inc(wo_done, 1)

                def begin(n, par):
                    for s in range(2):
                        pe.wait_ge(head_in[par][s], 16 * HEAD_DMAS * (n // 2 + 1))
                        upto(pe, exp_done, 10 * n - 1 + s)
                        scores(s, 0, par)

                def pair(i, par, first=False, last=False, norm=False):
                    def next_scores(s, g):
                        pe.wait_ge(exp_done, 10 * i + 2 * g - 1 + s)
                        scores(s, g, par)

                    next_scores(0, 1)
                    if not first:
                        denominators(i - 1)
                    next_scores(1, 1)
                    if not last:
                        values(i + 1)
                    next_scores(0, 2)
                    next_scores(1, 2)
                    if not last:
                        project(i + 1, 0)
                    pe.wait_ge(masked, 6 * i + 2)
                    upto(pe, ctx_read, 2 * i)
                    context(0, par)
                    next_scores(0, 3)
                    next_scores(1, 3)
                    if not last:
                        project(i + 1, 1)
                    context(1, par)
                    context(2, par)
                    if not first:
                        if last:
                            pe.wait_ge(den_read, 2 * i)
                        else:
                            pe.wait_ge(tanh_done, 4 * (i + 1) + 4)
                        output(i - 1)
                    next_scores(0, 4)
                    next_scores(1, 4)
                    pe.wait_ge(masked, 6 * i + 4)
                    context(3, par)
                    if not last:
                        begin(i + 1, 1 - par)
                    pe.wait_ge(masked, 6 * i + 6)
                    context(4, par)

                project(0, 0)
                project(0, 1)
                pe.wait_ge(tanh_done, 4)
                values(0)
                begin(0, 0)
                each_pair(pe, pair)
                denominators(N1 - 1)
                pe.wait_ge(den_read, 2 * N1)
                output(N1 - 1)

            @block.scalar
            def _(act):
                def tanh(n, j, par):
                    act.wait_ge(qk_done, 2 * n + j + 1)
                    for s in range(2):
                        wait_apart(act, head_in[1 - par][s], 16 * HEAD_DMAS * ((n + 1) // 2))
                    bias = qk_bias[:, j, bass.ds(n % PAIRS, 1)]
                    nc.scalar.activation(qk_hi[j], PJ, ACT.Tanh, scale=1.0 / WSCALE, bias=bias).then_inc(tanh_done, 1)
                    wait_apart(act, lo_done, 2 * (n - 1) + j + 1)
                    nc.scalar.activation(qk_f32[j], PJ, ACT.Tanh, scale=1.0 / WSCALE, bias=bias).then_inc(tanh_done, 1)

                def value_tanh(n, par):
                    act.wait_ge(vproj_done, n + 1)
                    if not isinstance(n, int) or n > 1:
                        act.wait_ge(pv_done, 5 * (n - 1))
                    nc.scalar.activation(vals[par], PJ.rearrange("p (t c) -> p t c", t=T), ACT.Tanh,
                                         scale=1.0 / WSCALE).then_inc(vals_ready, 1)

                def exp(i, s, g):
                    if s == 0 and (not isinstance(i, int) or i > 0):
                        act.wait_ge(pv_done, 5 * (i - 1) + g + 1)
                        if g == 0:
                            act.wait_ge(lo_summed, 2 * i)
                        elif g < 3:
                            act.wait_ge(full_summed, 2 * i)
                        else:
                            act.wait_ge(sums_done, i)
                    act.wait_ge(scores_done, 10 * i + 2 * g + s + 1)
                    nc.scalar.activation(probs[s][g], SC[s][:, 0:WIDTH[g]], ACT.Exp,
                                         scale=DH ** -0.5).then_inc(exp_done, 1)

                def pair(i, par, first=False, last=False, norm=False):
                    for g in range(2):
                        for s in range(2):
                            exp(i, s, g)
                    if not last:
                        value_tanh(i + 1, 1 - par)
                    exp(i, 0, 2)
                    exp(i, 1, 2)
                    if not last:
                        tanh(i + 1, 0, 1 - par)
                    exp(i, 0, 3)
                    exp(i, 1, 3)
                    if norm:
                        nc.scalar.activation(tile, one_tile(acc, i - NORM_FROM), ACT.Tanh, scale=1.0 / WSCALE
                                             ).then_inc(tile_tanh, 1)
                    if not last:
                        tanh(i + 1, 1, 1 - par)
                    for s in range(2):
                        exp(i, s, 4)

                tanh(0, 0, 0)
                tanh(0, 1, 0)
                value_tanh(0, 0)
                each_pair(act, pair)

            @block.gpsimd
            def _(pool):
                def keep_causal(v, blocks):
                    return nc.gpsimd.affine_select(out=v, in_=v, compare_op=ALU.is_ge, fill=0.0, base=0,
                                                   pattern=([[0, blocks]] if blocks > 1 else []) + [[1, P]], channel_multiplier=-1)

                def mask(i, s, g):
                    wait_apart(pool, exp_done, 10 * i + 2 * g + s + 1)
                    tiles = probs[s][g].rearrange("p (a c) -> p a c", a=2)[:, :, 0:P]
                    last = keep_causal(tiles, 2)
                    if g < 4:
                        last = keep_causal(probs[s][g][:, 7 * P:], 1)
                    last.then_inc(masked, 1)

                def inverse_deviation(t):
                    wait_apart(pool, tile_stats, 2 * t + 2)
                    nc.gpsimd.tensor_scalar(tile_rstd, tile_mv[:, 1:2], EPS, None, ALU.add).then_inc(tile_pow, 1)
                    pool.wait_ge(tile_pow, 2 * t + 1)
                    nc.gpsimd.tensor_tensor(tile_rstd, tile_rstd, mhalf[:, 0:1], ALU.pow).then_inc(tile_pow, 1)
                    nc.gpsimd.tensor_copy(one_tile(acc, t), ob_b[:, :]).then_inc(tile_reset, 1)

                def pair(i, par, first=False, last=False, norm=False):
                    for s in range(2):
                        mask(i, s, 0)
                    upto(pool, sums_done, i)
                    for s in range(2):
                        pool.wait_ge(exp_done, 10 * i + 5 + s)
                        nc.gpsimd.tensor_tensor(sum_full[s], probs[s][1], probs[s][2], ALU.add).then_inc(full_summed, 1)
                    for s in range(2):
                        mask(i, s, 3)
                    if norm:
                        inverse_deviation(i - NORM_FROM)
                    for s in range(2):
                        mask(i, s, 4)

                each_pair(pool, pair)
                input_deviation(pool, 0)
                input_deviation(pool, 1)
                pool.wait_ge(tile_reset, NORMED)

            @block.vector
            def _(dve):
                def low_part(n, j, par):
                    dve.wait_ge(tanh_done, 4 * n + 2 * j + 2)
                    for s in range(2):
                        upto(dve, head_in[1 - par][s], 16 * HEAD_DMAS * ((n + 1) // 2))
                    nc.vector.tensor_tensor(qk_lo[j], qk_f32[j], qk_hi[j], ALU.subtract).then_inc(lo_done, 1)

                def add_output(n):
                    dve.wait_ge(wo_done, n + 1)
                    upto(dve, acc_added, n)
                    if isinstance(n, int):
                        v = acc[:, (n // PAIRS) * T:(n // PAIRS + 1) * T, :]
                    else:
                        v = acc[:, bass.ds((n // PAIRS) * T, T), :]
                    nc.vector.tensor_tensor(v, PJ.rearrange("p (t c) -> p t c", t=T), v, ALU.add).then_inc(acc_added, 1)

                def normalise(n, steps):
                    for half in range(2):
                        dve.wait_ge(den_done, 2 * n + half + 1)
                        now = slice(half * HALF, (half + 1) * HALF)
                        nc.vector.transpose(denT[:, now], PJ[:, now]).then_inc(den_read, 1)
                    dve.wait_ge(den_read, 2 * n + 2)
                    steps.done(nc.vector.reciprocal(rden_col, denT.rearrange("p (b c) -> p b c", c=32)[:, :, 0]))
                    steps.now()
                    steps.done(nc.vector.transpose(rden.rearrange("p (b c) -> p b c", c=32),
                                                   rden_col.unsqueeze(2).to_broadcast([P, S // 32, 32])))
                    steps.now()
                    dve.wait_ge(pv_done, 5 * (n + 1))
                    upto(dve, wo_done, n)
                    for half in range(2):
                        now = slice(half * HALF, (half + 1) * HALF)
                        nc.vector.tensor_tensor(ctx_hi[:, now], OUT[half], rden[:, now], ALU.mult)
                        nc.vector.tensor_tensor(ctxT[:, now], OUT[half], rden[:, now], ALU.mult).then_inc(ctx_read, 1)
                    dve.wait_ge(ctx_read, 2 * n + 2)
                    nc.vector.tensor_tensor(ctx_lo, ctxT, ctx_hi, ALU.subtract).then_inc(ctx_ready, 1)

                def tile_moments(t):
                    wait_apart(dve, tile_tanh, t + 1)
                    nc.vector.bn_stats(tile_st, tile).then_inc(tile_stats, 1)
                    wait_apart(dve, tile_stats, 2 * t + 1)
                    nc.vector.bn_aggr(tile_mv, tile_st).then_inc(tile_stats, 1)

                def norm_tile(t):
                    wait_apart(dve, tile_pow, 2 * t + 2)
                    nc.vector.tensor_scalar(tile, tile, tile_mv[:, 0:1], tile_rstd, ALU.subtract, ALU.mult
                                            ).then_inc(tile_normed, 1)

                def add_tile(t):
                    dve.wait_ge(tile_normed, t + 1)
                    nc.vector.tensor_tensor(one_tile(X, t), tile, one_tile(X, t), ALU.add).then_inc(tile_added, 1)

                def pair(i, par, first=False, last=False, norm=False):
                    steps = Steps(dve, d1, D1, i)
                    if not first:
                        steps.base = steps.base - 2
                        normalise(i - 1, steps)
                    n0 = steps.n
                    for s in range(2):
                        dve.wait_ge(masked, 6 * i + 1 + s)
                        nc.vector.tensor_copy(sum_lo[s][:, 0:P], probs[s][0][:, 0:P])
                        steps.done(nc.vector.tensor_tensor(sum_lo[s][:, P:], probs[s][0][:, HALF:HALF + 3 * P],
                                                           probs[s][0][:, P:HALF], ALU.add))
                    for s in range(2):
                        steps.now(n0 + 1 + s)
                        v = sum_lo[s][:, 3 * P:]
                        nc.vector.tensor_tensor(v, v, probs[s][0][:, 7 * P:], ALU.add).then_inc(lo_summed, 1)
                    if not last:
                        low_part(i + 1, 0, 1 - par)
                    else:
                        dve.wait_ge(tile_added, 2 * T)
                        input_moments(ahead, 0)
                    for s in range(2):
                        dve.wait_ge(full_summed, 2 * i + 1 + s)
                        steps.done(nc.vector.tensor_tensor(sum_hi[s], sum_full[s][:, 0:HALF], sum_full[s][:, HALF:],
                                                           ALU.add))
                    if not last:
                        low_part(i + 1, 1, 1 - par)
                    else:
                        input_moments(ahead, 1)
                    if norm:
                        tile_moments(i - NORM_FROM)
                    for m, (q, c, n) in enumerate(((0, 0, 4 * P), (P, 4 * P, 3 * P), (3 * P, 7 * P, P))):
                        for s in range(2):
                            if m == 0:
                                dve.wait_ge(masked, 6 * i + 3 + s)
                            steps.now(n0 + 3 + 2 * m + s)
                            v = sum_hi[s][:, q:q + n]
                            steps.done(nc.vector.tensor_tensor(v, v, probs[s][3][:, c:c + n], ALU.add))
                    if not first:
                        add_output(i - 1)
                    if norm:
                        norm_tile(i - NORM_FROM)
                    for s in range(2):
                        dve.wait_ge(masked, 6 * i + 5 + s)
                        v = sum_lo[s][:, 2 * P:]
                        dve.wait_ge(lo_summed, 2 * i + 1 + s)
                        steps.done(nc.vector.tensor_tensor(v, v, probs[s][4][:, 0:2 * P], ALU.add))
                    if norm:
                        add_tile(i - NORM_FROM)
                    for s in range(2):
                        v = sum_hi[s][:, 2 * P:]
                        steps.now(n0 + 9 + s)
                        ins = nc.vector.tensor_tensor(v, v, probs[s][4][:, 2 * P:], ALU.add)
                        if s == 0:
                            steps.done(ins)
                        else:
                            ins.then_inc(sums_done, 1)
                    assert steps.n == D1 - 2 * first, steps.n

                ahead = Steps(dve, d2)
                low_part(0, 0, 0)
                low_part(0, 1, 0)
                each_pair(dve, pair)
                steps = Steps(dve, d1, D1, N1)
                steps.base -= 2
                normalise(N1 - 1, steps)
                inputs(dve, 0)
                inputs(dve, 1)
                add_output(N1 - 1)

        top = Arena(ARENA - TOP, ARENA)
        experts_in = top.take(E * F).rearrange("p (e f) -> p e f", e=E)
        w1_parts, w2_parts = (top.take(E * F, F16).rearrange("p (e h f) -> p e h f", e=E, h=2) for _ in range(2))
        experts_got, w_split = sem("experts_got"), sem("w_split")
        a2 = Arena()
        lat_vals = a2.take(NT * LAT).rearrange("p (t c) -> p t c", t=NT)
        q_rows = [a2.take(GH * S // 2, BF16).rearrange("p (j t) -> p j t", j=GH) for _ in range(2)]
        k_rows = [a2.take(GH * S // 2, BF16).rearrange("p (j t) -> p j t", j=GH) for _ in range(2)]
        kpm_rows = [a2.take(GH * S // 2, BF16).rearrange("p (j t) -> p j t", j=GH) for _ in range(2)]
        v_cols = [a2.take(T * GH * 32).rearrange("p (t j c) -> p t j c", t=T, j=GH) for _ in range(2)]
        ow_rows = [a2.take(D) for _ in range(2)]
        out_norm = a2.take(HALF)
        head_rows = a2.take(GH)
        scratch = a2.at
        hsT = [a2.take(S) for _ in range(2)]
        qk = [a2.take(S) for _ in range(2)]
        qk_rest = a2.take(S)
        qk_part = [[a2.take(S // 2, BF16) for _ in range(PARTS)] for _ in range(2)]
        kpm = a2.take(S)
        kpm_rest = a2.take(S)
        LEFT = NT - NORMED
        left_mv = a2.take(LEFT * 2).rearrange("p (t c) -> p t c", t=LEFT)
        left_rstd = a2.take(LEFT)
        kpm_part = [[a2.take(S // 2, BF16) for _ in range(PARTS)] for _ in range(2)]

        left_tanh, left_stats, left_pow, left_normed, left_added = (
            sem("left_tanh"), sem("left_stats"), sem("left_pow"), sem("left_normed"), sem("left_added"))
        hsT_ps, hsT_ready, qk_ps, lv_ps = sem("hsT_ps"), sem("hsT_ready"), sem("qk_ps"), sem("lv_ps")
        qk_ready, rest_ready, lv_ready = sem("qk_ready"), sem("rest_ready"), sem("lv_ready")
        part_ready = [sem(f"part_ready{c}") for c in range(PARTS)]
        kpm_ready, kpm_rest_ready = sem("kpm_ready"), sem("kpm_rest_ready")
        kpm_part_ready = [sem(f"kpm_part_ready{c}") for c in range(PARTS)]
        parts_out = [sem(f"parts_out{m}") for m in range(2)]
        BATCH_DMAS = 3 * PARTS
        act_cleared, dve_cleared, heads_set = sem("act_cleared"), sem("dve_cleared"), sem("heads_set")
        keys_pick, v_cleared = sem("keys_pick"), sem("v_cleared")
        acc_set = sem("acc_set")

        def wide(row, count=T):
            return row.unsqueeze(1).to_broadcast([P, count, row.shape[-1]])

        def words(v):
            return v.rearrange("p j t -> p (j t)").bitcast(F32)

        a3 = Arena(scratch)
        e_probs = [a3.take(GH * HALF).rearrange("p (j t) -> p j t", j=GH) for _ in range(2)]
        tops = a2.take(T * GH)
        top_rest = a2.take(T * GH)
        top_parts = a2.take(T * PARTS * GH // 2, BF16).rearrange("p (t c j) -> p t c j", t=T, c=PARTS)
        gap = a2.take(HALF)
        outT = a2.take(HALF)
        out_rden = a2.take(HALF // 32)
        aoT = a2.take(HALF)

        MX = [bank(0, 2), bank(2, 2)]
        TS = [bank(4), bank(5), bank(6)]
        OT = bank(7)
        FIRST_MX = (*MX, bank(4, 2))
        LAST_BATCH_AT = 9
        PROJECT1, TURN1, PROJECT0, TURN0 = 3, 6, 11, 14
        EXTRAS = (PROJECT1, TURN1, PROJECT0, TURN0)

        def slots(u):
            x = sum(e < u for e in EXTRAS)
            return MX[x % 2], MX[(x + 1) % 2], MX[(x + 1 + (u in EXTRAS)) % 2]

        TOPT, PO = slots(TURN1)[1][:, 0:HALF], slots(PROJECT1)[1][:, 0:HALF]

        d3s, gap_ready, tops_ready = sem("d3s"), sem("gap_ready"), sem("tops_ready")
        qk_in = [sem(f"qk_in{m}") for m in range(2)]
        ow_in = [sem(f"ow_in{m}") for m in range(2)]
        q_clear, v_ready, t_done, e_done, lpv_done = (sem("q_clear"), sem("v_ready"), sem("t_done"), sem("e_done"),
                                                      sem("lpv_done"))
        mx_done, top_done, parts_ready, topT_done, topT_read = (sem("mx_done"), sem("top_done"), sem("parts_ready"),
                                                                sem("topT_done"), sem("topT_read"))
        out_read, ao_ready, proj3_done, proj3_added, d3 = (sem("out_read"), sem("ao_ready"), sem("proj3_done"),
                                                           sem("proj3_added"), sem("d3"))
        STEPS3 = 2 * T
        QK_DMAS = PARTS + 2
        UNITS = T * GH
        D3 = 10
        AHEAD = 24

        def unit(n, u):
            m = AHEAD + 2 * u
            return n + m // UNITS, m % UNITS

        def batch_tiles(v, n, first, count):
            if isinstance(n, int):
                at = (n // GROUPS) * T + first
                return v[:, at:at + count, :]
            return v[:, bass.ds((n // GROUPS) * T + first, count), :]

        with nc.Block() as block:
            @block.vector
            def _(dve):
                steps = Steps(dve, d2)

                def latent(b):
                    dve.wait_ge(lv_ps, b + 1)
                    nc.vector.tensor_tensor(batch(lat_vals, b), bank(6 + b % 2).rearrange("p (t c) -> p t c", t=T),
                                            wide(vb_b[:, :]), ALU.add).then_inc(lv_ready, 1)
                    dve.wait_ge(part_ready[0], b + 1)
                    if b > 0:
                        dve.wait_ge(part_ready[2], b)
                    nc.vector.tensor_tensor(qk_rest, qk[b % 2], qk_part[b % 2][0], ALU.subtract).then_inc(rest_ready, 1)

                def last_part(b):
                    dve.wait_ge(part_ready[1], b + 1)
                    if b >= 2:
                        dve.wait_ge(parts_out[b % 2], 16 * BATCH_DMAS * (b // 2))
                    nc.vector.tensor_tensor(qk_part[b % 2][2], qk_rest, qk_part[b % 2][1], ALU.subtract
                                            ).then_inc(part_ready[2], 1)

                steps.base = 2 * T
                dve.wait_ge(left_tanh, 1)
                moments(steps, acc, left_mv, NORMED, LEFT).then_inc(left_stats, 1)
                nc.vector.tensor_tensor(head_rows, ident[:, MAXROW:MAXROW + GH], ident[:, MAXROW + GH:MAXROW + 2 * GH],
                                        ALU.add).then_inc(heads_set, 1)
                dve.wait_ge(heads_set, 1)
                nc.vector.tensor_tensor(head_rows, head_rows, ident[:, MAXROW + 2 * GH:MAXROW + 3 * GH],
                                        ALU.add).then_inc(heads_set, 1)
                dve.wait_ge(left_pow, 2)
                for t in range(LEFT):
                    last = nc.vector.tensor_scalar(acc[:, NORMED + t, :], acc[:, NORMED + t, :], left_mv[:, t, 0:1],
                                                   left_rstd[:, t:t + 1], ALU.subtract, ALU.mult)
                last.then_inc(left_normed, 1)
                dve.wait_ge(left_normed, 1)
                left = slice(NORMED, NT)
                nc.vector.tensor_tensor(X[:, left, :], X[:, left, :], acc[:, left, :], ALU.add).then_inc(left_added, 1)
                dve.wait_ge(left_added, 1)
                input_moments(steps, 2)
                input_moments(steps, 3)
                latent(0)
                inputs(dve, 2)
                inputs(dve, 3)

                def clear(v):
                    nc.vector.memset(v, 0.0).then_inc(dve_cleared, 1)

                def pick_heads(m):
                    nc.vector.tensor_copy(k_rows[m][MAXROW:MAXROW + PARTS * GH, :, :],
                                          head_rows[MAXROW:MAXROW + PARTS * GH, :].unsqueeze(2).to_broadcast([PARTS * GH, GH, S])
                                          ).then_inc(keys_pick, 1)

                dve.wait_ge(heads_set, 2)
                dve.wait_ge(act_cleared, 1)
                pick_heads(0)
                last_part(0)
                for v in (*ow_rows, out_norm):
                    clear(v)
                latent(1)
                clear(words(k_rows[1]))
                last_part(1)
                clear(words(q_rows[1]))
                latent(2)
                clear(words(kpm_rows[1]))
                dve.wait_ge(dve_cleared, 4)
                pick_heads(1)
                last_part(2)
                latent(3)

                def maxima(n, m, slot):
                    if m in (0, UNITS // 2):
                        if not isinstance(n, int) or n > 0:
                            dve.wait_ge(parts_ready, 2 * n - 1 + (m > 0))
                    if m % 2 == 1:
                        wait_apart(dve, gap_ready, (UNITS * n + m + 1) // 2)
                        nc.vector.tensor_tensor_reduce(
                            out=gap, in0=slot[:, 0:HALF], in1=gap, scale=0.5, scalar=LOWEST, op0=ALU.add, op1=ALU.max,
                            accum_out=tops[:, m:m + 1]).then_inc(top_done, 1)
                    else:
                        dve.wait_ge(mx_done, UNITS * n + m + 1)
                        nc.vector.tensor_reduce(tops[:, m:m + 1], slot, AX.X, ALU.max).then_inc(top_done, 1)

                def half_tops(v, h):
                    return v[:, 16 * h:16 * h + 16].rearrange("p (t j) -> p t j", j=GH)

                def half_part(c, h):
                    return top_parts[:, 4 * h:4 * h + 4, c, :]

                def top_part0(n, h, steps):
                    dve.wait_ge(top_done, UNITS * n + 16 * (h + 1))
                    if not isinstance(n, int) or n > 0:
                        dve.wait_ge(topT_done, 2 * n - 1 + h)
                    steps.done(nc.vector.tensor_scalar(half_part(0, h), half_tops(tops, h), -1.0, None, ALU.mult))

                def top_left(h, steps):
                    steps.now()
                    steps.done(nc.vector.scalar_tensor_tensor(half_tops(top_rest, h), half_tops(tops, h), -1.0,
                                                              half_part(0, h), ALU.mult, ALU.subtract))

                def top_part1(h, steps):
                    steps.now()
                    steps.done(nc.vector.tensor_copy(half_part(1, h), half_tops(top_rest, h)))

                def top_part2(h, steps):
                    steps.now()
                    nc.vector.tensor_tensor(half_part(2, h), half_tops(top_rest, h), half_part(1, h), ALU.subtract
                                            ).then_inc(parts_ready, 1)

                def spread_tops(n, par, h):
                    dve.wait_ge(topT_read, 2 * n + h + 1)
                    rows = q_rows[par][MAXROW:MAXROW + PARTS * GH, :, h * HALF:(h + 1) * HALF]
                    nc.vector.tensor_copy(rows[:, 1:, :], rows[:, 0:1, :].to_broadcast([PARTS * GH, GH - 1, HALF])
                                          ).then_inc(tops_ready, 1)

                def read_outputs(n, h):
                    dve.wait_ge(lpv_done, STEPS3 * n + T * (h + 1))
                    nc.vector.transpose(outT, OT).then_inc(out_read, 1)

                def invert(n, h, steps):
                    dve.wait_ge(out_read, 2 * n + h + 1)
                    steps.done(nc.vector.reciprocal(out_rden, outT.rearrange("p (b r) -> p b r", r=32)[:, :, KD]))

                def normalise(n, h, steps):
                    steps.now()
                    if not isinstance(n, int) or n > 0 or h > 0:
                        dve.wait_ge(proj3_done, 2 * n + h)
                    steps.done(nc.vector.tensor_tensor(
                        out_norm.rearrange("p (b r) -> p b r", r=32)[:, :, 0:KD],
                        outT.rearrange("p (b r) -> p b r", r=32)[:, :, 0:KD],
                        out_rden.unsqueeze(2).to_broadcast([P, HALF // 32, KD]), ALU.mult))

                def turn_outputs(steps):
                    steps.now()
                    nc.vector.transpose(aoT, out_norm).then_inc(ao_ready, 1)

                def add(n, h):
                    dve.wait_ge(proj3_done, 2 * n + h + 1)
                    upto(dve, proj3_added, 2 * n + h)
                    v = batch_tiles(acc, n, 4 * h, 4)
                    nc.vector.tensor_tensor(v, PO.rearrange("p (t c) -> p t c", t=4), v, ALU.add).then_inc(proj3_added, 1)

                def group(n, par, first=False, last=False):
                    steps = Steps(dve, d3, D3, n)
                    if not first:
                        steps.base = steps.base - 2
                    for u in range(STEPS3):
                        g, m = unit(0, u)
                        units = not (last and g)
                        if u == TURN1 + 1:
                            spread_tops(n, par, 1)
                        if u == TURN0 + 1 and not last:
                            spread_tops(n + 1, 1 - par, 0)
                        if units:
                            maxima(n + g, m, slots(u)[0])
                        if u == TURN1 - 2:
                            top_part0(n, 1, steps)
                        if u == TURN1 - 1:
                            top_part1(1, steps)
                        if u == TURN0 - 2 and not last:
                            top_part0(n + 1, 0, steps)
                        if u == TURN0 - 1 and not last:
                            top_part1(0, steps)
                        if u == 0 and not first:
                            read_outputs(n - 1, 1)
                        if u == 1 and not first:
                            normalise(n - 1, 1, steps)
                        if u == PROJECT1 and not first:
                            add(n - 1, 1)
                        if u == T:
                            read_outputs(n, 0)
                        if u == T + 1:
                            normalise(n, 0, steps)
                        if u == PROJECT0:
                            add(n, 0)
                        if units:
                            maxima(n + g, m + 1, slots(u)[2])
                        if u == TURN1 - 2:
                            top_left(1, steps)
                        if u == TURN1 - 1:
                            top_part2(1, steps)
                        if u == TURN0 - 2 and not last:
                            top_left(0, steps)
                        if u == TURN0 - 1 and not last:
                            top_part2(0, steps)
                        if u == 0 and not first:
                            invert(n - 1, 1, steps)
                        if u == 1 and not first:
                            turn_outputs(steps)
                        if u == T:
                            invert(n, 0, steps)
                        if u == T + 1:
                            turn_outputs(steps)
                    assert steps.n == D3 - 2 * first - 3 * last, steps.n

                dve.wait_ge(dve_cleared, 6)
                start = Steps(dve, d3s)
                for m in range(AHEAD):
                    maxima(0, m, FIRST_MX[m % 3])
                    if m == LAST_BATCH_AT + 2:
                        last_part(B - 1)
                    if m == UNITS // 2 - 1:
                        top_part0(0, 0, start)
                        top_left(0, start)
                        top_part1(0, start)
                        top_part2(0, start)
                spread_tops(0, 0, 0)
                dve.wait_ge(acc_set, 1)
                group(0, 0, first=True)
                group(1, 1)
                with dve.Fori(1, N2 // 2 - 1) as k:
                    for par in range(2):
                        group(2 * k + par, par)
                group(N2 - 2, 0)
                group(N2 - 1, 1, last=True)
                read_outputs(N2 - 1, 1)
                end = Steps(dve, d3s, 3, 1)
                invert(N2 - 1, 1, end)
                normalise(N2 - 1, 1, end)
                turn_outputs(end)
                add(N2 - 1, 1)

            @block.gpsimd
            def _(pool):
                def keys(b):
                    pool.wait_ge(qk_ready, b + 1)
                    if b > 0:
                        pool.wait_ge(kpm_rest_ready, b)
                    k = qk[b % 2]
                    nc.gpsimd.tensor_tensor(kpm[:, 0:HALF], k[:, 0:HALF], k[:, HALF:], ALU.add)
                    nc.gpsimd.tensor_tensor(kpm[:, HALF:], k[:, 0:HALF], k[:, HALF:], ALU.subtract).then_inc(kpm_ready, 1)
                    pool.wait_ge(kpm_part_ready[0], b + 1)
                    if b > 0:
                        pool.wait_ge(kpm_part_ready[2], b)
                    nc.gpsimd.tensor_tensor(kpm_rest, kpm, kpm_part[b % 2][0], ALU.subtract).then_inc(kpm_rest_ready, 1)

                def last_part(b):
                    pool.wait_ge(kpm_part_ready[1], b + 1)
                    if b >= 2:
                        pool.wait_ge(parts_out[b % 2], 16 * BATCH_DMAS * (b // 2))
                    nc.gpsimd.tensor_tensor(kpm_part[b % 2][2], kpm_rest, kpm_part[b % 2][1], ALU.subtract
                                            ).then_inc(kpm_part_ready[2], 1)

                for v in v_cols:
                    nc.gpsimd.memset(v.rearrange("p t j c -> p (t j c)"), 0.0).then_inc(v_cleared, 1)
                pool.wait_ge(left_stats, 1)
                nc.gpsimd.tensor_scalar(left_rstd, left_mv[:, :, 1], EPS, None, ALU.add).then_inc(left_pow, 1)
                pool.wait_ge(left_pow, 1)
                nc.gpsimd.tensor_tensor(left_rstd, left_rstd, mhalf[:, 0:LEFT], ALU.pow).then_inc(left_pow, 1)
                keys(0)
                input_deviation(pool, 2)
                input_deviation(pool, 3)
                last_part(0)
                pool.wait_ge(v_cleared, 2)
                for v in v_cols:
                    nc.gpsimd.memset(v[:, :, :, KD:KD + 1], 1.0).then_inc(v_cleared, 1)
                keys(1)
                last_part(1)
                for b in range(2, B):
                    keys(b)
                    last_part(b)
                pool.wait_ge(left_added, 1)
                nc.gpsimd.tensor_copy(acc[:, NORMED:, :], wide(ob_b[:, :], LEFT)).then_inc(acc_set, 1)
                pool.wait_ge(v_cleared, 4)
                pool.wait_ge(acc_set, 1)

                def take_values(n, par):
                    at = (n % GROUPS) * GH * KD
                    v = batch_tiles(lat_vals, n, 0, T)
                    v = v[:, :, at:at + GH * KD] if isinstance(n, int) else v[:, :, bass.ds(at, GH * KD)]
                    nc.gpsimd.tensor_copy(v_cols[par][:, :, :, 0:KD], v.rearrange("p t (j d) -> p t j d", d=KD)
                                          ).then_inc(v_ready, 1)

                def turn(n, par):
                    pool.wait_ge(v_ready, n)
                    wait_apart(pool, t_done, 64 * (n - 1))
                    nc.gpsimd.memset(q_rows[par][MAXROW:MAXROW + PARTS * GH, :, :].rearrange("p j t -> p (j t)").bitcast(F32),
                                     0.0).then_inc(q_clear, 1)
                    pool.wait_ge(q_clear, n - 1)
                    pool.wait_ge(lpv_done, STEPS3 * (n - 1))
                    take_values(n, par)

                pool.wait_ge(lv_ready, 1)
                for n in range(2):
                    take_values(n, n)
                for k, parts in enumerate((w1_parts, w2_parts)):
                    pool.wait_ge(experts_got, 16 * (k + 1))
                    nc.gpsimd.tensor_scalar(experts_in, experts_in, WSCALE, None, ALU.mult).then_inc(w_split, 1)
                    pool.wait_ge(w_split, 3 * k + 1)
                    nc.gpsimd.tensor_copy(parts[:, :, 0, :], experts_in).then_inc(w_split, 1)
                    pool.wait_ge(w_split, 3 * k + 2)
                    nc.gpsimd.tensor_tensor(parts[:, :, 1, :], experts_in, parts[:, :, 0, :], ALU.subtract
                                            ).then_inc(w_split, 1)
                    pool.wait_ge(w_split, 3 * k + 3)
                pool.wait_ge(lv_ready, B)
                with pool.Fori(1, N2 // 2) as k:
                    for par in range(2):
                        turn(2 * k + par, par)

            @block.scalar
            def _(act):
                left = acc[:, NORMED:, :]
                nc.scalar.activation(left, left, ACT.Tanh, scale=1.0 / WSCALE).then_inc(left_tanh, 1)

                def turned(b):
                    act.wait_ge(hsT_ps, b + 1)
                    if b >= 2:
                        act.wait_ge(lv_ps, b - 1)
                    nc.scalar.copy(hsT[b % 2], bank(2 * (b % 2), 2)).then_inc(hsT_ready, 1)

                def queries_keys(b):
                    m = b % 2
                    act.wait_ge(qk_ps, b + 1)
                    if b >= 2:
                        act.wait_ge(rest_ready, b - 1)
                        act.wait_ge(kpm_ready, b - 1)
                        act.wait_ge(parts_out[m], 16 * BATCH_DMAS * (b // 2))
                    nc.scalar.activation(qk[m], bank(4, 2), ACT.Identity, bias=b_lat[:, 0:1]).then_inc(qk_ready, 1)
                    nc.scalar.activation(qk_part[m][0], bank(4, 2), ACT.Identity, bias=b_lat[:, 0:1]
                                         ).then_inc(part_ready[0], 1)

                def parts(b):
                    m = b % 2
                    act.wait_ge(kpm_ready, b + 1)
                    nc.scalar.copy(kpm_part[m][0], kpm).then_inc(kpm_part_ready[0], 1)
                    act.wait_ge(rest_ready, b + 1)
                    nc.scalar.copy(qk_part[m][1], qk_rest).then_inc(part_ready[1], 1)

                def last_kpm_part(b):
                    act.wait_ge(kpm_rest_ready, b + 1)
                    nc.scalar.copy(kpm_part[b % 2][1], kpm_rest).then_inc(kpm_part_ready[1], 1)

                turned(0)
                for v in (k_rows[0], q_rows[0], kpm_rows[0]):
                    v = words(v)
                    nc.scalar.activation(v, ident[:, 0:1].to_broadcast([P, v.shape[1]]), ACT.Copy, scale=0.0
                                         ).then_inc(act_cleared, 1)
                queries_keys(0)
                turned(1)
                parts(0)
                queries_keys(1)
                last_kpm_part(0)
                turned(2)
                parts(1)
                last_kpm_part(1)
                queries_keys(2)
                turned(3)
                parts(2)
                queries_keys(3)
                last_kpm_part(2)

                def difference_sizes(n, m, slot):
                    act.wait_ge(mx_done, UNITS * n + m + 1)
                    nc.scalar.activation(gap, slot[:, HALF:], ACT.Abs).then_inc(gap_ready, 1)

                def exp(n, u, j):
                    act.wait_ge(t_done, 64 * n + 4 * u + j + 1)
                    if j == 0:
                        if not isinstance(n, int) or n > 0 or u >= 2:
                            act.wait_ge(lpv_done, STEPS3 * n + u - 1)
                    nc.scalar.activation(e_probs[u % 2][:, j, :], TS[(GH * u + j) % 3], ACT.Exp, scale=KD ** -0.5
                                         ).then_inc(e_done, 1)

                def top_rows_out(n, par, h):
                    act.wait_ge(topT_done, 2 * n + h + 1)
                    nc.scalar.copy(q_rows[par][MAXROW:MAXROW + PARTS * GH, 0, h * HALF:(h + 1) * HALF],
                                   TOPT.bitcast(BF16)[MAXROW:MAXROW + PARTS * GH, 0:HALF]).then_inc(topT_read, 1)

                def group(n, par, last=False):
                    for u in range(STEPS3):
                        for j in range(3):
                            exp(n, u, j)
                        if u == TURN1:
                            top_rows_out(n, par, 1)
                        if u == TURN0 and not last:
                            top_rows_out(n + 1, 1 - par, 0)
                        exp(n, u, 3)
                        g, m = unit(0, u)
                        if not (last and g):
                            difference_sizes(n + g, m + 1, slots(u)[2])

                for m in range(1, AHEAD, 2):
                    if m > 1:
                        act.wait_ge(top_done, m - 1)
                    difference_sizes(0, m, FIRST_MX[m % 3])
                    if m == LAST_BATCH_AT:
                        parts(B - 1)
                        last_kpm_part(B - 1)
                top_rows_out(0, 0, 0)
                group(0, 0)
                group(1, 1)
                with act.Fori(1, N2 // 2 - 1) as k:
                    for par in range(2):
                        group(2 * k + par, par)
                group(N2 - 2, 0)
                group(N2 - 1, 1, last=True)

            @block.tensor
            def _(pe):
                def turn(b):
                    pe.wait_ge(hs_ready, b + 1)
                    for t in range(T):
                        last = nc.tensor.transpose(bank(2 * (b % 2), 2)[:, t * P:(t + 1) * P], hs[:, b * T + t, :], ident[:, :])
                    last.then_inc(hsT_ps, 1)

                def queries_keys(b):
                    pe.wait_ge(hsT_ready, b + 1)
                    if b > 0:
                        pe.wait_ge(part_ready[0], b)
                    for half in range(2):
                        last = nc.tensor.matmul(bank(4 + half), w_lat[:, :], hsT[b % 2][:, half * HALF:(half + 1) * HALF],
                                                start=True, stop=True)
                    last.then_inc(qk_ps, 1)

                def latent_values(b):
                    if b >= 2:
                        pe.wait_ge(lv_ready, b - 1)
                    for t in range(T):
                        last = nc.tensor.matmul(bank(6 + b % 2)[:, t * LAT:(t + 1) * LAT], hsT[b % 2][:, t * P:(t + 1) * P],
                                                w_lv[:, :], start=True, stop=True, skip_group_check=True)
                    last.then_inc(lv_ps, 1)

                turn(0)
                for b in range(B):
                    queries_keys(b)
                    if b < B - 1:
                        turn(b + 1)
                    latent_values(b)

                def scores(n, par, u, j):
                    half, kt, at = u // T, u % T, GH * u + j
                    upto(pe, e_done, 64 * n + (at - 2 if at >= 3 else (0, -2, -1)[at]))
                    nc.tensor.matmul(TS[at % 3], k_rows[par][:, j, kt * P:(kt + 1) * P],
                                     q_rows[par][:, j, half * HALF:(half + 1) * HALF],
                                     start=True, stop=True).then_inc(t_done, 1)

                def values(n, par, u):
                    half, kt = u // T, u % T
                    pe.wait_ge(e_done, 64 * n + 4 * u + 4)
                    if kt == 0:
                        upto(pe, out_read, 2 * n + half)
                        if half == 0:
                            pe.wait_ge(v_ready, n + 1)
                    for j in range(GH):
                        last = nc.tensor.matmul(OT[32 * j:32 * (j + 1), :], v_cols[par][:, kt, j, :], e_probs[u % 2][:, j, :],
                                                start=(kt == 0), stop=(kt == T - 1), skip_group_check=True)
                    last.then_inc(lpv_done, 1)

                def maxima(par, m, slot):
                    qt, j = m // GH, m % GH
                    k = kpm_rows[par] if m % 2 else k_rows[par]
                    for h in range(2):
                        last = nc.tensor.matmul(slot[:, h * HALF:(h + 1) * HALF], q_rows[par][:, j, qt * P:(qt + 1) * P],
                                                k[:, j, h * HALF:(h + 1) * HALF], start=True, stop=True)
                    last.then_inc(mx_done, 1)

                def turn_tops(n, h):
                    pe.wait_ge(parts_ready, 2 * n + h + 1)
                    for t in range(4):
                        last = nc.tensor.transpose(TOPT.bitcast(BF16)[MAXROW:MAXROW + PARTS * GH, t * P:(t + 1) * P],
                                                   top_parts[:, 4 * h + t, :, :].rearrange("p c j -> p (c j)"), identb[:, :])
                    last.then_inc(topT_done, 1)

                def project(n, par, h):
                    pe.wait_ge(ao_ready, 2 * n + h + 1)
                    if h == 0:
                        pe.wait_ge(ow_in[par], 64 * (n // 2 + 1))
                    for t in range(4):
                        last = nc.tensor.matmul(PO[:, t * P:(t + 1) * P], aoT[:, t * P:(t + 1) * P], ow_rows[par],
                                                start=True, stop=True, skip_group_check=True)
                    last.then_inc(proj3_done, 1)

                def group(n, par, first=False, last=False):
                    for u in range(STEPS3):
                        if u % T == 0:
                            pe.wait_ge(tops_ready, 2 * n + u // T + 1)
                        g, m = unit(0, u)
                        units = not (last and g)
                        before = UNITS * n + AHEAD + 2 * u
                        if g and m == 0 and not last:
                            pe.wait_ge(qk_in[1 - par], 16 * QK_DMAS * ((n + 1) // 2 + 1))
                            if not first:
                                pe.wait_ge(q_clear, n)
                        for j in range(3):
                            scores(n, par, u, j)
                        def products():
                            if u > 0:
                                values(n, par, u - 1)
                            elif not first:
                                values(n - 1, 1 - par, STEPS3 - 1)

                        if u - 1 in EXTRAS:
                            products()
                        if u == PROJECT1 + 1 and not first:
                            pe.wait_ge(proj3_added, 2 * n)
                        elif u == TURN1 + 1:
                            pe.wait_ge(topT_read, 2 * n + 2)
                        elif u == PROJECT0 + 1:
                            pe.wait_ge(proj3_added, 2 * n + 1)
                        elif u == TURN0 + 1 and not last:
                            pe.wait_ge(topT_read, 2 * n + 3)
                        elif units:
                            pe.wait_ge(top_done, before - 1)
                        if units:
                            maxima((par + g) % 2, m, slots(u)[0])
                        if u - 1 not in EXTRAS:
                            products()
                        if units and u in EXTRAS:
                            pe.wait_ge(top_done, before)
                        if u == PROJECT1 and not first:
                            project(n - 1, 1 - par, 1)
                        if u == TURN1:
                            turn_tops(n, 1)
                        if u == PROJECT0:
                            project(n, par, 0)
                        if u == TURN0 and not last:
                            turn_tops(n + 1, 0)
                        scores(n, par, u, 3)
                        if units:
                            pe.wait_ge(top_done, before + (u in EXTRAS))
                            maxima((par + g) % 2, m + 1, slots(u)[2])

                pe.wait_ge(keys_pick, 2)
                pe.wait_ge(qk_in[0], 16 * QK_DMAS)
                for m in range(AHEAD):
                    if m >= 3:
                        pe.wait_ge(top_done, m - 2)
                    if m == 2:
                        pe.wait_ge(part_ready[0], B)
                    maxima(0, m, FIRST_MX[m % 3])
                pe.wait_ge(top_done, AHEAD)
                turn_tops(0, 0)
                group(0, 0, first=True)
                group(1, 1)
                with pe.Fori(1, N2 // 2 - 1) as k:
                    for par in range(2):
                        group(2 * k + par, par)
                group(N2 - 2, 0)
                group(N2 - 1, 1, last=True)
                values(N2 - 1, 1, STEPS3 - 1)
                project(N2 - 1, 1, 1)

            @block.sync
            def _(sp):
                sp.dma_start(experts_in, w1.rearrange("e d f -> d e f")).then_inc(experts_got, 16)

                def thrice(v):
                    return v.unsqueeze(1).to_broadcast([LAT, PARTS, S])

                def store(b):
                    m = b % 2
                    for c in range(PARTS):
                        sp.wait_ge(part_ready[c], b + 1)
                        sp.dma_start(q_dram[b, c, :, :], qk_part[m][c][0:LAT, :]).then_inc(parts_out[m], 16)
                        sp.dma_start(k_dram[b, c, :, :, :].rearrange("c r t -> r c t"), thrice(qk_part[m][c][LAT:, :])
                                     ).then_inc(parts_out[m], 16)
                        sp.wait_ge(kpm_part_ready[c], b + 1)
                        sp.dma_start(kpm_dram[b, c, :, :, :].rearrange("c r t -> r c t"), thrice(kpm_part[m][c][LAT:, :])
                                     ).then_inc(parts_out[m], 16)

                def load_qk(n, par):
                    b, heads = bass.ds(n // GROUPS, 1), bass.ds((n % GROUPS) * GH, GH)
                    q = q_dram[b, :, :, :].rearrange("o c (d h) t -> (o c d) h t", h=H2)[:, heads, :]
                    for a in range(PARTS):
                        sp.dma_start(q_rows[par][a * PARTS * KD:(a + 1) * PARTS * KD, :, :], q).then_inc(qk_in[par], 16)
                    for dst, src in ((kpm_rows, kpm_dram), (k_rows, k_dram)):
                        k = src[b, :, :, :, :].rearrange("o a c (d h) t -> (o a c d) h t", h=H2)[:, heads, :]
                        sp.dma_start(dst[par][0:PROD, :, :], k).then_inc(qk_in[par], 16)

                def load_ow(n, par):
                    at = (n % GROUPS) * GH * KD
                    for j in range(GH):
                        row = at + j * KD
                        src = o_w[row:row + KD, :] if isinstance(n, int) else o_w[bass.ds(row, KD), :]
                        sp.dma_start(ow_rows[par][32 * j:32 * j + KD, :], src).then_inc(ow_in[par], 16)

                store(0)
                store(1)
                sp.wait_ge(parts_out[0], 16 * BATCH_DMAS)
                sp.wait_ge(act_cleared, 3)
                load_qk(0, 0)
                sp.wait_ge(dve_cleared, 2)
                load_ow(0, 0)
                for b in range(2, B):
                    store(b)
                for m in range(2):
                    sp.wait_ge(parts_out[m], 16 * BATCH_DMAS * B // 2)
                sp.wait_ge(dve_cleared, 6)

                def group(n, par, first=False, last=False):
                    if not last:
                        if not first:
                            sp.wait_ge(t_done, 64 * n)
                        load_qk(n + 1, 1 - par)
                        if not first:
                            sp.wait_ge(proj3_done, 2 * n)
                        load_ow(n + 1, 1 - par)

                group(0, 0, first=True)
                sp.wait_ge(w_split, 3)
                sp.dma_start(experts_in.rearrange("p e (c d) -> p (e c) d", c=FC),
                             w2.rearrange("e (c p) d -> p (e c) d", p=P)).then_inc(experts_got, 16)
                group(1, 1)
                with sp.Fori(1, N2 // 2 - 1) as k:
                    for par in range(2):
                        group(2 * k + par, par)
                group(N2 - 2, 0)
                group(N2 - 1, 1, last=True)

        a4 = Arena()
        TC = P // E
        mT = a4.take(B * S, F16).rearrange("p (h t) -> p h t", h=2)
        mT_b = [a4.take(S) for _ in range(B)]
        cw = a4.take(E * NT).rearrange("p (e t) -> p e t", e=E)
        c_tok = a4.take(NT * E).rearrange("p (t e) -> p t e", t=NT)
        logits = a4.take(NT * E).rearrange("p (t e) -> p t e", t=NT)
        sorted8 = a4.take(NT * E).rearrange("p (t e) -> p t e", t=NT)
        index8 = a4.take(NT * E, U32).rearrange("p (t e) -> p t e", t=NT)
        index_f = a4.take(NT * 2).rearrange("p (t k) -> p t k", t=NT)
        picked = a4.take(NT * E).rearrange("p (t e) -> p t e", t=NT)
        row_top, row_sum, row_rcp = (a4.take(NT) for _ in range(3))
        shift = a4.take(NT)
        w1_e = [a4.take(F, F16).rearrange("p (h f) -> p h f", h=2) for _ in range(2)]
        w2_e = [a4.take(FC * D, F16).rearrange("p (h c d) -> p h c d", h=2, c=FC) for _ in range(2)]
        act_f32 = [[a4.take(S) for _ in range(FC)] for _ in range(2)]
        act_hi = [[a4.take(S // 2, F16) for _ in range(FC)] for _ in range(2)]
        act_lo = [[a4.take(S // 2, F16) for _ in range(FC)] for _ in range(2)]
        cT = a4.take(2 * P)
        b2_diag = a4.take(TC * D).rearrange("p (t d) -> p t d", t=TC)
        HP = [bank(0, 2), bank(2, 2)]
        YP = [bank(4, 2), bank(6, 2)]
        LOGITS = [bank(n)[:, 0:T * E] for n in (4, 6, 5, 7)]
        TURNED = [*YP, *HP]

        mT_ps, mT_ready, mhi_ready, mlo_ready = sem("mT_ps"), sem("mT_ready"), sem("mhi_ready"), sem("mlo_ready")
        lg_ps, lg_ready, exp4, cen4, d4, cw_ready = (sem("lg_ps"), sem("lg_ready"), sem("exp4"), sem("cen4"), sem("d4"),
                                                     sem("cw_ready"))
        w1_ready = [sem(f"w1_ready{m}") for m in range(2)]
        w2_ready = [sem(f"w2_ready{m}") for m in range(2)]
        h_done, gelu_done, y_done, y_added = sem("h_done"), sem("gelu_done"), sem("y_done"), sem("y_added")
        act_split = sem("act_split")
        diag_clear, cT_ps, cT_ready, b2_done, b2_added = (sem("diag_clear"), sem("cT_ps"), sem("cT_ready"), sem("b2_done"),
                                                          sem("b2_added"))
        stats5, pow5, rstd5, normed5, out_ready = (sem("stats5"), sem("pow5"), sem("rstd5"), sem("normed5"),
                                                   sem("out_ready"))
        dve_normed5, b2_in, stored = sem("dve_normed5"), sem("b2_in"), sem("stored")
        last_out_ready = sem("last_out_ready")
        N4 = E * B
        LOWS_SHARED = 3
        BIASES_AT = 2
        HT = T // 2

        def low(eng, ops, b):
            eng.wait_ge(mhi_ready, b + 1)
            upto(eng, mlo_ready, b)
            ops.tensor_tensor(mT[:, 1, b * S:(b + 1) * S], mT_b[b], mT[:, 0, b * S:(b + 1) * S], ALU.subtract
                              ).then_inc(mlo_ready, 1)

        def low_act(eng, ops, n, slot):
            for c in range(FC):
                if c == 0 and isinstance(n, int) and 0 < n <= LOWS_SHARED:
                    eng.wait_ge(act_split, FC * n)
                eng.wait_ge(gelu_done, FC * n + c + 1)
                ops.tensor_tensor(act_lo[slot][c], act_f32[slot][c], act_hi[slot][c], ALU.subtract).then_inc(act_split, 1)

        def over_e(col):
            return col.unsqueeze(2).to_broadcast([P, NT, E])

        with nc.Block() as block:
            @block.sync
            def _(sp):
                def load(e, par):
                    sp.dma_start(w1_e[par], w1_parts[:, bass.ds(e, 1), :, :].rearrange("p a h f -> p (a h) f")
                                 ).then_inc(w1_ready[par], 16)
                    sp.dma_start(w2_e[par].rearrange("p h c d -> p h (c d)"),
                                 w2_parts[:, bass.ds(e, 1), :, :].rearrange("p a h f -> p (a h) f")
                                 ).then_inc(w2_ready[par], 16)

                for e in range(2):
                    load(e, e)
                sp.wait_ge(diag_clear, 1)
                for t in range(TC):
                    sp.dma_start(b2_diag[t * E:(t + 1) * E, t, :], b2).then_inc(b2_in, 16)
                with sp.Fori(1, E // 2) as k:
                    for par in range(2):
                        sp.wait_ge(y_done, B * (2 * k + par - 1))
                        load(2 * k + par, par)
                for b in range(B):
                    now = slice(b * T, (b + 1) * T)
                    if b < B - 1:
                        sp.wait_ge(out_ready, b + 1)
                    else:
                        sp.wait_ge(last_out_ready, 1)
                    sp.dma_start(out_dram[:, now, :], X[:, now, :]).then_inc(stored, 16)
                sp.wait_ge(stored, 16 * B)

            @block.tensor
            def _(pe):
                def turn_inputs(b):
                    for t in range(T):
                        last = nc.tensor.transpose(TURNED[b][:, t * P:(t + 1) * P], acc[:, b * T + t, :], ident[:, :])
                    last.then_inc(mT_ps, 1)

                def route(b):
                    pe.wait_ge(mT_ready, b + 1)
                    pe.wait_ge(mhi_ready, b % 2 + 1)
                    for t in range(T):
                        last = nc.tensor.matmul(LOGITS[b][:, t * E:(t + 1) * E], mT_b[b][:, t * P:(t + 1) * P],
                                                w_router[:, :], start=True, stop=True, skip_group_check=True)
                    last.then_inc(lg_ps, 1)

                def hidden(e, par, b, first):
                    n = B * e + b
                    if b == 0:
                        pe.wait_ge(w1_ready[par], 16 * (e // 2 + 1))
                    if isinstance(e, int) and e == 0:
                        pe.wait_ge(mlo_ready, b + 1)
                    for c in range(FC):
                        if first:
                            pe.wait_ge(mhi_ready, c + 3)
                        elif c == 0 and isinstance(n, int) and n == B:
                            pe.wait_ge(cT_ready, 1)
                        else:
                            pe.wait_ge(gelu_done, FC * (n - 1) + c + 1)
                        for half in range(2):
                            tok = slice(b * S + half * HALF, b * S + (half + 1) * HALF)
                            passes = ((0, 0), (0, 1), (1, 0))
                            for m, (w, x) in enumerate(passes):
                                last = nc.tensor.matmul(HP[c][:, half * HALF:(half + 1) * HALF],
                                                        w1_e[par][:, w, c * P:(c + 1) * P], mT[:, x, tok],
                                                        start=(m == 0), stop=(m == 2))
                        last.then_inc(h_done, 1)

                def output(n, par, slot):
                    pe.wait_ge(act_split, FC * (n + 1))
                    if isinstance(n, int) and n < 2:
                        pe.wait_ge(lg_ready, n + 3)
                    elif isinstance(n, int) and BIASES_AT < n <= BIASES_AT + B:
                        pe.wait_ge(b2_added, n - BIASES_AT)
                    else:
                        pe.wait_ge(y_added, n - 1)
                    pe.wait_ge(w2_ready[par], 16 * (n // (2 * B) + 1))
                    for t in range(T):
                        tok = slice(t * P, (t + 1) * P)
                        for c in range(FC):
                            passes = ((act_hi, 0), (act_hi, 1), (act_lo, 0))
                            for m, (h, w) in enumerate(passes):
                                last = nc.tensor.matmul(YP[slot][:, tok], h[slot][c][:, tok], w2_e[par][:, w, c, :],
                                                        start=(c == 0 and m == 0), stop=(c == FC - 1 and m == 2))
                    last.then_inc(y_done, 1)

                def turn_weights():
                    pe.wait_ge(cw_ready, 1)
                    pe.wait_ge(gelu_done, FC * B - 1)
                    for k in range(2):
                        last = nc.tensor.transpose(HP[0][:, k * P:(k + 1) * P],
                                                   c_tok[:, k * TC:(k + 1) * TC, :].rearrange("p t e -> p (t e)"), ident[:, :])
                    last.then_inc(cT_ps, 1)

                def bias(b):
                    pe.wait_ge(y_added, BIASES_AT + b)
                    if b == 0:
                        pe.wait_ge(b2_in, 16 * TC)
                        pe.wait_ge(cT_ready, 1)
                    k, at = b * T // TC, b * T % TC
                    for half in range(2):
                        first = at + half * T // 2
                        last = nc.tensor.matmul(YP[(b + 1) % 2][:, half * HALF:(half + 1) * HALF], cT[:, k * P:(k + 1) * P],
                                                b2_diag[:, first:first + T // 2, :].rearrange("p t d -> p (t d)"),
                                                start=True, stop=True)
                    last.then_inc(b2_done, 1)

                def expert(e, par, biases=False):
                    for b in range(B):
                        hidden(e, par, b, False)
                        output(B * e + b - 1, par if b > 0 else 1 - par, (b - 1) % 2)
                        if biases and b < B - 1:
                            bias(b + 1)

                for b in range(B):
                    turn_inputs(b)
                for b in range(B):
                    route(b)
                hidden(0, 0, 0, True)
                hidden(0, 0, 1, False)
                output(0, 0, 0)
                hidden(0, 0, 2, False)
                output(1, 0, 1)
                hidden(0, 0, 3, False)
                turn_weights()
                output(2, 0, 0)
                bias(0)
                expert(1, 1, biases=True)
                with pe.Fori(1, E // 2) as k:
                    for par in range(2):
                        expert(2 * k + par, par)
                output(N4 - 1, 1, 1)

            @block.scalar
            def _(act):
                def inputs(b):
                    act.wait_ge(mT_ps, b + 1)
                    nc.scalar.copy(mT_b[b], TURNED[b]).then_inc(mT_ready, 1)

                def inputs_hi(b):
                    nc.scalar.copy(mT[:, 0, b * S:(b + 1) * S], TURNED[b]).then_inc(mhi_ready, 1)

                def unit(e, b):
                    n = B * e + b
                    for c in range(FC):
                        if c == 0 and (not isinstance(n, int) or n >= 2):
                            act.wait_ge(y_done, n - 1)
                        wait_apart(act, h_done, FC * n + c + 1)
                        at = FC * e + c
                        bias = b1T[:, at:at + 1] if isinstance(e, int) else b1T[:, bass.ds(at, 1)]
                        nc.scalar.activation(act_hi[b % 2][c], HP[c], ACT.Gelu, scale=1.0 / WSCALE, bias=bias)
                        nc.scalar.activation(act_f32[b % 2][c], HP[c], ACT.Gelu, scale=1.0 / WSCALE, bias=bias
                                             ).then_inc(gelu_done, 1)

                def normed(b, tiles):
                    act.wait_ge(rstd5, 2 * b + 2)
                    for t in range(b * T, b * T + tiles):
                        last = nc.scalar.activation(hs[:, t, :], hs[:, t, :], ACT.Identity, scale=rstd[:, t:t + 1],
                                                    bias=shift[:, t:t + 1])
                    last.then_inc(normed5, 1)

                inputs(0)
                inputs_hi(0)
                inputs(1)
                inputs_hi(1)
                inputs(2)
                inputs(3)
                inputs_hi(2)
                inputs_hi(3)
                act.wait_ge(cen4, 1)
                nc.scalar.activation(logits, logits, ACT.Exp).then_inc(exp4, 1)
                for e in range(2):
                    for b in range(B):
                        unit(e, b)
                    if e == 0:
                        act.wait_ge(cT_ps, 1)
                        nc.scalar.copy(cT, HP[0][:, 0:2 * P]).then_inc(cT_ready, 1)
                with act.Fori(2, E) as e:
                    for b in range(B):
                        unit(e, b)
                for b in range(B - 1):
                    normed(b, T)
                normed(B - 1, HT)

            @block.gpsimd
            def _(pool):
                nc.gpsimd.memset(b2_diag, 0.0).then_inc(diag_clear, 1)
                for b in range(2, B):
                    low(pool, nc.gpsimd, b)
                for n in range(1, LOWS_SHARED):
                    low_act(pool, nc.gpsimd, n, n % 2)

                def residual(b):
                    pool.wait_ge(normed5, b + 1)
                    nc.gpsimd.tensor_tensor(batch(X, b), batch(X, b), batch(hs, b), ALU.add).then_inc(out_ready, 1)

                for b in range(B):
                    now = slice(b * T, (b + 1) * T)
                    pool.wait_ge(stats5, b + 1)
                    nc.gpsimd.tensor_scalar(shift[:, now], mv[:, now, 0], -1.0, None, ALU.mult).then_inc(pow5, 1)
                    nc.gpsimd.tensor_scalar(rstd[:, now], mv[:, now, 1], EPS, None, ALU.add).then_inc(pow5, 1)
                    pool.wait_ge(pow5, 2 * b + 2)
                    nc.gpsimd.tensor_tensor(rstd[:, now], rstd[:, now], mhalf[:, now], ALU.pow).then_inc(rstd5, 1)
                    pool.wait_ge(rstd5, 2 * b + 1)
                    nc.gpsimd.tensor_tensor(shift[:, now], shift[:, now], rstd[:, now], ALU.mult).then_inc(rstd5, 1)
                    if b > 0:
                        residual(b - 1)

            @block.vector
            def _(dve):
                steps = Steps(dve, d4)

                def step(ins):
                    steps.done(ins)
                    steps.now()

                def take_logits(b):
                    dve.wait_ge(lg_ps, b + 1)
                    nc.vector.tensor_tensor(batch(logits, b), LOGITS[b].rearrange("p (t e) -> p t e", t=T),
                                            wide(rb_b[:, :]), ALU.add).then_inc(lg_ready, 1)

                def add(e, b):
                    n = B * e + b
                    dve.wait_ge(y_done, n + 1)
                    if isinstance(e, int) and e == 1:
                        dve.wait_ge(b2_added, b + 1)
                    elif not isinstance(n, int) or n >= B:
                        dve.wait_ge(y_added, n - B + 1)
                    for t in range(b * T, (b + 1) * T):
                        c = cw[:, e, t:t + 1] if isinstance(e, int) else cw[:, bass.ds(e, 1), t]
                        last = nc.vector.scalar_tensor_tensor(hs[:, t, :], YP[b % 2][:, (t % T) * P:(t % T + 1) * P], c,
                                                              hs[:, t, :], ALU.mult, ALU.add)
                    last.then_inc(y_added, 1)

                low(dve, nc.vector, 0)
                take_logits(0)
                low(dve, nc.vector, 1)
                take_logits(1)
                take_logits(2)
                take_logits(3)
                dve.wait_ge(lg_ready, B)
                step(nc.vector.tensor_reduce(row_top, logits, AX.X, ALU.max))
                nc.vector.tensor_tensor(logits, logits, over_e(row_top), ALU.subtract).then_inc(cen4, 1)
                dve.wait_ge(exp4, 1)
                step(nc.vector.tensor_reduce(row_sum, logits, AX.X, ALU.add))
                step(nc.vector.reciprocal(row_rcp, row_sum))
                step(nc.vector.tensor_tensor(logits, logits, over_e(row_rcp), ALU.mult))
                for t in range(NT):
                    steps.done(nc.vector.max(sorted8[:, t, :], logits[:, t, :]))
                steps.now()
                low_act(dve, nc.vector, 0, 0)
                for t in range(NT):
                    steps.done(nc.vector.max_index(index8[:, t, :], sorted8[:, t, :], logits[:, t, :]))
                steps.now()
                step(nc.vector.tensor_copy(index_f, index8[:, :, 0:2]))
                step(nc.vector.scalar_tensor_tensor(row_sum, sorted8[:, :, 0], 1e-8, sorted8[:, :, 1], ALU.add, ALU.add))
                step(nc.vector.reciprocal(row_rcp, row_sum))
                for k, dst in ((0, c_tok), (1, picked)):
                    step(nc.vector.tensor_tensor(dst, wide(iota_e[:, :], NT), over_e(index_f[:, :, k]), ALU.is_equal))
                    step(nc.vector.tensor_tensor(dst, dst, over_e(sorted8[:, :, k]), ALU.mult))
                step(nc.vector.tensor_tensor(c_tok, c_tok, picked, ALU.add))
                step(nc.vector.tensor_scalar(row_rcp, row_rcp, 0.3, None, ALU.mult))
                nc.vector.tensor_tensor(c_tok, c_tok, over_e(row_rcp), ALU.mult).then_inc(cw_ready, 1)
                dve.wait_ge(cw_ready, 1)
                step(nc.vector.tensor_scalar(cw.rearrange("p e t -> p t e"), c_tok, 1.0 / WSCALE, None, ALU.mult))

                def add_bias(b):
                    dve.wait_ge(b2_done, b + 1)
                    dve.wait_ge(y_added, b + 1)
                    v = batch(hs, b)
                    nc.vector.tensor_tensor(v, YP[(b + 1) % 2].rearrange("p (t d) -> p t d", t=T), v, ALU.add
                                            ).then_inc(b2_added, 1)

                def finish(b):
                    dve.wait_ge(rstd5, 2 * b + 1)
                    for t in range(b * T + HT, (b + 1) * T):
                        last = nc.vector.tensor_scalar(hs[:, t, :], hs[:, t, :], mv[:, t, 0:1], rstd[:, t:t + 1],
                                                       ALU.subtract, ALU.mult)
                    last.then_inc(dve_normed5, 1)
                    dve.wait_ge(dve_normed5, 1)
                    dve.wait_ge(normed5, b + 1)
                    nc.vector.tensor_tensor(batch(X, b), batch(X, b), batch(hs, b), ALU.add).then_inc(last_out_ready, 1)

                for e in range(2):
                    for b in range(B):
                        if B * e + b >= LOWS_SHARED - 1:
                            low_act(dve, nc.vector, B * e + b + 1, (b + 1) % 2)
                        add(e, b)
                        if BIASES_AT <= B * e + b < BIASES_AT + B:
                            add_bias(B * e + b - BIASES_AT)
                with dve.Fori(2, E - 1) as e:
                    for b in range(B):
                        low_act(dve, nc.vector, B * e + b + 1, (b + 1) % 2)
                        add(e, b)
                for b in range(B):
                    if b < B - 1:
                        low_act(dve, nc.vector, N4 - B + b + 1, (b + 1) % 2)
                    add(E - 1, b)
                    dve.wait_ge(y_added, N4 - B + b + 1)
                    for t in range(b * T, (b + 1) * T):
                        steps.done(nc.vector.bn_stats(stats[:, t, :], hs[:, t, :]))
                    steps.now()
                    for t in range(b * T, (b + 1) * T):
                        last = nc.vector.bn_aggr(mv[:, t, :], stats[:, t, :])
                    last.then_inc(stats5, 1)
                finish(B - 1)


_INS = ["L0_attn_states", "L0_attn_Wq", "L0_attn_bq", "L0_attn_Wk", "L0_attn_bk", "L0_attn_Wv", "L0_attn_bv",
        "L0_attn_Wo", "L0_attn_bo", "L0_ffn_q_w", "L0_ffn_q_b", "L0_ffn_k_w", "L0_ffn_k_b", "L0_ffn_v_w",
        "L0_ffn_v_b", "L0_ffn_o_w", "L0_ffn_o_b", "L0_ffn_router_w", "L0_ffn_router_b", "L0_ffn_w1", "L0_ffn_b1",
        "L0_ffn_w2", "L0_ffn_b2"]


def kernel(**inputs):
    import numpy as np
    from concourse import bacc
    from concourse.bass_utils import run_bass_kernel_spmd

    nc = bacc.Bacc("TRN2", target_bir_lowering=False, num_devices=1)
    arrays, args = {}, []
    for name in _INS:
        a = np.ascontiguousarray(inputs[name])
        arrays[f"in_{name}"] = a
        args.append(nc.dram_tensor(f"in_{name}", a.shape, mybir.dt.from_np(a.dtype), kind="ExternalInput").ap())
    out = nc.dram_tensor("out_x", (B, S, D), F32, kind="ExternalOutput").ap()
    build(nc, *args, out)
    r = run_bass_kernel_spmd(nc, [arrays], core_ids=[0])
    return r.results[0]["out_x"]
```
